# Optimizing a Trainium2 kernel written in Bass

```python
import numpy as np
import jax
import jax.numpy as jnp

def _softmax(x, axis=-1):
    return jax.nn.softmax(x, axis=axis)

def _gelu(x):
    return jax.nn.gelu(x, approximate=True)

def _silu(x):
    return jax.nn.silu(x)

def _sigmoid(x):
    return jax.nn.sigmoid(x)

def _layernorm(x, axis=-1, eps=1e-05):
    m = jnp.mean(x, axis=axis, keepdims=True)
    v = jnp.var(x, axis=axis, keepdims=True)
    return (x - m) / jnp.sqrt(v + eps)

def _scatter_add(tgt, idx, src, axis=0):
    return tgt.at[idx].add(src)

def _segment_sum(src, seg, n):
    return jax.ops.segment_sum(src, seg, n)
kernel_name = 'mk_seq_preln_d4_jaxref_r8_ded13d'

def setup_inputs(seed: int=0):
    np.random.seed(seed)
    _w = jnp.asarray

    def _L0_attn_setup():
        import jax, jax.numpy as jnp
        import numpy as np
        DIM = 128
        HEADS = 16
        key = jax.random.key(seed)
        ks = jax.random.split(key, 7)
        b, n, d = (4, 256, DIM)
        s = 1.0 / np.sqrt(d)
        return {'x': jax.random.normal(ks[0], (b, n, d), dtype=jnp.float32), 'Wq': jax.random.normal(ks[1], (d, d), dtype=jnp.float32) * s, 'bq': jnp.zeros((d,), dtype=jnp.float32), 'Wkv': jax.random.normal(ks[2], (d, 2 * d), dtype=jnp.float32) * s, 'bkv': jnp.zeros((2 * d,), dtype=jnp.float32), 'Wo': jax.random.normal(ks[3], (d, d), dtype=jnp.float32) * s, 'bo': jnp.zeros((d,), dtype=jnp.float32)}
    _L0_attn_in = _L0_attn_setup()

    def _L0_ffn_setup():
        import jax, jax.numpy as jnp
        import numpy as np
        B, L, D = (1, 256, 128)
        E, H, G, K = (64, 32, 64, 16)

        def _grouped_routing_scores(router_scores):
            T, En = router_scores.shape
            Tq = T // G
            budget = Tq * K
            order = jnp.argsort(-router_scores, axis=0)
            sorted_vals = jnp.take_along_axis(router_scores, order, axis=0)
            group_score = sorted_vals.reshape(Tq, G, En).sum(axis=1)
            _, top_flat = jax.lax.top_k(group_score.reshape(-1), budget)
            gmask = jnp.zeros((Tq * En,), bool).at[top_flat].set(True).reshape(Tq, En)
            mask_sorted = jnp.broadcast_to(gmask[:, None, :], (Tq, G, En)).reshape(T, En)
            mask = jnp.zeros((T, En), bool).at[order, jnp.arange(En)[None, :]].set(mask_sorted)
            fs = jnp.where(mask, router_scores, 0.0)
            return fs / (fs.sum(axis=-1, keepdims=True) + 1e-06)
        key = jax.random.key(seed)
        ks = jax.random.split(key, 6)
        s = lambda k, shape, scale: jax.random.normal(k, shape, jnp.float32) * scale
        return {'x': jax.random.normal(ks[0], (B, L, D), jnp.float32), 'Wr': s(ks[1], (D, E), D ** (-0.5)), 'br': jnp.zeros((E,), jnp.float32), 'Wup': s(ks[2], (E, D, H), D ** (-0.5)), 'bup': jnp.zeros((E, H), jnp.float32), 'Wgate': s(ks[3], (E, D, H), D ** (-0.5)), 'bgate': jnp.zeros((E, H), jnp.float32), 'Wdown': s(ks[4], (E, H, D), H ** (-0.5)), 'bdown': jnp.zeros((E, D), jnp.float32)}
    _L0_ffn_in = _L0_ffn_setup()

    def _L1_attn_setup():
        import jax, jax.numpy as jnp
        import numpy as np
        D = 128
        H = 16
        DH = D // H
        key = jax.random.key(seed)
        ks = jax.random.split(key, 7)
        s = 0.02
        return {'z': jax.random.normal(ks[0], (8, 128, D), dtype=jnp.float32), 'ln_w': jnp.ones((D,), dtype=jnp.float32), 'ln_b': jnp.zeros((D,), dtype=jnp.float32), 'W_qkv': jax.random.normal(ks[1], (D, 3 * D), dtype=jnp.float32) * s, 'b_qkv': jnp.zeros((3 * D,), dtype=jnp.float32), 'W_proj': jax.random.normal(ks[2], (D, D), dtype=jnp.float32) * s, 'b_proj': jnp.zeros((D,), dtype=jnp.float32)}
    _L1_attn_in = _L1_attn_setup()

    def _L1_ffn_setup():
        import jax, jax.numpy as jnp
        import numpy as np
        D = 128
        LW = 16
        DEPTH = 8
        NN = 2 ** DEPTH - 1
        NL = 2 ** DEPTH
        B, S = (2, 128)

        def _fff(x, nw, nb, w1, b1, w2, b2, act):
            node = jnp.zeros(x.shape[:2], dtype=jnp.int32)
            for _ in range(DEPTH):
                logit = jnp.einsum('bsd,bsd->bs', x, nw[node]) + nb[node]
                node = 2 * node + 1 + (logit > 0).astype(jnp.int32)
            leaf = node - NN
            h = act(jnp.einsum('bsd,bsdl->bsl', x, w1[leaf]) + b1[leaf])
            return jnp.einsum('bsl,bsld->bsd', h, w2[leaf]) + b2[leaf]

        def _forward(x, q_nw, q_nb, q_w1, q_b1, q_w2, q_b2, k_nw, k_nb, k_w1, k_b1, k_w2, k_b2, v_nw, v_nb, v_w1, v_b1, v_w2, v_b2, f_nw, f_nb, f_w1, f_b1, f_w2, f_b2):
            mu = jnp.mean(x, -1, keepdims=True)
            sd = jnp.std(x, -1, ddof=1, keepdims=True)
            xn = (x - mu) / jnp.sqrt(sd + 1e-05)
            relu = jax.nn.relu
            q = _fff(xn, q_nw, q_nb, q_w1, q_b1, q_w2, q_b2, relu)
            k = _fff(xn, k_nw, k_nb, k_w1, k_b1, k_w2, k_b2, relu)
            v = _fff(xn, v_nw, v_nb, v_w1, v_b1, v_w2, v_b2, relu)
            att = jax.nn.softmax(jnp.einsum('bqd,bkd->bqk', q, k) / jnp.sqrt(jnp.float32(D)), axis=-1)
            y = xn + jnp.einsum('bqk,bkd->bqd', att, v)
            gelu = lambda t: jax.nn.gelu(t, approximate=False)
            return y + _fff(y, f_nw, f_nb, f_w1, f_b1, f_w2, f_b2, gelu)

        def _make_fff_params(key, scale_in, scale_leaf):
            ks = jax.random.split(key, 4)
            nw = jax.random.normal(ks[0], (NN, D), jnp.float32) * scale_in
            nb = jnp.zeros((NN,), jnp.float32)
            w1 = jax.random.normal(ks[1], (NL, D, LW), jnp.float32) * scale_in
            b1 = jax.random.normal(ks[2], (NL, LW), jnp.float32) * 0.01
            w2 = jax.random.normal(ks[3], (NL, LW, D), jnp.float32) * scale_leaf
            b2 = jnp.zeros((NL, D), jnp.float32)
            return (nw, nb, w1, b1, w2, b2)
        key = jax.random.key(seed)
        kx, kq, kk, kv, kf = jax.random.split(key, 5)
        s_in = 1.0 / np.sqrt(D)
        s_lf = 1.0 / np.sqrt(LW)
        inp = {'x': jax.random.normal(kx, (B, S, D), jnp.float32)}
        for name, kk_ in (('q', kq), ('k', kk), ('v', kv), ('f', kf)):
            nw, nb, w1, b1, w2, b2 = _make_fff_params(kk_, s_in, s_lf)
            inp.update({f'{name}_nw': nw, f'{name}_nb': nb, f'{name}_w1': w1, f'{name}_b1': b1, f'{name}_w2': w2, f'{name}_b2': b2})
        return inp
    _L1_ffn_in = _L1_ffn_setup()

    def _L2_attn_setup():
        import jax, jax.numpy as jnp
        import numpy as np
        from functools import partial
        B, S, D = (8, 256, 128)
        HEADS, DIM_HEAD = (16, 64)
        MAX_ALLOWABLE = 128 * 128 * 8

        def _max_pow2_divides(n):
            i = 1
            while n % 2 == 0:
                i *= 2
                n //= 2
            return i

        def _n_splits(bh, sq, sk):
            dimprod = bh * sq * sk
            true_divisor = dimprod / MAX_ALLOWABLE
            if true_divisor < 1:
                return 1
            if true_divisor >= bh:
                return bh
            nearest_pow2 = 2 ** np.round(np.log2(true_divisor))
            return int(min(_max_pow2_divides(bh), nearest_pow2))

        def _sdp_attention(q, k, v, scale):
            scores = jnp.einsum('bid,bjd->bij', q, k) * scale
            probs = jax.nn.softmax(scores, axis=2)
            return jnp.einsum('bij,bjd->bid', probs, v)

        def _scan_attention(q, k, v, scale, n_splits):
            bh = q.shape[0]
            nq, nk, nv = [h.reshape(n_splits, bh // n_splits, h.shape[-2], h.shape[-1]) for h in (q, k, v)]

            def body(carry, args):
                cq, ck, cv = args
                return (None, _sdp_attention(cq, ck, cv, scale))
            outs = jax.lax.scan(body, None, (nq, nk, nv))[1]
            return outs.reshape(-1, outs.shape[-2], outs.shape[-1])

        def _heads_to_batch(t, heads):
            b, s, d = t.shape
            return t.reshape(b, s, heads, d // heads).transpose(0, 2, 1, 3).reshape(b * heads, s, d // heads)

        def _batch_to_heads(t, heads):
            bh, s, d = t.shape
            return t.reshape(bh // heads, heads, s, d).transpose(0, 2, 1, 3).reshape(bh // heads, s, d * heads)
        key = jax.random.key(seed)
        k1, k2, k3, k4 = jax.random.split(key, 4)
        inner = HEADS * DIM_HEAD
        return {'hidden_states': jax.random.normal(k1, (B, S, D), jnp.float32), 'Wq': jax.random.normal(k2, (D, inner), jnp.float32) * D ** (-0.5), 'Wkv': jax.random.normal(k3, (D, 2 * inner), jnp.float32) * D ** (-0.5), 'Wo': jax.random.normal(k4, (inner, D), jnp.float32) * inner ** (-0.5), 'bo': jnp.zeros((D,), jnp.float32)}
    _L2_attn_in = _L2_attn_setup()

    def _L2_ffn_setup():
        import jax, jax.numpy as jnp
        import numpy as np
        EMB_DIM = 128
        HIDDEN = int(2 / 3 * 4 * EMB_DIM)
        NUM_EXPERTS = 8
        TOP_K = 2
        B, S = (4, 128)
        key = jax.random.key(seed)
        ks = jax.random.split(key, 5)
        sc = 1.0 / np.sqrt(EMB_DIM)
        sh = 1.0 / np.sqrt(HIDDEN)
        return {'x': jax.random.normal(ks[0], (B, S, EMB_DIM), dtype=jnp.float32), 'Wg': jax.random.normal(ks[1], (NUM_EXPERTS, EMB_DIM), dtype=jnp.float32) * sc, 'W1': jax.random.normal(ks[2], (NUM_EXPERTS, HIDDEN, EMB_DIM), dtype=jnp.float32) * sc, 'W2': jax.random.normal(ks[3], (NUM_EXPERTS, HIDDEN, EMB_DIM), dtype=jnp.float32) * sc, 'W3': jax.random.normal(ks[4], (NUM_EXPERTS, EMB_DIM, HIDDEN), dtype=jnp.float32) * sh}
    _L2_ffn_in = _L2_ffn_setup()

    def _L3_attn_setup():
        import jax, jax.numpy as jnp
        import numpy as np
        KEY_DIM = 64
        key = jax.random.key(seed)
        ks = jax.random.split(key, 5)
        B, N, D, H, K, V = (2, 256, 128, 16, 64, 64)
        scale = 0.02
        return {'x': jax.random.normal(ks[0], (B, N, D), dtype=jnp.float32), 'query_proj': jax.random.normal(ks[1], (H, K, D), dtype=jnp.float32) * scale, 'key_proj': jax.random.normal(ks[2], (D, K), dtype=jnp.float32) * scale, 'value_proj': jax.random.normal(ks[3], (D, V), dtype=jnp.float32) * scale, 'output_proj': jax.random.normal(ks[4], (D, H, V), dtype=jnp.float32) * scale}
    _L3_attn_in = _L3_attn_setup()

    def _L3_ffn_setup():
        import jax, jax.numpy as jnp
        import numpy as np
        MAX_VAL = 100.0
        key = jax.random.key(seed)
        k1, k2, k3 = jax.random.split(key, 3)
        B, S, D_IN, D_OUT = (4, 1024, 128, 128)
        x = jax.random.normal(k1, (B, S, D_IN), dtype=jnp.float32)
        weights = jax.random.normal(k2, (D_OUT, D_IN), dtype=jnp.float32)
        scale = jnp.ones((D_OUT,), dtype=jnp.float32)
        bias = jax.random.normal(k3, (D_OUT,), dtype=jnp.float32)
        return {'x': x, 'weights': weights, 'scale': scale, 'bias': bias}
    _L3_ffn_in = _L3_ffn_setup()
    _d = {'L0_attn_x': _L0_attn_in['x'], 'L0_attn_Wq': _L0_attn_in['Wq'], 'L0_attn_bq': _L0_attn_in['bq'], 'L0_attn_Wkv': _L0_attn_in['Wkv'], 'L0_attn_bkv': _L0_attn_in['bkv'], 'L0_attn_Wo': _L0_attn_in['Wo'], 'L0_attn_bo': _L0_attn_in['bo'], 'L0_ffn_Wr': _L0_ffn_in['Wr'], 'L0_ffn_br': _L0_ffn_in['br'], 'L0_ffn_Wup': _L0_ffn_in['Wup'], 'L0_ffn_bup': _L0_ffn_in['bup'], 'L0_ffn_Wgate': _L0_ffn_in['Wgate'], 'L0_ffn_bgate': _L0_ffn_in['bgate'], 'L0_ffn_Wdown': _L0_ffn_in['Wdown'], 'L0_ffn_bdown': _L0_ffn_in['bdown'], 'L1_attn_ln_w': _L1_attn_in['ln_w'], 'L1_attn_ln_b': _L1_attn_in['ln_b'], 'L1_attn_W_qkv': _L1_attn_in['W_qkv'], 'L1_attn_b_qkv': _L1_attn_in['b_qkv'], 'L1_attn_W_proj': _L1_attn_in['W_proj'], 'L1_attn_b_proj': _L1_attn_in['b_proj'], 'L1_ffn_q_nw': _L1_ffn_in['q_nw'], 'L1_ffn_q_nb': _L1_ffn_in['q_nb'], 'L1_ffn_q_w1': _L1_ffn_in['q_w1'], 'L1_ffn_q_b1': _L1_ffn_in['q_b1'], 'L1_ffn_q_w2': _L1_ffn_in['q_w2'], 'L1_ffn_q_b2': _L1_ffn_in['q_b2'], 'L1_ffn_k_nw': _L1_ffn_in['k_nw'], 'L1_ffn_k_nb': _L1_ffn_in['k_nb'], 'L1_ffn_k_w1': _L1_ffn_in['k_w1'], 'L1_ffn_k_b1': _L1_ffn_in['k_b1'], 'L1_ffn_k_w2': _L1_ffn_in['k_w2'], 'L1_ffn_k_b2': _L1_ffn_in['k_b2'], 'L1_ffn_v_nw': _L1_ffn_in['v_nw'], 'L1_ffn_v_nb': _L1_ffn_in['v_nb'], 'L1_ffn_v_w1': _L1_ffn_in['v_w1'], 'L1_ffn_v_b1': _L1_ffn_in['v_b1'], 'L1_ffn_v_w2': _L1_ffn_in['v_w2'], 'L1_ffn_v_b2': _L1_ffn_in['v_b2'], 'L1_ffn_f_nw': _L1_ffn_in['f_nw'], 'L1_ffn_f_nb': _L1_ffn_in['f_nb'], 'L1_ffn_f_w1': _L1_ffn_in['f_w1'], 'L1_ffn_f_b1': _L1_ffn_in['f_b1'], 'L1_ffn_f_w2': _L1_ffn_in['f_w2'], 'L1_ffn_f_b2': _L1_ffn_in['f_b2'], 'L2_attn_Wq': _L2_attn_in['Wq'], 'L2_attn_Wkv': _L2_attn_in['Wkv'], 'L2_attn_Wo': _L2_attn_in['Wo'], 'L2_attn_bo': _L2_attn_in['bo'], 'L2_ffn_Wg': _L2_ffn_in['Wg'], 'L2_ffn_W1': _L2_ffn_in['W1'], 'L2_ffn_W2': _L2_ffn_in['W2'], 'L2_ffn_W3': _L2_ffn_in['W3'], 'L3_attn_query_proj': _L3_attn_in['query_proj'], 'L3_attn_key_proj': _L3_attn_in['key_proj'], 'L3_attn_value_proj': _L3_attn_in['value_proj'], 'L3_attn_output_proj': _L3_attn_in['output_proj'], 'L3_ffn_weights': _L3_ffn_in['weights'], 'L3_ffn_scale': _L3_ffn_in['scale'], 'L3_ffn_bias': _L3_ffn_in['bias']}
    _x0 = _d['L0_attn_x']
    _d['L0_attn_x'] = jax.random.normal(jax.random.fold_in(jax.random.key(seed), 1), (2, 1024, 128), dtype=_x0.dtype)
    del _x0
    return _d

def reference(L0_attn_x, L0_attn_Wq, L0_attn_bq, L0_attn_Wkv, L0_attn_bkv, L0_attn_Wo, L0_attn_bo, L0_ffn_Wr, L0_ffn_br, L0_ffn_Wup, L0_ffn_bup, L0_ffn_Wgate, L0_ffn_bgate, L0_ffn_Wdown, L0_ffn_bdown, L1_attn_ln_w, L1_attn_ln_b, L1_attn_W_qkv, L1_attn_b_qkv, L1_attn_W_proj, L1_attn_b_proj, L1_ffn_q_nw, L1_ffn_q_nb, L1_ffn_q_w1, L1_ffn_q_b1, L1_ffn_q_w2, L1_ffn_q_b2, L1_ffn_k_nw, L1_ffn_k_nb, L1_ffn_k_w1, L1_ffn_k_b1, L1_ffn_k_w2, L1_ffn_k_b2, L1_ffn_v_nw, L1_ffn_v_nb, L1_ffn_v_w1, L1_ffn_v_b1, L1_ffn_v_w2, L1_ffn_v_b2, L1_ffn_f_nw, L1_ffn_f_nb, L1_ffn_f_w1, L1_ffn_f_b1, L1_ffn_f_w2, L1_ffn_f_b2, L2_attn_Wq, L2_attn_Wkv, L2_attn_Wo, L2_attn_bo, L2_ffn_Wg, L2_ffn_W1, L2_ffn_W2, L2_ffn_W3, L3_attn_query_proj, L3_attn_key_proj, L3_attn_value_proj, L3_attn_output_proj, L3_ffn_weights, L3_ffn_scale, L3_ffn_bias):

    def _L0_attn_ref(x, Wq, bq, Wkv, bkv, Wo, bo):
        import jax, jax.numpy as jnp
        import numpy as np
        DIM = 128
        HEADS = 16
        b, n, d = x.shape
        h = HEADS
        dh = d // h
        scale = dh ** (-0.5)
        q = x @ Wq + bq
        kv = x @ Wkv + bkv
        k, v = jnp.split(kv, 2, axis=-1)

        def split_heads(t):
            return t.reshape(b, n, h, dh).transpose(0, 2, 1, 3)
        q, k, v = (split_heads(q), split_heads(k), split_heads(v))
        dots = jnp.einsum('bhid,bhjd->bhij', q, k) * scale
        mask_value = jnp.finfo(dots.dtype).min
        causal_mask = jnp.triu(jnp.ones((n, n), dtype=bool), k=1)
        dots = jnp.where(causal_mask, mask_value, dots)
        attn = jax.nn.softmax(dots, axis=-1)
        out = jnp.einsum('bhij,bhjd->bhid', attn, v)
        out = out.transpose(0, 2, 1, 3).reshape(b, n, d)
        return out @ Wo + bo

    def _L0_ffn_ref(x, Wr, br, Wup, bup, Wgate, bgate, Wdown, bdown):
        import jax, jax.numpy as jnp
        import numpy as np
        B, L, D = (1, 256, 128)
        E, H, G, K = (64, 32, 64, 16)

        def _grouped_routing_scores(router_scores):
            T, En = router_scores.shape
            Tq = T // G
            budget = Tq * K
            order = jnp.argsort(-router_scores, axis=0)
            sorted_vals = jnp.take_along_axis(router_scores, order, axis=0)
            group_score = sorted_vals.reshape(Tq, G, En).sum(axis=1)
            _, top_flat = jax.lax.top_k(group_score.reshape(-1), budget)
            gmask = jnp.zeros((Tq * En,), bool).at[top_flat].set(True).reshape(Tq, En)
            mask_sorted = jnp.broadcast_to(gmask[:, None, :], (Tq, G, En)).reshape(T, En)
            mask = jnp.zeros((T, En), bool).at[order, jnp.arange(En)[None, :]].set(mask_sorted)
            fs = jnp.where(mask, router_scores, 0.0)
            return fs / (fs.sum(axis=-1, keepdims=True) + 1e-06)
        Bx, Lx, Dx = x.shape
        xt = x.reshape(-1, Dx)
        router_scores = jax.nn.softmax(xt @ Wr + br, axis=-1)
        fs = _grouped_routing_scores(router_scores)
        up = jnp.einsum('td,edh->teh', xt, Wup) + bup
        gate = jnp.einsum('td,edh->teh', xt, Wgate) + bgate
        h = jax.nn.silu(up) * gate * fs[:, :, None]
        out = jnp.einsum('teh,ehd->td', h, Wdown) + fs @ bdown
        return out.reshape(Bx, Lx, Dx)

    def _L1_attn_ref(z, ln_w, ln_b, W_qkv, b_qkv, W_proj, b_proj):
        import jax, jax.numpy as jnp
        import numpy as np
        D = 128
        H = 16
        DH = D // H
        b, n, d = z.shape
        mu = jnp.mean(z, axis=-1, keepdims=True)
        var = jnp.var(z, axis=-1, keepdims=True)
        zn = (z - mu) / jnp.sqrt(var + 1e-05) * ln_w + ln_b
        qkv = (zn @ W_qkv + b_qkv).reshape(b, n, 3, H, DH)
        q = qkv[:, :, 0].transpose(0, 2, 1, 3)
        k = qkv[:, :, 1].transpose(0, 2, 1, 3)
        v = qkv[:, :, 2].transpose(0, 2, 1, 3)
        scale = 1.0 / jnp.sqrt(jnp.asarray(DH, dtype=z.dtype))
        scores = jnp.einsum('bhqd,bhkd->bhqk', q, k) * scale
        attn = jax.nn.softmax(scores, axis=-1)
        msa = jnp.einsum('bhqk,bhkd->bhqd', attn, v)
        msa_cat = msa.transpose(0, 2, 1, 3).reshape(b, n, d)
        out = msa_cat @ W_proj + b_proj
        return z + out

    def _L1_ffn_ref(x, q_nw, q_nb, q_w1, q_b1, q_w2, q_b2, k_nw, k_nb, k_w1, k_b1, k_w2, k_b2, v_nw, v_nb, v_w1, v_b1, v_w2, v_b2, f_nw, f_nb, f_w1, f_b1, f_w2, f_b2):
        import jax, jax.numpy as jnp
        import numpy as np
        D = 128
        LW = 16
        DEPTH = 8
        NN = 2 ** DEPTH - 1
        NL = 2 ** DEPTH
        B, S = (2, 128)

        def _fff(x, nw, nb, w1, b1, w2, b2, act):
            node = jnp.zeros(x.shape[:2], dtype=jnp.int32)
            for _ in range(DEPTH):
                logit = jnp.einsum('bsd,bsd->bs', x, nw[node]) + nb[node]
                node = 2 * node + 1 + (logit > 0).astype(jnp.int32)
            leaf = node - NN
            h = act(jnp.einsum('bsd,bsdl->bsl', x, w1[leaf]) + b1[leaf])
            return jnp.einsum('bsl,bsld->bsd', h, w2[leaf]) + b2[leaf]

        def _forward(x, q_nw, q_nb, q_w1, q_b1, q_w2, q_b2, k_nw, k_nb, k_w1, k_b1, k_w2, k_b2, v_nw, v_nb, v_w1, v_b1, v_w2, v_b2, f_nw, f_nb, f_w1, f_b1, f_w2, f_b2):
            mu = jnp.mean(x, -1, keepdims=True)
            sd = jnp.std(x, -1, ddof=1, keepdims=True)
            xn = (x - mu) / jnp.sqrt(sd + 1e-05)
            relu = jax.nn.relu
            q = _fff(xn, q_nw, q_nb, q_w1, q_b1, q_w2, q_b2, relu)
            k = _fff(xn, k_nw, k_nb, k_w1, k_b1, k_w2, k_b2, relu)
            v = _fff(xn, v_nw, v_nb, v_w1, v_b1, v_w2, v_b2, relu)
            att = jax.nn.softmax(jnp.einsum('bqd,bkd->bqk', q, k) / jnp.sqrt(jnp.float32(D)), axis=-1)
            y = xn + jnp.einsum('bqk,bkd->bqd', att, v)
            gelu = lambda t: jax.nn.gelu(t, approximate=False)
            return y + _fff(y, f_nw, f_nb, f_w1, f_b1, f_w2, f_b2, gelu)

        def _make_fff_params(key, scale_in, scale_leaf):
            ks = jax.random.split(key, 4)
            nw = jax.random.normal(ks[0], (NN, D), jnp.float32) * scale_in
            nb = jnp.zeros((NN,), jnp.float32)
            w1 = jax.random.normal(ks[1], (NL, D, LW), jnp.float32) * scale_in
            b1 = jax.random.normal(ks[2], (NL, LW), jnp.float32) * 0.01
            w2 = jax.random.normal(ks[3], (NL, LW, D), jnp.float32) * scale_leaf
            b2 = jnp.zeros((NL, D), jnp.float32)
            return (nw, nb, w1, b1, w2, b2)
        return _forward(x, q_nw, q_nb, q_w1, q_b1, q_w2, q_b2, k_nw, k_nb, k_w1, k_b1, k_w2, k_b2, v_nw, v_nb, v_w1, v_b1, v_w2, v_b2, f_nw, f_nb, f_w1, f_b1, f_w2, f_b2)

    def _L2_attn_ref(hidden_states, Wq, Wkv, Wo, bo):
        import jax, jax.numpy as jnp
        import numpy as np
        from functools import partial
        B, S, D = (8, 256, 128)
        HEADS, DIM_HEAD = (16, 64)
        MAX_ALLOWABLE = 128 * 128 * 8

        def _max_pow2_divides(n):
            i = 1
            while n % 2 == 0:
                i *= 2
                n //= 2
            return i

        def _n_splits(bh, sq, sk):
            dimprod = bh * sq * sk
            true_divisor = dimprod / MAX_ALLOWABLE
            if true_divisor < 1:
                return 1
            if true_divisor >= bh:
                return bh
            nearest_pow2 = 2 ** np.round(np.log2(true_divisor))
            return int(min(_max_pow2_divides(bh), nearest_pow2))

        def _sdp_attention(q, k, v, scale):
            scores = jnp.einsum('bid,bjd->bij', q, k) * scale
            probs = jax.nn.softmax(scores, axis=2)
            return jnp.einsum('bij,bjd->bid', probs, v)

        def _scan_attention(q, k, v, scale, n_splits):
            bh = q.shape[0]
            nq, nk, nv = [h.reshape(n_splits, bh // n_splits, h.shape[-2], h.shape[-1]) for h in (q, k, v)]

            def body(carry, args):
                cq, ck, cv = args
                return (None, _sdp_attention(cq, ck, cv, scale))
            outs = jax.lax.scan(body, None, (nq, nk, nv))[1]
            return outs.reshape(-1, outs.shape[-2], outs.shape[-1])

        def _heads_to_batch(t, heads):
            b, s, d = t.shape
            return t.reshape(b, s, heads, d // heads).transpose(0, 2, 1, 3).reshape(b * heads, s, d // heads)

        def _batch_to_heads(t, heads):
            bh, s, d = t.shape
            return t.reshape(bh // heads, heads, s, d).transpose(0, 2, 1, 3).reshape(bh // heads, s, d * heads)
        scale = DIM_HEAD ** (-0.5)
        q = hidden_states @ Wq
        kv = hidden_states @ Wkv
        k, v = jnp.split(kv, 2, axis=-1)
        q = _heads_to_batch(q, HEADS)
        k = _heads_to_batch(k, HEADS)
        v = _heads_to_batch(v, HEADS)
        n_splits = _n_splits(q.shape[0], q.shape[1], k.shape[1])
        out = _scan_attention(q, k, v, scale, n_splits)
        out = _batch_to_heads(out, HEADS)
        return out @ Wo + bo

    def _L2_ffn_ref(x, Wg, W1, W2, W3):
        import jax, jax.numpy as jnp
        import numpy as np
        EMB_DIM = 128
        HIDDEN = int(2 / 3 * 4 * EMB_DIM)
        NUM_EXPERTS = 8
        TOP_K = 2
        B, S = (4, 128)
        gate_logits = jnp.einsum('bsd,ed->bse', x, Wg)
        top_v, top_i = jax.lax.top_k(gate_logits, TOP_K)
        mask = jnp.any(top_i[..., :, None] == jnp.arange(NUM_EXPERTS), axis=-2)
        sparse_logits = jnp.where(mask, gate_logits, -jnp.inf)
        gating = jax.nn.softmax(sparse_logits, axis=-1)
        h1 = jnp.einsum('bsd,ehd->bseh', x, W1)
        h2 = jnp.einsum('bsd,ehd->bseh', x, W2)
        hidden = jax.nn.silu(h1) * h2
        expert_out = jnp.einsum('bseh,edh->bsed', hidden, W3)
        return jnp.einsum('bsed,bse->bsd', expert_out, gating)

    def _L3_attn_ref(x, query_proj, key_proj, value_proj, output_proj):
        import jax, jax.numpy as jnp
        import numpy as np
        KEY_DIM = 64
        B, D = (x.shape[0], x.shape[-1])
        r = x.reshape(B, -1, D)
        q = jnp.einsum('bnd,hkd->bnhk', r, query_proj)
        k = jnp.einsum('bmd,dk->bmk', r, key_proj)
        v = jnp.einsum('bmd,dv->bmv', r, value_proj)
        sim = jnp.einsum('bnhk,bmk->bnhm', q, k) / jnp.sqrt(jnp.asarray(KEY_DIM, dtype=r.dtype))
        attn = jax.nn.softmax(sim, axis=-1)
        o = jnp.einsum('bnhm,bmv->bnhv', attn, v)
        out = jnp.einsum('bnhv,dhv->bnd', o, output_proj)
        return out.reshape(x.shape)

    def _L3_ffn_ref(x, weights, scale, bias):
        import jax, jax.numpy as jnp
        import numpy as np
        MAX_VAL = 100.0
        w = (weights >= 0.0).astype(x.dtype) * 2.0 - 1.0
        y = jnp.einsum('bsi,oi->bso', x, w)
        y = y * scale + bias
        y = jnp.clip(y, -MAX_VAL, MAX_VAL)
        return y
    x = L0_attn_x
    x = x + _L0_attn_ref(_layernorm(x, axis=-1), L0_attn_Wq, L0_attn_bq, L0_attn_Wkv, L0_attn_bkv, L0_attn_Wo, L0_attn_bo)
    x = x + _L0_ffn_ref(_layernorm(x, axis=-1), L0_ffn_Wr, L0_ffn_br, L0_ffn_Wup, L0_ffn_bup, L0_ffn_Wgate, L0_ffn_bgate, L0_ffn_Wdown, L0_ffn_bdown)
    x = x + _L1_attn_ref(_layernorm(x, axis=-1), L1_attn_ln_w, L1_attn_ln_b, L1_attn_W_qkv, L1_attn_b_qkv, L1_attn_W_proj, L1_attn_b_proj)
    x = x + _L1_ffn_ref(_layernorm(x, axis=-1), L1_ffn_q_nw, L1_ffn_q_nb, L1_ffn_q_w1, L1_ffn_q_b1, L1_ffn_q_w2, L1_ffn_q_b2, L1_ffn_k_nw, L1_ffn_k_nb, L1_ffn_k_w1, L1_ffn_k_b1, L1_ffn_k_w2, L1_ffn_k_b2, L1_ffn_v_nw, L1_ffn_v_nb, L1_ffn_v_w1, L1_ffn_v_b1, L1_ffn_v_w2, L1_ffn_v_b2, L1_ffn_f_nw, L1_ffn_f_nb, L1_ffn_f_w1, L1_ffn_f_b1, L1_ffn_f_w2, L1_ffn_f_b2)
    x = x + _L2_attn_ref(_layernorm(x, axis=-1), L2_attn_Wq, L2_attn_Wkv, L2_attn_Wo, L2_attn_bo)
    x = x + _L2_ffn_ref(_layernorm(x, axis=-1), L2_ffn_Wg, L2_ffn_W1, L2_ffn_W2, L2_ffn_W3)
    x = x + _L3_attn_ref(_layernorm(x, axis=-1), L3_attn_query_proj, L3_attn_key_proj, L3_attn_value_proj, L3_attn_output_proj)
    x = x + _L3_ffn_ref(_layernorm(x, axis=-1), L3_ffn_weights, L3_ffn_scale, L3_ffn_bias)
    return x

_drawn_inputs = setup_inputs


def setup_inputs(seed=0):
    import zlib

    import numpy as np

    out = dict(_drawn_inputs(seed))
    spreads = {'L0_attn_bq': (0.0, 0.1),
     'L0_attn_bkv': (0.0, 0.1),
     'L0_attn_bo': (0.0, 0.1),
     'L0_ffn_br': (0.0, 0.1),
     'L0_ffn_bup': (0.0, 0.1),
     'L0_ffn_bgate': (0.0, 0.1),
     'L0_ffn_bdown': (0.0, 0.1),
     'L1_attn_ln_w': (1.0, 0.6),
     'L1_attn_ln_b': (0.0, 0.28),
     'L1_attn_b_qkv': (0.0, 0.1),
     'L1_attn_b_proj': (0.0, 0.1),
     'L1_ffn_q_nb': (0.0, 0.1),
     'L1_ffn_q_b2': (0.0, 0.442),
     'L1_ffn_k_nb': (0.0, 0.1),
     'L1_ffn_k_b2': (0.0, 0.504),
     'L1_ffn_v_nb': (0.0, 0.1),
     'L1_ffn_v_b2': (0.0, 0.1),
     'L1_ffn_f_nb': (0.0, 0.1),
     'L1_ffn_f_b2': (0.0, 0.1),
     'L2_attn_bo': (0.0, 0.1),
     'L3_ffn_scale': (1.0, 0.2)}
    factors = {'L1_ffn_q_b1': 8.0,
     'L1_ffn_k_b1': 8.0,
     'L1_ffn_v_b1': 6.003,
     'L1_ffn_f_b1': 8.0,
     'L3_attn_query_proj': 8.0,
     'L3_attn_key_proj': 8.0,
     'L3_attn_value_proj': 7.972,
     'L3_attn_output_proj': 7.29}
    for name, (base, spread) in spreads.items():
        noise = np.random.default_rng([zlib.crc32(name.encode()), seed]).standard_normal(out[name].shape)
        drawn = base * np.exp(spread * noise) if base else spread * noise
        out[name] = jnp.asarray(drawn.astype(out[name].dtype))
    for name, factor in factors.items():
        out[name] = (out[name] * factor).astype(out[name].dtype)
    return out
```

```python
from contextlib import ExitStack

import numpy as np
import concourse.bass as bass
from concourse import mybir
from concourse.alu_op_type import AluOpType as ALU

ACT = mybir.ActivationFunctionType
F32 = mybir.dt.float32
BF16 = mybir.dt.bfloat16
AX_X = mybir.AxisListType.X

P = 128
B, S, D = 2, 1024, 128
NT = B * S // P
TB = S // P
W = 512
NG = B * S // W
HEADS = 16
NEG = -1e30


class Scope:

    SPENT = []

    def __init__(self, nc, name):
        self.nc, self.name, self.ctx, self.sems = nc, name, ExitStack(), []

    def __enter__(self):
        return self

    def __exit__(self, *e):
        Scope.SPENT += self.sems
        return self.ctx.__exit__(*e)

    def sb(self, name, shape, dt=F32):
        return self.ctx.enter_context(self.nc.sbuf_tensor(f"{self.name}_{name}", shape, dt))

    def ps(self, name, shape, dt=F32):
        return self.ctx.enter_context(self.nc.psum_tensor(f"{self.name}_{name}", shape, dt))

    def sem(self, name):
        self.sems.append(self.nc.alloc_semaphore(f"{self.name}_{name}"))
        return self.sems[-1]


def recycle(nc):
    nc.clear_and_free_semaphores(Scope.SPENT)
    Scope.SPENT = []
    nc.all_engine_barrier()


def layer_norm(nc, name, src, dst, ident, xT=None, affine=None, root_of_deviation=False, eps=1e-5):
    with Scope(nc, name) as m:
        stats = m.sb("stats", [P, NT, 6])
        moments = m.sb("moments", [P, NT, 2])
        power = m.sb("power", [P, 2, NT])
        spread = m.sb("spread", [P, NT])
        turned = m.ps("turned", [P, NG, W])
        moments_ready = m.sem("moments_ready")
        rstd_ready = m.sem("rstd_ready")
        tile_normed = m.sem("tile_normed")
        group_turned = m.sem("group_turned")

        with nc.Block() as block:
            @block.vector
            def _(dve):
                for t in range(NT):
                    nc.vector.bn_stats(stats[:, t, :], src[:, t, :])
                dve.drain()
                for t in range(NT):
                    last = nc.vector.bn_aggr(moments[:, t, :], stats[:, t, :])
                last.then_inc(moments_ready, 1)
                dve.wait_ge(rstd_ready, 1)
                for t in range(NT):
                    nc.vector.tensor_scalar(dst[:, t, :], src[:, t, :], moments[:, t, 0:1], spread[:, t:t + 1],
                                            ALU.subtract, ALU.mult).then_inc(tile_normed, 1)

            @block.gpsimd
            def _(pool):
                nc.gpsimd.memset(power[:, 0, :], -0.5)
                nc.gpsimd.memset(power[:, 1, :], 0.5)
                pool.wait_ge(moments_ready, 1)
                if root_of_deviation:
                    nc.gpsimd.tensor_scalar(spread[:], moments[:, :, 1], D / (D - 1.0), None, ALU.mult)
                    pool.drain()
                    nc.gpsimd.tensor_tensor(spread[:], spread[:], power[:, 1, :], ALU.pow)
                    pool.drain()
                    nc.gpsimd.tensor_scalar(spread[:], spread[:], eps, None, ALU.add)
                else:
                    nc.gpsimd.tensor_scalar(spread[:], moments[:, :, 1], eps, None, ALU.add)
                pool.drain()
                nc.gpsimd.tensor_tensor(spread[:], spread[:], power[:, 0, :], ALU.pow).then_inc(rstd_ready, 1)

            if xT is not None:
                @block.tensor
                def _(pe):
                    for g in range(NG):
                        pe.wait_ge(tile_normed, 4 * g + 4)
                        for c in range(4):
                            last = nc.tensor.transpose(turned[:, g, c * P:(c + 1) * P], dst[:, 4 * g + c, :], ident[:])
                        last.then_inc(group_turned, 1)

                @block.scalar
                def _(act):
                    for g in range(NG):
                        act.wait_ge(group_turned, g + 1)
                        to, frm = xT[:, g * W:(g + 1) * W], turned[:, g, :]
                        if affine is None:
                            nc.scalar.copy(to, frm)
                        else:
                            nc.scalar.activation(to, frm, ACT.Identity, bias=affine[:, 1:2], scale=affine[:, 0:1])


def narrow_attention(nc, name, x, xT, residual, weights, consts, causal):
    DH, HG = 8, 4
    G = HEADS // HG
    ROWS, STACK = 9 * DH, 96
    SCALE = DH ** -0.5
    wq, wk, wv, bq, bk, bv, wo, bo = weights
    q_dram = nc.dram_tensor(f"{name}_q_parts", [3, P, B * S], BF16, kind="Internal").ap()
    k_dram = nc.dram_tensor(f"{name}_k_parts", [3, P, B * S], BF16, kind="Internal").ap()
    with Scope(nc, name) as outer:
        v_tok = outer.sb("v_tok", [P, NT, P])
        wo_sb = outer.sb("wo_sb", [P, G, P])
        spread_den = outer.sb("spread_den", [P, P])

        with Scope(nc, name + "p") as m:
            w_sb = m.sb("w_sb", [P, 3, P])
            b_col = m.sb("b_col", [P, 2])
            b_row = m.sb("b_row", [P, 2, P])
            full = m.sb("full", [P, 2, B * S])
            rest = m.sb("rest", [P, B * S])
            parts = m.sb("parts", [P, 2, 3, B * S], BF16)
            qk_ps = m.ps("qk_ps", [P, 4, W])
            v_ps = m.ps("v_ps", [P, NG, W])
            loaded = m.sem("loaded")
            qk_made = m.sem("qk_made")
            qk_moved = m.sem("qk_moved")
            v_made = m.sem("v_made")
            parts_ready = m.sem("parts_ready")
            stored = m.sem("stored")
            with nc.Block() as block:
                @block.sync
                def _(sp):
                    for n, w in enumerate((wq, wk, wv)):
                        sp.dma_start(w_sb[:, n, :], w).then_inc(loaded, 16)
                    for n, b in enumerate((bq, bk)):
                        sp.dma_start(b_col[:, n:n + 1], b.rearrange("(p a) -> p a", a=1)).then_inc(loaded, 16)
                    for n, b in enumerate((bv, bo)):
                        sp.dma_start(b_row[:, n, :], b.partition_broadcast(P)).then_inc(loaded, 16)
                    sp.dma_start(wo_sb[:], wo.rearrange("g p n -> p g n")).then_inc(loaded, 16)
                    sp.dma_start(spread_den[:], consts["spread_den"]).then_inc(loaded, 16)
                    sp.wait_ge(loaded, 16 * 9)
                    for n, dram in enumerate((q_dram, k_dram)):
                        sp.wait_ge(parts_ready, n + 1)
                        sp.dma_start(dram.rearrange("c p n -> p c n"), parts[:, n, :, :]).then_inc(stored, 16)
                    sp.wait_ge(stored, 32)

                @block.tensor
                def _(pe):
                    pe.wait_ge(loaded, 16 * 9)
                    for n in range(2):
                        for g in range(NG):
                            if n:
                                pe.wait_ge(qk_moved, g + 1)
                            nc.tensor.matmul(qk_ps[:, g, :], w_sb[:, n, :], xT[:, g * W:(g + 1) * W],
                                             start=True, stop=True).then_inc(qk_made, 1)
                    for t in range(NT):
                        nc.tensor.matmul(v_ps[:, t // 4, t % 4 * P:(t % 4 + 1) * P], xT[:, t * P:(t + 1) * P],
                                         w_sb[:, 2, :], start=True, stop=True).then_inc(v_made, 1)

                @block.scalar
                def _(act):
                    act.wait_ge(loaded, 16 * 9)
                    for n in range(2):
                        for g in range(NG):
                            act.wait_ge(qk_made, NG * n + g + 1)
                            nc.scalar.activation(full[:, n, g * W:(g + 1) * W], qk_ps[:, g, :], ACT.Identity,
                                                 bias=b_col[:, n:n + 1]).then_inc(qk_moved, 1)

                @block.vector
                def _(dve):
                    dve.wait_ge(loaded, 16 * 9)
                    wide_bo = b_row[:, 1:2, :].to_broadcast([P, NT, P])
                    nc.vector.tensor_tensor(x[:], x[:], wide_bo, ALU.add)
                    if residual is not None:
                        dve.drain()
                        nc.vector.tensor_tensor(x[:], x[:], residual[:], ALU.add)
                    for n in range(2):
                        dve.wait_ge(qk_moved, NG * (n + 1))
                        high, mid, low = (parts[:, n, c, :] for c in range(3))
                        nc.vector.tensor_copy(high, full[:, n, :])
                        dve.drain()
                        nc.vector.tensor_tensor(rest[:], full[:, n, :], high, ALU.subtract)
                        dve.drain()
                        nc.vector.tensor_copy(mid, rest[:])
                        dve.drain()
                        nc.vector.tensor_tensor(low, rest[:], mid, ALU.subtract).then_inc(parts_ready, 1)
                        dve.drain()
                    for g in range(NG):
                        dve.wait_ge(v_made, 4 * g + 4)
                        nc.vector.tensor_tensor(v_tok[:, 4 * g:4 * g + 4, :],
                                                v_ps[:, g, :].rearrange("p (t n) -> p t n", n=P),
                                                b_row[:, 0:1, :].to_broadcast([P, 4, P]), ALU.add)

        NQ = S // W
        steps = [(Q, k) for Q in range(NQ) for k in range(4 * Q + 4 if causal else TB)]
        NS = len(steps)
        chunks = [(j, qt, c) for j in range(HG) for qt in range(TB) for c in range(2)
                  if not causal or c * W < (qt + 1) * P]
        NCH = len(chunks)
        first_step, n_steps = 2, NS - 5
        share = -(-NCH // n_steps)
        NMISC = 2 * NQ + 1
        with Scope(nc, name + "m") as m:
            qs = [m.sb(f"qs{b}", [STACK, HG, S], BF16) for b in range(B)]
            ks = [m.sb(f"ks{b}", [STACK, HG, S], BF16) for b in range(B)]
            vb = [m.sb(f"vb{b}", [P, TB, HG, 32]) for b in range(B)]
            plain = m.sb("plain", [3, 2, HG * S], BF16)
            mask = m.sb("mask", [P, 3, P], BF16)
            probs = m.sb("probs", [P, 2, HG, W])
            part_max = m.sb("part_max", [P, 2, HG * TB])
            neg_max = m.sb("neg_max", [P, HG * TB])
            shift = m.sb("shift", [HG * TB, 2, P])
            shift_parts = m.sb("shift_parts", [HG * TB, 3, P], BF16)
            sums = m.sb("sums", [P, W])
            recip = m.sb("recip", [P, W])
            normed = m.sb("normed", [P, W])
            s_ps = m.ps("s_ps", [P, HG, W])
            m_ps = m.ps("m_ps", [P, 2, W])
            o_ps = m.ps("o_ps", [P, W])
            misc = m.ps("misc", [P, W])
            constants_set = m.sem("constants_set")
            constants_in = m.sem("constants_in")
            stacks_in = m.sem("stacks_in")
            shift_in = m.sem("shift_in")
            v_in = m.sem("v_in")
            scores_ready = m.sem("scores_ready")
            probs_ready = m.sem("probs_ready")
            probs_free = m.sem("probs_free")
            max_full = m.sem("max_full")
            max_free = m.sem("max_free")
            neg_max_ready = m.sem("neg_max_ready")
            shift_ready = m.sem("shift_ready")
            out_full = m.sem("out_full")
            out_free = m.sem("out_free")
            misc_full = m.sem("misc_full")
            misc_free = m.sem("misc_free")
            normed_ready = m.sem("normed_ready")

            def load_unit(sp, u, b, g):
                for stack, dram, order in ((qs[b], q_dram, 0), (ks[b], k_dram, 1)):
                    for j in range(HG):
                        rows = dram[:, bass.ds(g * (HG * DH) + j * DH, DH), b * S:(b + 1) * S]
                        for a in range(3):
                            if order == 0:
                                src = rows[a:a + 1, :, :].to_broadcast([3, DH, S])
                            else:
                                src = rows
                            sp.dma_start(stack[3 * DH * a:3 * DH * (a + 1), j, :], src).then_inc(stacks_in, 16)
                sp.dma_start(qs[b][ROWS:ROWS + 3, :, :].rearrange("p h n -> p (h n)"),
                             plain[:, 0, :]).then_inc(stacks_in, 16)

            N_LOADS = 2 * HG * 3 + 1

            def load_shift(sp, u, b):
                sp.wait_ge(shift_ready, u + 1)
                for c in range(3):
                    sp.dma_start(qs[b][ROWS + c:ROWS + c + 1, :, :].rearrange("p h n -> p (h n)"),
                                 shift_parts[:, c, :]).then_inc(shift_in, 16)

            def pe_max(pe, u, b, which):
                for i, (j, qt, c) in which:
                    pe.wait_ge(max_free, u * NCH + i + 1)
                    end = min(W, (qt + 1) * P - c * W) if causal else W
                    diagonal = causal and c * W <= qt * P < (c + 1) * W
                    mm = nc.tensor.matmul(m_ps[:, i % 2, 0:end], qs[b][:, j, qt * P:(qt + 1) * P],
                                          ks[b][:, j, c * W:c * W + end], start=True, stop=not diagonal)
                    if diagonal:
                        mm = nc.tensor.matmul(m_ps[:, i % 2, end - P:end], mask[:, 0, :], mask[:, 1, :],
                                              start=False, stop=True)
                    mm.then_inc(max_full, 1)

            def dve_max(dve, u, which):
                for i, (j, qt, c) in which:
                    dve.wait_ge(max_full, u * NCH + i + 1)
                    end = min(W, (qt + 1) * P - c * W) if causal else W
                    col = j * TB + qt
                    nc.vector.tensor_reduce(part_max[:, c, col:col + 1], m_ps[:, i % 2, 0:end], AX_X,
                                            ALU.max).then_inc(max_free, 1)

            def pe_turn_max(pe, u, use):
                pe.wait_ge(neg_max_ready, u + 1)
                pe.wait_ge(misc_free, use + 1)
                nc.tensor.transpose(misc[0:HG * TB, 0:P], neg_max[:], consts["ident_sb"][:]).then_inc(misc_full, 1)

            def dve_neg_max(dve, u):
                dve.drain()
                nc.vector.tensor_tensor(neg_max[:], part_max[:, 0, :], part_max[:, 1, :], ALU.max)
                dve.drain()
                nc.vector.tensor_scalar(neg_max[:], neg_max[:], -1.0, None, ALU.mult).then_inc(neg_max_ready, 1)

            def dve_split_shift(dve, u, use):
                dve.wait_ge(misc_full, use + 1)
                dve.wait_ge(shift_in, 48 * u + 48)
                nc.vector.tensor_copy(shift[:, 0, :], misc[0:HG * TB, 0:P]).then_inc(misc_free, 1)
                dve.drain()
                nc.vector.tensor_copy(shift_parts[:, 0, :], shift[:, 0, :])
                dve.drain()
                nc.vector.tensor_tensor(shift[:, 1, :], shift[:, 0, :], shift_parts[:, 0, :], ALU.subtract)
                dve.drain()
                nc.vector.tensor_copy(shift_parts[:, 1, :], shift[:, 1, :])
                dve.drain()
                nc.vector.tensor_tensor(shift_parts[:, 2, :], shift[:, 1, :], shift_parts[:, 1, :],
                                        ALU.subtract).then_inc(shift_ready, 1)

            def pe_scores(pe, u, b, n):
                Q, k = steps[n]
                lo = max(0, k - 4 * Q) * P if causal else 0
                for j in range(HG):
                    if n:
                        pe.wait_ge(probs_ready, (u * NS + n - 1) * HG + j + 1)
                    diagonal = causal and k >= 4 * Q
                    mm = nc.tensor.matmul(s_ps[:, j, lo:W], ks[b][:, j, k * P:(k + 1) * P],
                                          qs[b][:, j, Q * W + lo:(Q + 1) * W], start=True, stop=not diagonal)
                    if diagonal:
                        mm = nc.tensor.matmul(s_ps[:, j, lo:lo + P], mask[:, 0, :], mask[:, 2, :],
                                              start=False, stop=True)
                    mm.then_inc(scores_ready, 1)

            def pe_sums(pe, u, b, n):
                Q, k = steps[n]
                lo = max(0, k - 4 * Q) * P if causal else 0
                last_k = n + 1 == NS or steps[n + 1][0] != Q
                if k == 0:
                    pe.wait_ge(out_free, u * NQ + Q + 1)
                for j in range(HG):
                    pe.wait_ge(probs_ready, (u * NS + n) * HG + j + 1)
                    mm = nc.tensor.matmul(o_ps[32 * j:32 * j + 32, lo:W], vb[b][:, k, j, :], probs[:, n % 2, j, lo:W],
                                          start=(k == 0), stop=last_k)
                mm.then_inc(probs_free, 1)

            def dve_evacuate(dve, u, Q):
                n_last = max(n for n in range(NS) if steps[n][0] == Q)
                dve.wait_ge(probs_free, u * NS + n_last + 1 + 2)
                nc.vector.tensor_copy(sums[:], o_ps[:]).then_inc(out_free, 1)

            def pe_denominators(pe, u, Q, use):
                pe.wait_ge(out_free, u * NQ + Q + 2)
                pe.wait_ge(misc_free, use + 1)
                nc.tensor.matmul(misc[:], spread_den[:], sums[:], start=True, stop=True).then_inc(misc_full, 1)

            def dve_normalize(dve, u, Q, use):
                dve.wait_ge(misc_full, use + 1)
                nc.vector.reciprocal(recip[:], misc[:]).then_inc(misc_free, 1)
                dve.drain()
                nc.vector.tensor_tensor(normed[:], sums[:], recip[:], ALU.mult).then_inc(normed_ready, 1)

            def pe_project(pe, u, g, Q, use):
                pe.wait_ge(normed_ready, u * NQ + Q + 1)
                pe.wait_ge(misc_free, use + 1)
                for c in range(4):
                    mm = nc.tensor.matmul(misc[:, c * P:(c + 1) * P], normed[:, c * P:(c + 1) * P],
                                          wo_sb[:, g, :], start=True, stop=True)
                mm.then_inc(misc_full, 1)

            def dve_add(dve, b, Q, use):
                dve.wait_ge(misc_full, use + 1)
                at = x[:, b * TB + 4 * Q:b * TB + 4 * Q + 4, :].rearrange("p t n -> p (t n)")
                nc.vector.tensor_tensor(at, misc[:], at, ALU.add).then_inc(misc_free, 1)
                dve.drain()

            q_end = [max(n for n in range(NS) if steps[n][0] == Q) for Q in range(NQ)]
            numbered = [list(enumerate(chunks))[i * share:(i + 1) * share] for i in range(n_steps)]

            def misc_use(u, i):
                return u * NMISC + 1 + i

            with nc.Block() as block:
                @block.sync
                def _(sp):
                    sp.wait_ge(constants_set, 3)
                    for b in range(B):
                        sp.dma_start(ks[b][ROWS:ROWS + 3, :, :].rearrange("p h n -> p (h n)"),
                                     plain[:, 1, :]).then_inc(constants_in, 16)
                    sp.dma_start(mask[:, 0, :], consts["ident_bf"]).then_inc(constants_in, 16)
                    sp.dma_start(mask[:, 1, :], consts["mask_q"]).then_inc(constants_in, 16)
                    sp.dma_start(mask[:, 2, :], consts["mask_k"]).then_inc(constants_in, 16)
                    load_unit(sp, 0, 0, 0)
                    load_shift(sp, 0, 0)

                    def slots(g, last):
                        for b in range(B):
                            u = 2 * g + b
                            if b == 0 or not last:
                                sp.wait_ge(probs_free, u * NS + 2)
                                load_unit(sp, u + 1, 1 - b, g + b)
                                load_shift(sp, u + 1, 1 - b)

                    with sp.Fori(0, G - 1) as g:
                        slots(g, False)
                    slots(G - 1, True)

                @block.gpsimd
                def _(pool):
                    for b in range(B):
                        nc.gpsimd.memset(vb[b][:, :, :, DH + 1:32], 0.0)
                        nc.gpsimd.memset(vb[b][:, :, :, DH:DH + 1], 1.0)
                    pool.drain()
                    for b in range(B):
                        nc.gpsimd.memset(qs[b][64:STACK, :, :], 0.0)
                        pool.drain()
                        nc.gpsimd.memset(ks[b][64:STACK, :, :], 0.0)
                        pool.drain()
                    nc.gpsimd.memset(plain[:, 0, :], 0.0)
                    nc.gpsimd.memset(plain[:, 1, :], 1.0)
                    pool.drain()
                    pool.sem_inc(constants_set, 3)

                    def fill(u, b, g):
                        for j in range(HG):
                            nc.gpsimd.tensor_copy(vb[b][:, :, j, 0:DH],
                                                         v_tok[:, b * TB:(b + 1) * TB,
                                                               bass.ds(g * (HG * DH) + j * DH, DH)])
                        pool.drain()
                        pool.sem_inc(v_in, 1)

                    for b in range(B):
                        fill(b, b, 0)
                    with pool.Fori(1, G) as g:
                        for b in range(B):
                            pool.wait_ge(probs_free, (2 * g + b - 1) * NS + 2)
                            fill(2 * g + b, b, g)

                @block.tensor
                def _(pe):
                    pe.sem_inc(probs_free, 2)
                    pe.wait_ge(constants_in, 16 * 5)
                    pe.wait_ge(stacks_in, 16 * N_LOADS)
                    pe_max(pe, 0, 0, list(enumerate(chunks)))
                    pe_turn_max(pe, 0, 0)

                    def slots(g, last):
                        for b in range(B):
                            u = 2 * g + b
                            has_next = b == 0 or not last
                            pe.wait_ge(shift_in, 48 * u + 96)
                            pe_scores(pe, u, b, 0)
                            pe.wait_ge(v_in, u + 1)
                            for n in range(NS):
                                if n + 1 < NS:
                                    pe_scores(pe, u, b, n + 1)
                                for Q in range(NQ - 1):
                                    if n == q_end[Q] + 2:
                                        pe_denominators(pe, u, Q, misc_use(u, 2 * Q))
                                    if n == q_end[Q] + 4:
                                        pe_project(pe, u, g, Q, misc_use(u, 2 * Q + 1))
                                if has_next and first_step <= n < first_step + n_steps:
                                    if n == first_step:
                                        pe.wait_ge(stacks_in, 16 * N_LOADS * (u + 2))
                                    pe_max(pe, u + 1, 1 - b, numbered[n - first_step])
                                pe_sums(pe, u, b, n)
                                if has_next and n == NS - 2:
                                    pe_turn_max(pe, u + 1, misc_use(u, 2 * NQ - 2))
                            at = 2 * NQ - 2 + has_next
                            pe_denominators(pe, u, NQ - 1, misc_use(u, at))
                            pe_project(pe, u, g, NQ - 1, misc_use(u, at + 1))

                    with pe.Fori(0, G - 1) as g:
                        slots(g, False)
                    slots(G - 1, True)

                @block.scalar
                def _(act):
                    def slot(u):
                        for n, (Q, k) in enumerate(steps):
                            lo = max(0, k - 4 * Q) * P if causal else 0
                            act.wait_ge(probs_free, u * NS + n + 1)
                            for j in range(HG):
                                act.wait_ge(scores_ready, (u * NS + n) * HG + j + 1)
                                nc.scalar.activation(probs[:, n % 2, j, lo:W], s_ps[:, j, lo:W], ACT.Exp,
                                                     scale=SCALE).then_inc(probs_ready, 1)

                    with act.Fori(0, B * G) as u:
                        slot(u)

                @block.vector
                def _(dve):
                    nc.vector.memset(part_max[:], NEG)
                    dve.sem_inc(max_free, 2)
                    dve.sem_inc(misc_free, 1)
                    dve.sem_inc(out_free, 1)
                    dve.sem_inc(shift_in, 48)
                    dve.drain()
                    dve_max(dve, 0, list(enumerate(chunks)))
                    dve_neg_max(dve, 0)
                    dve_split_shift(dve, 0, 0)

                    def slots(g, last):
                        for b in range(B):
                            u = 2 * g + b
                            has_next = b == 0 or not last
                            for n in range(NS):
                                for Q in range(NQ - 1):
                                    if n == q_end[Q] + 2:
                                        dve_normalize(dve, u, Q, misc_use(u, 2 * Q))
                                    if n == q_end[Q] + 4:
                                        dve_add(dve, b, Q, misc_use(u, 2 * Q + 1))
                                if has_next and first_step <= n < first_step + n_steps:
                                    dve_max(dve, u + 1, numbered[n - first_step])
                                    if n == first_step + n_steps - 1:
                                        dve_neg_max(dve, u + 1)
                                if n in q_end:
                                    if n == NS - 1 and has_next:
                                        dve_split_shift(dve, u + 1, misc_use(u, 2 * NQ - 2))
                                    dve_evacuate(dve, u, steps[n][0])
                            at = 2 * NQ - 2 + has_next
                            dve_normalize(dve, u, NQ - 1, misc_use(u, at))
                            dve_add(dve, b, NQ - 1, misc_use(u, at + 1))

                    with dve.Fori(0, G - 1) as g:
                        slots(g, False)
                    slots(G - 1, True)


def wide_attention(nc, name, x, xT, weights, consts, shared_keys):
    DH = 64
    SCALE = DH ** -0.5
    wq, wk, wv, wo, bo = weights
    NH_K = 1 if shared_keys else HEADS
    NQ = S // W
    steps = [(Q, k) for Q in range(NQ) for k in range(TB)]
    NS = len(steps)
    chunks = [(qt, c) for qt in range(TB) for c in range(2)]
    NCH = len(chunks)
    PROJ_AT, MAX_AT = 0, 6
    with Scope(nc, name) as m:
        wq_all = m.sb("wq_all", [P, HEADS, P])
        wk_all = m.sb("wk_all", [P, NH_K, P])
        wv_all = m.sb("wv_all", [P, NH_K, DH])
        wo_all = m.sb("wo_all", [DH + 1, HEADS, D + 1])
        w_now = m.sb("w_now", [P, 2, P])
        bo_row = m.sb("bo_row", [P, D])
        qf = [m.sb(f"qf{b}", [P, S]) for b in range(B)]
        kf = [m.sb(f"kf{b}", [P, S]) for b in range(B)]
        qm = [m.sb(f"qm{b}", [P, S], BF16) for b in range(B)]
        kh = [m.sb(f"kh{b}", [P, S], BF16) for b in range(B)]
        km = [m.sb(f"km{b}", [P, S], BF16) for b in range(B)]
        vb = [m.sb(f"vb{b}", [P, TB, DH + 1]) for b in range(B)]
        probs = m.sb("probs", [P, 3, W])
        part_max = m.sb("part_max", [P, 2, TB])
        neg_max = m.sb("neg_max", [P, TB])
        shift = m.sb("shift", [TB, P])
        sums = m.sb("sums", [DH + 1, W])
        recip = m.sb("recip", [P, 2])
        s_ps = m.ps("s_ps", [P, 2, W])
        m_ps = m.ps("m_ps", [P, 2, W])
        o_ps = m.ps("o_ps", [P, W])
        p_ps = m.ps("p_ps", [P, 2, W])
        misc = m.ps("misc", [P, W])
        loaded = m.sem("loaded")
        constants_set = m.sem("constants_set")
        weights_now = m.sem("weights_now")
        proj_full = m.sem("proj_full")
        proj_free = m.sem("proj_free")
        unit_made = m.sem("unit_made")
        shift_ready = m.sem("shift_ready")
        shift_in = m.sem("shift_in")
        scores_ready = m.sem("scores_ready")
        probs_ready = m.sem("probs_ready")
        probs_free = m.sem("probs_free")
        max_full = m.sem("max_full")
        max_free = m.sem("max_free")
        neg_max_ready = m.sem("neg_max_ready")
        out_free = m.sem("out_free")
        misc_full = m.sem("misc_full")
        misc_free = m.sem("misc_free")

        def jobs(first):
            made = [("q", c) for c in range(NQ)]
            if first or not shared_keys:
                made += [("k", c) for c in range(NQ)] + [("v", 0)]
            return made

        NJ = len(jobs(False))
        FIRST = [len(jobs(True))] * B if shared_keys else [NJ] * B
        HEAD_JOBS = sum(FIRST)

        def job_index(h, b, i):
            return HEAD_JOBS + ((h - 1) * B + b) * NJ + i if not isinstance(h, int) or h else sum(FIRST[:b]) + i

        def misc_use(u, i):
            return u * (2 * NQ + 1) + 1 + i

        with nc.Block() as block:
            @block.sync
            def _(sp):
                for dst, src in ((wq_all, wq), (wk_all, wk), (wv_all, wv), (wo_all, wo)):
                    sp.dma_start(dst[:], src).then_inc(loaded, 16)
                sp.dma_start(bo_row[:], bo.partition_broadcast(P)).then_inc(loaded, 16)
                with sp.Fori(0, HEADS) as h:
                    for b in range(B):
                        sp.wait_ge(shift_ready, 2 * h + b + 1)
                        sp.dma_start(qf[b][DH:DH + 1, :], shift[:]).then_inc(shift_in, 16)

            @block.gpsimd
            def _(pool):
                for b in range(B):
                    nc.gpsimd.memset(vb[b][:, :, DH:DH + 1], 1.0)
                    pool.drain()
                    nc.gpsimd.memset(qf[b][DH:P, :], 0.0)
                    pool.drain()
                    nc.gpsimd.memset(kf[b][DH:P, :], 0.0)
                    pool.drain()
                    nc.gpsimd.memset(kf[b][DH:DH + 1, :], 1.0)
                    pool.drain()
                pool.sem_inc(constants_set, 1)
                pool.wait_ge(loaded, 80)

                def fetch(h):
                    for n, w in enumerate((wq_all, wk_all)):
                        if n == 0 or not shared_keys or isinstance(h, int):
                            nc.gpsimd.tensor_copy(w_now[:, n, :], w[:, h, :] if isinstance(h, int)
                                                  else w[:, bass.ds(h, 1), :].rearrange("p a n -> p (a n)"))
                    pool.drain()
                    pool.sem_inc(weights_now, 1)

                fetch(0)
                with pool.Fori(1, HEADS) as h:
                    pool.wait_ge(proj_full, job_index(h, 0, 0))
                    fetch(h)

            def pe_job(pe, h, b, i, what, c):
                pe.wait_ge(proj_free, job_index(h, b, i) + 1)
                bank = p_ps[:, i % 2 if not shared_keys or not isinstance(h, int) else i % 2, :]
                cols = slice(b * S + c * W, b * S + (c + 1) * W)
                if what in "qk":
                    nc.tensor.matmul(bank, w_now[:, "qk".index(what), :], xT[:, cols],
                                     start=True, stop=True).then_inc(proj_full, 1)
                else:
                    hv = 0 if shared_keys else h
                    for t in range(TB):
                        rhs = wv_all[:, hv, :] if isinstance(hv, int) else \
                            wv_all[:, bass.ds(hv, 1), :].rearrange("p a n -> p (a n)")
                        mm = nc.tensor.matmul(bank[:, t * DH:(t + 1) * DH], xT[:, b * S + t * P:b * S + (t + 1) * P],
                                              rhs, start=True, stop=True)
                    mm.then_inc(proj_full, 1)

            def act_job(act, h, b, i, what, c):
                act.wait_ge(proj_full, job_index(h, b, i) + 1)
                bank = p_ps[:, i % 2, :]
                if what == "v":
                    nc.scalar.copy(vb[b][:, :, 0:DH], bank.rearrange("p (t n) -> p t n", n=DH)).then_inc(unit_made, 1)
                else:
                    full = (qf if what == "q" else kf)[b]
                    high = (qm if what == "q" else kh)[b]
                    nc.scalar.copy(full[0:DH, c * W:(c + 1) * W], bank[0:DH, :])
                    nc.scalar.copy(high[:, c * W:(c + 1) * W], bank).then_inc(unit_made, 1)

            def dve_job(dve, h, b, i, what, c):
                n = job_index(h, b, i)
                dve.wait_ge(unit_made, n + 1)
                bank = p_ps[:, i % 2, :]
                cols = slice(c * W, (c + 1) * W)
                if what == "q":
                    nc.vector.tensor_tensor(qm[b][DH:P, cols], bank[DH:P, :], qm[b][DH:P, cols],
                                            ALU.subtract).then_inc(proj_free, 1)
                elif what == "k":
                    nc.vector.tensor_tensor(km[b][:, cols], bank, kh[b][:, cols], ALU.subtract).then_inc(proj_free, 1)
                else:
                    dve.sem_inc(proj_free, 1)

            def pe_max(pe, u, b, which):
                for i in which:
                    qt, c = chunks[i]
                    pe.wait_ge(max_free, u * NCH + i + 1)
                    q = qm[b][:, qt * P:(qt + 1) * P]
                    nc.tensor.matmul(m_ps[:, i % 2, :], q, kh[b][:, c * W:(c + 1) * W], start=True, stop=False)
                    nc.tensor.matmul(m_ps[:, i % 2, :], q, km[b][:, c * W:(c + 1) * W],
                                     start=False, stop=True).then_inc(max_full, 1)

            def dve_max(dve, u, which):
                for i in which:
                    qt, c = chunks[i]
                    dve.wait_ge(max_full, u * NCH + i + 1)
                    nc.vector.tensor_reduce(part_max[:, c, qt:qt + 1], m_ps[:, i % 2, :], AX_X,
                                            ALU.max).then_inc(max_free, 1)

            def dve_neg_max(dve):
                dve.drain()
                nc.vector.tensor_tensor(neg_max[:], part_max[:, 0, :], part_max[:, 1, :], ALU.max)
                dve.drain()
                nc.vector.tensor_scalar(neg_max[:], neg_max[:], -1.0, None, ALU.mult).then_inc(neg_max_ready, 1)

            def pe_turn_max(pe, u, use):
                pe.wait_ge(neg_max_ready, u + 1)
                pe.wait_ge(misc_free, use + 1)
                nc.tensor.transpose(misc[0:TB, 0:P], neg_max[:], consts["ident_sb"][:]).then_inc(misc_full, 1)

            def dve_shift(dve, u, use):
                dve.wait_ge(misc_full, use + 1)
                dve.wait_ge(shift_in, 16 * u + 16)
                nc.vector.tensor_copy(shift[:], misc[0:TB, 0:P])
                dve.drain()
                dve.sem_inc(misc_free, 1)
                dve.sem_inc(shift_ready, 1)

            def pe_scores(pe, u, b, n):
                Q, k = steps[n]
                if n >= 2:
                    pe.wait_ge(probs_ready, u * NS + n - 1)
                nc.tensor.matmul(s_ps[:, n % 2, :], kf[b][:, k * P:(k + 1) * P], qf[b][:, Q * W:(Q + 1) * W],
                                 start=True, stop=True).then_inc(scores_ready, 1)

            def pe_sums(pe, u, b, n):
                Q, k = steps[n]
                if k == 0:
                    pe.wait_ge(out_free, u * NQ + Q + 1)
                pe.wait_ge(probs_ready, u * NS + n + 1)
                nc.tensor.matmul(o_ps[0:DH + 1, :], vb[b][:, k, :], probs[:, n % 2, :],
                                 start=(k == 0), stop=(k == TB - 1)).then_inc(probs_free, 1)

            def dve_evacuate(dve, u, Q):
                dve.wait_ge(probs_free, u * NS + (Q + 1) * TB + 2)
                nc.vector.tensor_copy(sums[:], o_ps[0:DH + 1, :]).then_inc(out_free, 1)

            def pe_project(pe, u, h, Q, half, use):
                pe.wait_ge(out_free, u * NQ + Q + 2)
                pe.wait_ge(misc_free, use + 1)
                rhs = wo_all[:, h, :] if isinstance(h, int) else \
                    wo_all[:, bass.ds(h, 1), :].rearrange("p a n -> p (a n)")
                for c in range(2):
                    at = 2 * half + c
                    mm = nc.tensor.matmul(misc[:, c * (D + 1):(c + 1) * (D + 1)], sums[:, at * P:(at + 1) * P],
                                          rhs, start=True, stop=True)
                mm.then_inc(misc_full, 1)

            def dve_add(dve, b, Q, half, use):
                dve.wait_ge(misc_full, use + 1)
                for c in range(2):
                    nc.vector.reciprocal(recip[:, c:c + 1], misc[:, c * (D + 1) + D:(c + 1) * (D + 1)])
                dve.drain()
                for c in range(2):
                    t = b * TB + 4 * Q + 2 * half + c
                    nc.vector.scalar_tensor_tensor(x[:, t, :], misc[:, c * (D + 1):c * (D + 1) + D],
                                                   recip[:, c:c + 1], x[:, t, :], ALU.mult, ALU.add)
                dve.drain()
                dve.sem_inc(misc_free, 1)

            at_max = {MAX_AT + n: [2 * n, 2 * n + 1] for n in range(NCH // 2)}

            @block.tensor
            def _(pe):
                pe.wait_ge(loaded, 80)
                pe.wait_ge(constants_set, 1)
                pe.wait_ge(weights_now, 1)
                for i, (what, c) in enumerate(jobs(True)):
                    pe_job(pe, 0, 0, i, what, c)
                pe.wait_ge(proj_free, FIRST[0] + 2)
                pe_max(pe, 0, 0, range(NCH))
                pe_turn_max(pe, 0, 0)

                def slot(h, b, u, next_h, has_next, first):
                    nb = 1 - b
                    pe.wait_ge(shift_in, 16 * u + 32)
                    pe_scores(pe, u, b, 0)
                    made = jobs(first) if has_next else []
                    for n in range(NS):
                        if n + 1 < NS:
                            pe_scores(pe, u, b, n + 1)
                        if has_next and n == 0 and b == 1:
                            pe.wait_ge(weights_now, next_h + 1)
                        if n < len(made):
                            pe_job(pe, next_h, nb, n, *made[n])
                        if n == TB + 2 or n == TB + 4:
                            pe_project(pe, u, h, 0, (n - TB - 2) // 2, misc_use(u, (n - TB - 2) // 2))
                        if has_next and n in at_max:
                            if n == MAX_AT:
                                pe.wait_ge(proj_free, job_index(next_h, nb, len(made) - 1) + 3)
                            pe_max(pe, u + 1, nb, at_max[n])
                        if has_next and n == NS - 1:
                            pe_turn_max(pe, u + 1, misc_use(u, 2))
                        pe_sums(pe, u, b, n)
                    for half in range(2):
                        pe_project(pe, u, h, NQ - 1, half, misc_use(u, 2 + has_next + half))

                slot(0, 0, 0, 0, True, shared_keys)
                slot(0, 1, 1, 1, True, False)
                with pe.Fori(1, HEADS - 1) as h:
                    slot(h, 0, 2 * h, h, True, False)
                    slot(h, 1, 2 * h + 1, h + 1, True, False)
                slot(HEADS - 1, 0, 2 * HEADS - 2, HEADS - 1, True, False)
                slot(HEADS - 1, 1, 2 * HEADS - 1, None, False, False)

            @block.scalar
            def _(act):
                act.wait_ge(constants_set, 1)
                for i, (what, c) in enumerate(jobs(True)):
                    act_job(act, 0, 0, i, what, c)

                def slot(b, u, next_h, has_next, first):
                    made = jobs(first) if has_next else []
                    for n in range(NS):
                        act.wait_ge(scores_ready, u * NS + n + 1)
                        act.wait_ge(probs_free, u * NS + n + 1)
                        nc.scalar.activation(probs[:, n % 2, :], s_ps[:, n % 2, :], ACT.Exp,
                                             scale=SCALE).then_inc(probs_ready, 1)
                        if n < len(made):
                            act_job(act, next_h, 1 - b, n, *made[n])

                slot(0, 0, 0, True, shared_keys)
                slot(1, 1, 1, True, False)
                with act.Fori(1, HEADS - 1) as h:
                    slot(0, 2 * h, h, True, False)
                    slot(1, 2 * h + 1, h + 1, True, False)
                slot(0, 2 * HEADS - 2, HEADS - 1, True, False)
                slot(1, 2 * HEADS - 1, None, False, False)

            @block.vector
            def _(dve):
                dve.sem_inc(proj_free, 2)
                dve.sem_inc(probs_free, 2)
                dve.sem_inc(max_free, 2)
                dve.sem_inc(out_free, 1)
                dve.sem_inc(misc_free, 1)
                dve.sem_inc(shift_in, 16)
                dve.wait_ge(loaded, 80)
                nc.vector.tensor_tensor(x[:], x[:], bo_row[:, None, :].to_broadcast([P, NT, D]), ALU.add)
                for i, (what, c) in enumerate(jobs(True)):
                    dve_job(dve, 0, 0, i, what, c)
                dve_max(dve, 0, range(NCH))
                dve_neg_max(dve)
                dve_shift(dve, 0, 0)

                def slot(b, u, next_h, has_next, first):
                    made = jobs(first) if has_next else []
                    for n in range(NS):
                        if n < len(made):
                            dve_job(dve, next_h, 1 - b, n, *made[n])
                        if n == TB + 2 or n == TB + 4:
                            dve_add(dve, b, 0, (n - TB - 2) // 2, misc_use(u, (n - TB - 2) // 2))
                        if has_next and n in at_max:
                            dve_max(dve, u + 1, at_max[n])
                            if n == max(at_max):
                                dve_neg_max(dve)
                        if has_next and n == NS - 1:
                            dve_shift(dve, u + 1, misc_use(u, 2))
                        if n % TB == TB - 1:
                            dve_evacuate(dve, u, n // TB)
                    for half in range(2):
                        dve_add(dve, b, NQ - 1, half, misc_use(u, 2 + has_next + half))

                slot(0, 0, 0, True, shared_keys)
                slot(1, 1, 1, True, False)
                with dve.Fori(1, HEADS - 1) as h:
                    slot(0, 2 * h, h, True, False)
                    slot(1, 2 * h + 1, h + 1, True, False)
                slot(0, 2 * HEADS - 2, HEADS - 1, True, False)
                slot(1, 2 * HEADS - 1, None, False, False)



def binary_linear(nc, name, x, xT, wT, scale, bias):
    TOP = 100.0
    with Scope(nc, name) as m:
        w_sb = m.sb("w_sb", [P, D])
        signs = m.sb("signs", [P, D])
        rows = m.sb("rows", [P, 2, D])
        y = m.sb("y", [P, NG, 4, D])
        y_ps = m.ps("y_ps", [P, NG, W])
        loaded = m.sem("loaded")
        signs_ready = m.sem("signs_ready")
        made = m.sem("made")
        with nc.Block() as block:
            @block.sync
            def _(sp):
                sp.dma_start(w_sb[:], wT).then_inc(loaded, 16)
                sp.dma_start(rows[:, 0, :], scale.partition_broadcast(P)).then_inc(loaded, 16)
                sp.dma_start(rows[:, 1, :], bias.partition_broadcast(P)).then_inc(loaded, 16)

            @block.tensor
            def _(pe):
                pe.wait_ge(signs_ready, 1)
                for g in range(NG):
                    for c in range(4):
                        t = 4 * g + c
                        mm = nc.tensor.matmul(y_ps[:, g, c * P:(c + 1) * P], xT[:, t * P:(t + 1) * P], signs[:],
                                              start=True, stop=True)
                    mm.then_inc(made, 1)

            @block.vector
            def _(dve):
                dve.wait_ge(loaded, 48)
                nc.vector.tensor_scalar(signs[:], w_sb[:], 0.0, 2.0, ALU.is_ge, ALU.mult)
                dve.drain()
                nc.vector.tensor_scalar(signs[:], signs[:], -1.0, None, ALU.add).then_inc(signs_ready, 1)
                for g in range(NG):
                    dve.wait_ge(made, g + 1)
                    yg = y[:, g, :, :]
                    nc.vector.tensor_tensor(yg, y_ps[:, g, :].rearrange("p (t n) -> p t n", n=D),
                                            rows[:, 0:1, :].to_broadcast([P, 4, D]), ALU.mult)
                    dve.drain()
                    nc.vector.tensor_tensor(yg, yg, rows[:, 1:2, :].to_broadcast([P, 4, D]), ALU.add)
                    dve.drain()
                    nc.vector.tensor_scalar(yg, yg, TOP, -TOP, ALU.min, ALU.max)
                    dve.drain()
                    xg = x[:, 4 * g:4 * g + 4, :]
                    nc.vector.tensor_tensor(xg, xg, yg, ALU.add)


def top2_experts(nc, name, x, xT, wg, w1, w2, w3, lower):
    E, HT, HP = 8, 3, 114
    with Scope(nc, name) as m:
        wg_sb = m.sb("wg_sb", [P, E])
        lower_sb = m.sb("lower_sb", [P, E, E])
        logits = m.sb("logits", [P, NT, E])
        gating = m.sb("gating", [P, NT, E])
        gate_now = m.sb("gate_now", [P, 2, NT])
        above = m.sb("above", [P, NT, E, E])
        ties = m.sb("ties", [P, NT, E, E])
        rank = m.sb("rank", [P, NT, E])
        stat = m.sb("stat", [P, NT])
        w12 = m.sb("w12", [P, 2, 2, HT * HP])
        w3_sb = m.sb("w3_sb", [HP, 2, HT, D])
        silu = m.sb("silu", [HP, 2, W])
        hidden = m.sb("hidden", [HP, 2, HT, W])
        g_ps = m.ps("g_ps", [P, W])
        up_ps = m.ps("up_ps", [P, 2, W])
        lin_ps = m.ps("lin_ps", [P, 2, W])
        y_ps = m.ps("y_ps", [P, 2, W])
        loaded = m.sem("loaded")
        logits_made = m.sem("logits_made")
        shifted = m.sem("shifted")
        exps_ready = m.sem("exps_ready")
        weights_in = [m.sem(f"weights_in{r}") for r in range(2)]
        up_full = m.sem("up_full")
        lin_full = m.sem("lin_full")
        silu_done = m.sem("silu_done")
        hidden_ready = m.sem("hidden_ready")
        y_full = m.sem("y_full")
        y_free = m.sem("y_free")

        with nc.Block() as block:
            @block.sync
            def _(sp):
                sp.dma_start(wg_sb[:], wg).then_inc(loaded, 16)
                sp.dma_start(lower_sb[:], lower.partition_broadcast(P)).then_inc(loaded, 16)

                def load(e, r):
                    one = bass.ds(e, 1)
                    sp.dma_start(w12[:, r, 0, :], w1[one, :, :].rearrange("a p n -> p (a n)")).then_inc(weights_in[r], 16)
                    sp.dma_start(w12[:, r, 1, :], w2[one, :, :].rearrange("a p n -> p (a n)")).then_inc(weights_in[r], 16)
                    sp.dma_start(w3_sb[:, r, :, :], w3[one, :, :, :].rearrange("a p t n -> p (a t) n")
                                 ).then_inc(weights_in[r], 16)

                load(0, 0)
                load(1, 1)
                with sp.Fori(1, E // 2) as pair:
                    for r in range(2):
                        sp.wait_ge(y_full, (2 * pair + r - 1) * NG + 2)
                        load(2 * pair + r, r)

            @block.tensor
            def _(pe):
                pe.wait_ge(loaded, 32)
                for t in range(NT):
                    mm = nc.tensor.matmul(g_ps[:, t * E:(t + 1) * E], xT[:, t * P:(t + 1) * P], wg_sb[:],
                                          start=True, stop=True)
                mm.then_inc(logits_made, 1)

                def up(e, r, g, i):
                    n = (e * NG + g) * HT + i
                    k = (g * HT + i) % 2
                    for ps, j, full, freed in ((up_ps, 0, up_full, silu_done), (lin_ps, 1, lin_full, hidden_ready)):
                        pe.wait_ge(freed, n + 1)
                        nc.tensor.matmul(ps[0:HP, k, :], w12[:, r, j, i * HP:(i + 1) * HP],
                                         xT[:, g * W:(g + 1) * W], start=True, stop=True).then_inc(full, 1)

                def down(e, r, g):
                    n = e * NG + g
                    pe.wait_ge(y_free, n + 1)
                    pe.wait_ge(hidden_ready, (n + 1) * HT + 2)
                    for c in range(4):
                        for i in range(HT):
                            mm = nc.tensor.matmul(y_ps[:, g % 2, c * P:(c + 1) * P],
                                                  hidden[:, g % 2, i, c * P:(c + 1) * P], w3_sb[:, r, i, :],
                                                  start=(i == 0), stop=(i == HT - 1))
                    mm.then_inc(y_full, 1)

                with pe.Fori(0, E // 2) as pair:
                    for r in range(2):
                        e = 2 * pair + r
                        pe.wait_ge(weights_in[r], 48 * (pair + 1))
                        for g in range(NG):
                            for i in range(HT):
                                up(e, r, g, i)
                                if i == 1 and g:
                                    down(e, r, g - 1)
                        down(e, r, NG - 1)

            @block.scalar
            def _(act):
                act.wait_ge(shifted, 1)
                nc.scalar.activation(gating[:], gating[:], ACT.Exp).then_inc(exps_ready, 1)
                with act.Fori(0, E // 2) as pair:
                    for r in range(2):
                        for g in range(NG):
                            for i in range(HT):
                                n = ((2 * pair + r) * NG + g) * HT + i
                                k = (g * HT + i) % 2
                                act.wait_ge(up_full, n + 1)
                                act.wait_ge(hidden_ready, n + 1)
                                nc.scalar.activation(silu[:, k, :], up_ps[0:HP, k, :],
                                                     ACT.Silu).then_inc(silu_done, 1)

            @block.vector
            def _(dve):
                dve.sem_inc(silu_done, 2)
                dve.sem_inc(hidden_ready, 2)
                dve.sem_inc(y_full, 2)
                dve.sem_inc(y_free, 2)
                dve.wait_ge(logits_made, 1)
                nc.vector.tensor_copy(logits[:], g_ps[:, 0:NT * E].rearrange("p (t e) -> p t e", e=E))
                dve.drain()
                nc.vector.tensor_reduce(stat[:], logits[:], AX_X, ALU.max)
                dve.drain()
                nc.vector.tensor_tensor(gating[:], logits[:], stat[:, :, None].to_broadcast([P, NT, E]),
                                        ALU.subtract).then_inc(shifted, 1)
                for t in range(NT):
                    other = logits[:, t, None, :].to_broadcast([P, E, E])
                    own = logits[:, t, :, None].to_broadcast([P, E, E])
                    nc.vector.tensor_tensor(above[:, t, :, :], other, own, ALU.is_gt)
                    nc.vector.tensor_tensor(ties[:, t, :, :], other, own, ALU.is_equal)
                dve.drain()
                nc.vector.tensor_tensor(ties[:].rearrange("p t a b -> p t (a b)"),
                                        ties[:].rearrange("p t a b -> p t (a b)"),
                                        lower_sb[:].rearrange("p a b -> p (a b)")[:, None, :]
                                        .to_broadcast([P, NT, E * E]), ALU.mult)
                dve.drain()
                nc.vector.tensor_tensor(above[:], above[:], ties[:], ALU.add)
                dve.drain()
                nc.vector.tensor_reduce(rank[:], above[:], AX_X, ALU.add)
                dve.drain()
                nc.vector.tensor_scalar(rank[:], rank[:], 1.5, None, ALU.is_lt)
                dve.wait_ge(exps_ready, 1)
                dve.drain()
                nc.vector.tensor_tensor(gating[:], gating[:], rank[:], ALU.mult)
                dve.drain()
                nc.vector.tensor_reduce(stat[:], gating[:], AX_X, ALU.add)
                dve.drain()
                nc.vector.reciprocal(stat[:], stat[:])
                dve.drain()
                nc.vector.tensor_tensor(gating[:], gating[:], stat[:, :, None].to_broadcast([P, NT, E]), ALU.mult)
                dve.drain()

                def product(e, g, i):
                    n = (e * NG + g) * HT + i
                    k = (g * HT + i) % 2
                    if i == 0:
                        dve.wait_ge(y_full, e * NG + g + 1)
                    dve.wait_ge(lin_full, n + 1)
                    dve.wait_ge(silu_done, n + 3)
                    nc.vector.tensor_tensor(hidden[:, g % 2, i, :], silu[:, k, :], lin_ps[0:HP, k, :],
                                            ALU.mult).then_inc(hidden_ready, 1)

                def add(e, r, g):
                    dve.wait_ge(y_full, e * NG + g + 3)
                    for c in range(4):
                        t = 4 * g + c
                        last = nc.vector.scalar_tensor_tensor(x[:, t, :], y_ps[:, g % 2, c * P:(c + 1) * P],
                                                              gate_now[:, r, t:t + 1], x[:, t, :], ALU.mult, ALU.add)
                    last.then_inc(y_free, 1)

                with dve.Fori(0, E // 2) as pair:
                    for r in range(2):
                        e = 2 * pair + r
                        nc.vector.tensor_copy(gate_now[:, r, :],
                                              gating[:, :, bass.ds(e, 1)].rearrange("p t a -> p (t a)"))
                        for g in range(NG):
                            for i in range(HT):
                                product(e, g, i)
                                if i == 2 and g:
                                    add(e, r, g - 1)
                        add(e, r, NG - 1)
                        dve.drain()


def routed_experts(nc, name, x, xT, w, consts):
    E, H, GS, BUDGET = 64, 32, 64, (B * S // 64) * 16
    N = B * S
    HT = E * H // P
    BIG = 1e30
    with Scope(nc, name) as outer:
        fsT = outer.sb("fsT", [E, N])

        with Scope(nc, name + "r") as m:
            wr = m.sb("wr", [P, E])
            br = m.sb("br", [P, E])
            rank_row = m.sb("rank_row", [P, N // 2])
            ones = m.sb("ones", [P, E])
            score = m.sb("score", [P, NT, E])
            stat = m.sb("stat", [P, NT])
            sT = m.sb("sT", [E, N])
            halves = m.sb("halves", [P, 2, N // 2])
            other = m.sb("other", [E, N // 2])
            sums = m.sb("sums", [P, 16])
            all_sums = m.sb("all_sums", [P, N])
            greater = m.sb("greater", [P, N])
            ties = m.sb("ties", [P, N])
            so_far = m.sb("so_far", [E, N])
            always = m.sb("always", [E, N])
            counts = m.sb("counts", [P, 16])
            one = m.sb("one", [P, 8])
            per_expert = m.sb("per_expert", [E, E])
            t_ps = m.ps("t_ps", [P, 4, W])
            l_ps = m.ps("l_ps", [P, 2, W])
            loaded = m.sem("loaded")
            logits_made = m.sem("logits_made")
            shifted = m.sem("shifted")
            exps_ready = m.sem("exps_ready")
            scores_ready = m.sem("scores_ready")
            turned = m.sem("turned")
            sums_ready = m.sem("sums_ready")
            sums_turned = m.sem("sums_turned")
            least_ready = m.sem("least_ready")
            least_turned = m.sem("least_turned")
            fs_ready = m.sem("fs_ready")
            totals_made = m.sem("totals_made")

            with nc.Block() as block:
                @block.sync
                def _(sp):
                    sp.dma_start(wr[:], w["wr"]).then_inc(loaded, 16)
                    sp.dma_start(br[:], w["br"].partition_broadcast(P)).then_inc(loaded, 16)
                    sp.dma_start(rank_row[:], consts["rank_row"]).then_inc(loaded, 16)

                @block.tensor
                def _(pe):
                    ident = consts["ident_sb"]
                    pe.wait_ge(loaded, 48)
                    for t in range(NT):
                        at = 2 * (t % TB) + t // TB
                        mm = nc.tensor.matmul(l_ps[:, at // 8, at % 8 * E:(at % 8 + 1) * E], xT[:, t * P:(t + 1) * P],
                                              wr[:], start=True, stop=True)
                    mm.then_inc(logits_made, 1)
                    pe.wait_ge(scores_ready, 1)
                    for t in range(TB):
                        mm = nc.tensor.transpose(t_ps[:, t // 4, t % 4 * P:(t % 4 + 1) * P],
                                                 score[:, 2 * t:2 * t + 2, :].rearrange("p h e -> p (h e)"), ident[:])
                    mm.then_inc(turned, 1)
                    pe.wait_ge(sums_ready, 1)
                    for c in range(16):
                        mm = nc.tensor.transpose(t_ps[:, c // 4, c % 4 * P:(c % 4 + 1) * P],
                                                 sums[:, c:c + 1].to_broadcast([P, P]), ident[:])
                    mm.then_inc(sums_turned, 1)
                    pe.wait_ge(least_ready, 1)
                    nc.tensor.transpose(l_ps[:, 0, 0:P], one[:, 0:1].to_broadcast([P, P]),
                                        ident[:]).then_inc(least_turned, 1)
                    pe.wait_ge(fs_ready, 1)
                    for g in range(NG):
                        mm = nc.tensor.matmul(t_ps[0:E, g, :], ones[0:E, :], fsT[:, g * W:(g + 1) * W],
                                              start=True, stop=True)
                    mm.then_inc(totals_made, 1)

                @block.scalar
                def _(act):
                    act.wait_ge(shifted, 1)
                    nc.scalar.activation(score[:], score[:], ACT.Exp).then_inc(exps_ready, 1)

                @block.vector
                def _(dve):
                    tt, ts = nc.vector.tensor_tensor, nc.vector.tensor_scalar
                    nc.vector.memset(ones[:], 1.0)
                    nc.vector.memset(always[:], 1.0)
                    dve.wait_ge(loaded, 48)
                    dve.wait_ge(logits_made, 1)
                    for h in range(2):
                        tt(score[:, 8 * h:8 * h + 8, :], l_ps[:, h, :].rearrange("p (t e) -> p t e", e=E),
                           br[:, None, :].to_broadcast([P, 8, E]), ALU.add)
                    dve.drain()
                    nc.vector.tensor_reduce(stat[:], score[:], AX_X, ALU.max)
                    dve.drain()
                    wide = stat[:, :, None].to_broadcast([P, NT, E])
                    tt(score[:], score[:], wide, ALU.subtract).then_inc(shifted, 1)
                    dve.wait_ge(exps_ready, 1)
                    nc.vector.tensor_reduce(stat[:], score[:], AX_X, ALU.add)
                    dve.drain()
                    nc.vector.reciprocal(stat[:], stat[:])
                    dve.drain()
                    tt(score[:], score[:], wide, ALU.mult).then_inc(scores_ready, 1)

                    dve.wait_ge(turned, 1)
                    for h in range(2):
                        at = slice(h * W, (h + 1) * W)
                        nc.vector.tensor_copy(sT[:, at], t_ps[0:E, h, :])
                        nc.vector.tensor_copy(sT[:, N // 2 + h * W:N // 2 + (h + 1) * W], t_ps[E:P, h, :])
                        nc.vector.tensor_copy(halves[0:E, 0, at], t_ps[0:E, h, :])
                        ts(halves[E:P, 0, at], t_ps[E:P, h, :], -1.0, None, ALU.mult)
                    dve.drain()

                    src = 0
                    n = N // 2

                    def exchange(frm, to, k, j):
                        turns = 2 if k < n else 1
                        views = [halves[:, v, :].rearrange("p (a d b s j) -> p a d b s j", d=turns, b=k // (2 * j),
                                                           s=2, j=j) for v in (frm, to)]
                        for d in range(turns):
                            lo, hi = (views[0][:, :, d, :, s, :] for s in range(2))
                            for s in range(2):
                                tt(views[1][:, :, d, :, s, :], lo, hi, ALU.max if s == d else ALU.min)
                        dve.drain()

                    k = 2
                    while k <= n:
                        j = k // 2
                        while j:
                            exchange(src, 1 - src, k, j)
                            src = 1 - src
                            j //= 2
                        k *= 2
                    ts(other[:], halves[E:P, src, :], -1.0, None, ALU.mult)
                    dve.drain()
                    tt(halves[0:E, 1 - src, :], halves[0:E, src, :], other[:], ALU.max)
                    tt(halves[E:P, 1 - src, :], halves[0:E, src, :], other[:], ALU.min)
                    dve.drain()
                    src = 1 - src
                    j = n // 2
                    while j:
                        exchange(src, 1 - src, n, j)
                        src = 1 - src
                        j //= 2
                    ranked = halves[:, src, :]

                    nc.vector.tensor_reduce(sums[:], ranked.rearrange("p (g n) -> p g n", n=GS), AX_X,
                                            ALU.add).then_inc(sums_ready, 1)
                    dve.wait_ge(sums_turned, 1)
                    flat = all_sums[:].rearrange("p (h c e) -> p c h e", h=2, e=E)
                    for c in range(16):
                        nc.vector.tensor_copy(flat[:, c, :, :], t_ps[:, c // 4, c % 4 * P:(c % 4 + 1) * P]
                                              .rearrange("p (h e) -> p h e", e=E))
                    dve.drain()
                    for c in range(16):
                        ts(greater[:], all_sums[:], sums[:, c:c + 1], 0.0, ALU.is_gt, ALU.add,
                           accum_out=counts[:, c:c + 1])
                        dve.drain()
                    ts(counts[:], counts[:], BUDGET - 0.5, BIG, ALU.is_gt, ALU.mult)
                    dve.drain()
                    tt(counts[:], counts[:], sums[:], ALU.add)
                    dve.drain()
                    nc.vector.tensor_reduce(one[:, 0:1], counts[:], AX_X, ALU.min).then_inc(least_ready, 1)
                    dve.wait_ge(least_turned, 1)
                    nc.vector.tensor_reduce(one[:, 1:2], l_ps[:, 0, 0:P], AX_X, ALU.min)
                    dve.drain()

                    def keep(values, least, budget, room, rows):
                        gr, ti = greater[0:rows, :], ties[0:rows, :]
                        ts(gr, values, least, 0.0, ALU.is_gt, ALU.add, accum_out=room)
                        dve.drain()
                        if isinstance(budget, float):
                            ts(room, room, -1.0, budget, ALU.mult, ALU.add)
                        else:
                            tt(room, budget, room, ALU.subtract)
                        ts(ti, values, least, None, ALU.is_equal)
                        dve.drain()
                        nc.vector.tensor_tensor_scan(so_far[0:rows, :], always[0:rows, :], ti, 0.0,
                                                     ALU.mult, ALU.add)
                        dve.drain()
                        ts(so_far[0:rows, :], so_far[0:rows, :], room, None, ALU.is_le)
                        dve.drain()
                        tt(ti, ti, so_far[0:rows, :], ALU.mult)
                        dve.drain()
                        tt(gr, gr, ti, ALU.add)
                        dve.drain()

                    keep(all_sums[0:E, :], one[0:E, 1:2], float(BUDGET), one[0:E, 2:3], E)
                    nc.vector.tensor_reduce(per_expert[:], greater[0:E, :].rearrange("p (g e) -> p e g", e=E), AX_X,
                                            ALU.add)
                    dve.drain()
                    tt(per_expert[:], per_expert[:], consts["ident_sb"][0:E, 0:E], ALU.mult)
                    dve.drain()
                    nc.vector.tensor_reduce(one[0:E, 3:4], per_expert[:], AX_X, ALU.add)
                    dve.drain()
                    ts(one[0:E, 4:5], one[0:E, 3:4], float(GS), None, ALU.mult)
                    ts(one[E:P, 4:5], one[0:E, 3:4], float(GS), None, ALU.mult)
                    dve.drain()
                    ts(halves[:, 1 - src, :], rank_row[:], one[:, 4:5], BIG, ALU.is_ge, ALU.mult)
                    dve.drain()
                    tt(halves[:, 1 - src, :], halves[:, 1 - src, :], ranked, ALU.add)
                    dve.drain()
                    nc.vector.tensor_reduce(one[:, 5:6], halves[:, 1 - src, :], AX_X, ALU.min)
                    dve.drain()
                    nc.vector.tensor_copy(one[0:E, 6:7], one[E:P, 5:6])
                    dve.drain()
                    tt(one[0:E, 5:6], one[0:E, 5:6], one[0:E, 6:7], ALU.min)
                    dve.drain()
                    keep(sT[:], one[0:E, 5:6], one[0:E, 4:5], one[0:E, 7:8], E)
                    tt(fsT[:], sT[:], greater[0:E, :], ALU.mult).then_inc(fs_ready, 1)
                    dve.wait_ge(totals_made, 1)
                    total = t_ps[0:E, :, :].rearrange("p g n -> p (g n)")
                    ts(sT[:], total, 1e-6, None, ALU.add)
                    dve.drain()
                    nc.vector.reciprocal(sT[:], sT[:])
                    dve.drain()
                    tt(fsT[:], fsT[:], sT[:], ALU.mult)

        with Scope(nc, name + "f") as m:
            wup = m.sb("wup", [P, E * H])
            wgate = m.sb("wgate", [P, E * H])
            wdown = m.sb("wdown", [P, HT, D])
            bdown = m.sb("bdown", [E, D])
            spread = m.sb("spread", [E, HT, P])
            bias = m.sb("bias", [P, 2, HT])
            fs_now = m.sb("fs_now", [E, W])
            silu = m.sb("silu", [P, 2, W])
            prod = m.sb("prod", [P, 2, W])
            hidden = m.sb("hidden", [P, HT, W])
            up_ps = m.ps("up_ps", [P, 2, W])
            gate_ps = m.ps("gate_ps", [P, 2, W])
            fs_ps = m.ps("fs_ps", [P, 2, W])
            y_ps = m.ps("y_ps", [P, W])
            loaded = m.sem("loaded")
            up_full = m.sem("up_full")
            gate_full = m.sem("gate_full")
            fs_full = m.sem("fs_full")
            silu_done = m.sem("silu_done")
            prod_done = m.sem("prod_done")
            hidden_ready = m.sem("hidden_ready")
            fs_copied = m.sem("fs_copied")
            y_full = m.sem("y_full")
            y_free = m.sem("y_free")
            with nc.Block() as block:
                @block.sync
                def _(sp):
                    for dst, src in ((wup, "wup"), (wgate, "wgate"), (wdown, "wdown"), (bdown, "bdown"),
                                     (bias, "bias")):
                        sp.dma_start(dst[:], w[src]).then_inc(loaded, 16)
                    sp.dma_start(spread[:], consts["spread_expert"]).then_inc(loaded, 16)

                @block.tensor
                def _(pe):
                    pe.wait_ge(loaded, 96)
                    with pe.Fori(0, NG) as g:
                        for i in range(HT):
                            n = g * HT + i
                            tokens = xT[:, bass.ds(g * W, W)]
                            pe.wait_ge(silu_done, n + 1)
                            nc.tensor.matmul(up_ps[:, i % 2, :], wup[:, i * P:(i + 1) * P], tokens,
                                             start=True, stop=True).then_inc(up_full, 1)
                            pe.wait_ge(prod_done, n + 1)
                            nc.tensor.matmul(gate_ps[:, i % 2, :], wgate[:, i * P:(i + 1) * P], tokens,
                                             start=True, stop=True).then_inc(gate_full, 1)
                            pe.wait_ge(hidden_ready, n + 1)
                            if i == 0:
                                pe.wait_ge(fs_copied, g + 1)
                            nc.tensor.matmul(fs_ps[:, i % 2, :], spread[:, i, :], fs_now[:],
                                             start=True, stop=True).then_inc(fs_full, 1)
                        pe.wait_ge(y_free, g + 1)
                        pe.wait_ge(hidden_ready, (g + 1) * HT + 2)
                        for c in range(4):
                            cols = slice(c * P, (c + 1) * P)
                            for i in range(HT):
                                nc.tensor.matmul(y_ps[:, cols], hidden[:, i, cols], wdown[:, i, :],
                                                 start=(i == 0), stop=False)
                            mm = nc.tensor.matmul(y_ps[:, cols], fs_now[:, cols], bdown[:], start=False, stop=True)
                        mm.then_inc(y_full, 1)

                @block.scalar
                def _(act):
                    act.wait_ge(loaded, 96)
                    with act.Fori(0, NG) as g:
                        act.wait_ge(y_full, g + 1)
                        nc.scalar.copy(fs_now[:], fsT[:, bass.ds(g * W, W)]).then_inc(fs_copied, 1)
                        for i in range(HT):
                            n = g * HT + i
                            act.wait_ge(up_full, n + 1)
                            act.wait_ge(prod_done, n + 1)
                            nc.scalar.activation(silu[:, i % 2, :], up_ps[:, i % 2, :], ACT.Silu,
                                                 bias=bias[:, 0, i:i + 1]).then_inc(silu_done, 1)

                @block.vector
                def _(dve):
                    for s, k in ((silu_done, 2), (prod_done, 2), (hidden_ready, 2), (y_full, 1), (y_free, 1)):
                        dve.sem_inc(s, k)
                    dve.wait_ge(loaded, 96)
                    with dve.Fori(0, NG) as g:
                        for i in range(HT + 1):
                            n = g * HT + i
                            if i < HT:
                                dve.wait_ge(gate_full, n + 1)
                                dve.wait_ge(silu_done, n + 3)
                                dve.wait_ge(hidden_ready, n + 1)
                                nc.vector.scalar_tensor_tensor(prod[:, i % 2, :], gate_ps[:, i % 2, :],
                                                               bias[:, 1, i:i + 1], silu[:, i % 2, :],
                                                               ALU.add, ALU.mult).then_inc(prod_done, 1)
                            if i == 0:
                                dve.wait_ge(y_full, g + 1)
                            else:
                                k = i - 1
                                dve.wait_ge(fs_full, n)
                                dve.wait_ge(prod_done, n + 2)
                                nc.vector.tensor_tensor(hidden[:, k, :], prod[:, k % 2, :], fs_ps[:, k % 2, :],
                                                        ALU.mult).then_inc(hidden_ready, 1)
                        dve.wait_ge(y_full, g + 2)
                        xg = x[:, bass.ds(g * 4, 4), :].rearrange("p t n -> p (t n)")
                        nc.vector.tensor_tensor(xg, y_ps[:], xg, ALU.add).then_inc(y_free, 1)
                        dve.drain()


def leaf_layers(nc, name, yT, outT, w, act_fn, consts):
    DEPTH, NL, LW = 8, 256, 16
    TILES = NL * LW // P
    with Scope(nc, name) as outer:
        onesT = outer.sb("onesT", [P, 2, B * S], BF16)
        b2_parts = outer.sb("b2_parts", [P, 3, 2, D], BF16)
        pick = outer.sb("pick", [P, TILES // 2, P], BF16)

        with Scope(nc, name + "t") as m:
            nw = m.sb("nw", [P, NL])
            nb = m.sb("nb", [P, NL])
            b2 = m.sb("b2", [P, 2, 2, D])
            ident_bf = m.sb("ident_bf", [P, P], BF16)
            right = m.sb("right", [P, NT, NL], BF16)
            ways = m.sb("ways", [P, 2, NT, NL], BF16)
            l_ps = m.ps("l_ps", [P, 4, W])
            t_ps = m.ps("t_ps", [P, 2, 2, S], BF16)
            loaded = m.sem("loaded")
            logits_full = m.sem("logits_full")
            logits_free = m.sem("logits_free")
            ones_ready = m.sem("ones_ready")
            turned = m.sem("turned")
            with nc.Block() as block:
                @block.sync
                def _(sp):
                    sp.dma_start(nw[:], w["nw"]).then_inc(loaded, 16)
                    sp.dma_start(nb[:], w["nb"].partition_broadcast(P)).then_inc(loaded, 16)
                    sp.dma_start(b2[:, 0, :, :], w["b2"]).then_inc(loaded, 16)
                    sp.dma_start(ident_bf[:], consts["ident_bf"]).then_inc(loaded, 16)
                    sp.dma_start(pick[:], consts["pick"]).then_inc(loaded, 16)
                    sp.wait_ge(loaded, 80)

                @block.tensor
                def _(pe):
                    pe.wait_ge(loaded, 80)
                    for t in range(NT):
                        if t >= 8 and t % 2 == 0:
                            pe.wait_ge(logits_free, t // 2 - 3)
                        mm = nc.tensor.matmul(l_ps[:, t // 2 % 4, t % 2 * NL:(t % 2 + 1) * NL],
                                              yT[:, t * P:(t + 1) * P], nw[:], start=True, stop=True)
                        if t % 2:
                            mm.then_inc(logits_full, 1)
                    pe.wait_ge(ones_ready, 1)
                    last = DEPTH % 2
                    for h in range(2):
                        for t in range(NT):
                            mm = nc.tensor.transpose(t_ps[:, h, t // TB, t % TB * P:(t % TB + 1) * P],
                                                     ways[:, last, t, h * P:(h + 1) * P], ident_bf[:])
                    mm.then_inc(turned, 1)

                @block.vector
                def _(dve):
                    dve.wait_ge(loaded, 80)
                    nc.vector.tensor_scalar(nb[:], nb[:], -1.0, None, ALU.mult)
                    nc.vector.memset(ways[:, 0, :, 0:1], 1.0)
                    nc.vector.tensor_copy(b2_parts[:, 0, :, :], b2[:, 0, :, :])
                    dve.drain()
                    nc.vector.tensor_tensor(b2[:, 1, :, :], b2[:, 0, :, :], b2_parts[:, 0, :, :], ALU.subtract)
                    dve.drain()
                    nc.vector.tensor_copy(b2_parts[:, 1, :, :], b2[:, 1, :, :])
                    dve.drain()
                    nc.vector.tensor_tensor(b2_parts[:, 2, :, :], b2[:, 1, :, :], b2_parts[:, 1, :, :], ALU.subtract)
                    for s in range(NT // 2):
                        dve.wait_ge(logits_full, s + 1)
                        nc.vector.tensor_tensor(right[:, 2 * s:2 * s + 2, :],
                                                l_ps[:, s % 4, :].rearrange("p (t n) -> p t n", n=NL),
                                                nb[:, None, :].to_broadcast([P, 2, NL]),
                                                ALU.is_gt).then_inc(logits_free, 1)
                    for level in range(DEPTH):
                        n = 2 ** level
                        now = ways[:, level % 2, :, 0:n]
                        nxt = ways[:, 1 - level % 2, :, 0:2 * n].rearrange("p t (j s) -> p t j s", s=2)
                        dve.drain()
                        nc.vector.tensor_tensor(nxt[:, :, :, 1], now, right[:, :, n - 1:2 * n - 1], ALU.mult)
                        dve.drain()
                        last = nc.vector.tensor_tensor(nxt[:, :, :, 0], now, nxt[:, :, :, 1], ALU.subtract)
                    last.then_inc(ones_ready, 1)

                @block.scalar
                def _(act):
                    act.wait_ge(turned, 1)
                    for h in range(2):
                        for b in range(B):
                            nc.scalar.copy(onesT[:, h, b * S:(b + 1) * S], t_ps[:, h, b, :])

        with Scope(nc, name + "l") as m:
            w1 = m.sb("w1", [P, 2, P + 1])
            w2 = m.sb("w2", [P, 2, D])
            active = m.sb("active", [P, 2, W])
            own = m.sb("own", [P, NG, W])
            acc = m.ps("acc", [P, NG, W])
            h_ps = m.ps("h_ps", [P, 2, W])
            m_ps = m.ps("m_ps", [P, 2, W])
            weights_in = [m.sem(f"weights_in{r}") for r in range(2)]
            hidden_full = m.sem("hidden_full")
            ones_full = m.sem("ones_full")
            active_done = m.sem("active_done")
            own_done = m.sem("own_done")
            summed = m.sem("summed")
            finished = m.sem("finished")
            with nc.Block() as block:
                @block.sync
                def _(sp):
                    def load(i, r):
                        for dst, src in ((w1, w["w1"]), (w2, w["w2"])):
                            sp.dma_start(dst[:, r, :], src[bass.ds(i, 1), :, :].rearrange("a p n -> p (a n)")
                                         ).then_inc(weights_in[r], 16)

                    load(0, 0)
                    load(1, 1)
                    with sp.Fori(1, TILES // 2) as pair:
                        for r in range(2):
                            sp.wait_ge(summed, NG * (2 * pair + r))
                            load(2 * pair + r, r)

                @block.tensor
                def _(pe):
                    def hidden(pair, r, g, half, at):
                        k = (2 * pair + r) * NG + g
                        cols = slice(g * W, (g + 1) * W)
                        if g == 0:
                            pe.wait_ge(weights_in[r], 32 * (pair + 1))
                        pe.wait_ge(active_done, k + 1)
                        nc.tensor.matmul(h_ps[:, g % 2, :], w1[:, r, 0:P], yT[:, cols],
                                         start=True, stop=True).then_inc(hidden_full, 1)
                        pe.wait_ge(own_done, k + 1)
                        rows = pick[:, at, :] if isinstance(at, int) else \
                            pick[:, bass.ds(at, 1), :].rearrange("p a n -> p (a n)")
                        nc.tensor.matmul(m_ps[:, g % 2, :], rows, onesT[:, half, cols],
                                         start=True, stop=True).then_inc(ones_full, 1)

                    def total(pair, r, g):
                        k = (2 * pair + r) * NG + g
                        pe.wait_ge(own_done, k + 3)
                        nc.tensor.matmul(acc[:, g, :], w2[:, r, :], own[:, g, :],
                                         start=False, stop=False).then_inc(summed, 1)

                    def biases(half):
                        for g in range(NG):
                            for c in range(3):
                                mm = nc.tensor.matmul(acc[:, g, :], b2_parts[:, c, half, :],
                                                      onesT[:, half, g * W:(g + 1) * W],
                                                      start=(half == 0 and c == 0), stop=(half == 1 and c == 2))
                        return mm

                    def body(pair, half, at, first):
                        for r in range(2):
                            for g in range(NG):
                                hidden(pair, r, g, half, at + r)
                                back = NG * r + g - 2
                                if back >= 0:
                                    total(pair, back // NG, back % NG)
                                elif not first:
                                    total(pair - 1, 1, NG + back)

                    biases(0)
                    body(0, 0, 0, True)
                    with pe.Fori(1, TILES // 4) as pair:
                        body(pair, 0, 2 * pair, False)
                    with pe.Fori(TILES // 4, TILES // 2) as pair:
                        body(pair, 1, 2 * pair - TILES // 2, False)
                    for g in (NG - 2, NG - 1):
                        total(TILES // 2 - 1, 1, g)
                    biases(1).then_inc(finished, 1)

                @block.scalar
                def _(act):
                    with act.Fori(0, TILES // 2) as pair:
                        for r in range(2):
                            for g in range(NG):
                                k = (2 * pair + r) * NG + g
                                act.wait_ge(hidden_full, k + 1)
                                act.wait_ge(own_done, k + 1)
                                nc.scalar.activation(active[:, g % 2, :], h_ps[:, g % 2, :], act_fn,
                                                     bias=w1[:, r, P:P + 1]).then_inc(active_done, 1)
                    act.wait_ge(finished, 1)
                    for g in range(NG):
                        nc.scalar.copy(outT[:, g * W:(g + 1) * W], acc[:, g, :])

                @block.vector
                def _(dve):
                    dve.sem_inc(active_done, 2)
                    dve.sem_inc(own_done, 2)
                    dve.sem_inc(summed, 4)
                    with dve.Fori(0, TILES) as i:
                        for g in range(NG):
                            k = i * NG + g
                            dve.wait_ge(active_done, k + 3)
                            dve.wait_ge(ones_full, k + 1)
                            dve.wait_ge(summed, k + 1)
                            nc.vector.tensor_tensor(own[:, g, :], active[:, g % 2, :], m_ps[:, g % 2, :],
                                                    ALU.mult).then_inc(own_done, 1)


def single_attention(nc, name, xn, yT, qT, kT, vT, consts):
    SCALE = D ** -0.5
    with Scope(nc, name) as m:
        v_tok = m.sb("v_tok", [P, NT, D])
        q_now = m.sb("q_now", [P, B, P])
        probs = m.sb("probs", [P, 2, S])
        probsT = m.sb("probsT", [P, TB, P])
        top = m.sb("top", [P, 2, 4])
        s_ps = m.ps("s_ps", [P, B, S])
        t_ps = m.ps("t_ps", [P, TB * P])
        o_ps = m.ps("o_ps", [P, W])
        v_turned = m.sem("v_turned")
        v_copied = m.sem("v_copied")
        q_in = m.sem("q_in")
        scores_full = m.sem("scores_full")
        top_ready = m.sem("top_ready")
        probs_ready = m.sem("probs_ready")
        turned = m.sem("turned")
        copied = m.sem("copied")
        out_full = m.sem("out_full")
        out_free = m.sem("out_free")
        ident = consts["ident_sb"]
        with nc.Block() as block:
            @block.gpsimd
            def _(pool):
                with pool.Fori(0, TB) as t:
                    for b in range(B):
                        pool.wait_ge(probs_ready, 2 * t + 1 + b)
                        nc.gpsimd.tensor_copy(q_now[:, b, :], qT[:, bass.ds(b * S + t * P, P)])
                        pool.drain()
                        pool.sem_inc(q_in, 1)

            @block.tensor
            def _(pe):
                for b in range(B):
                    for t in range(TB):
                        mm = nc.tensor.transpose(s_ps[:, b, t * P:(t + 1) * P],
                                                 vT[:, b * S + t * P:b * S + (t + 1) * P], ident[:])
                    mm.then_inc(v_turned, 1)
                pe.wait_ge(v_copied, 2)
                with pe.Fori(0, TB) as t:
                    for b in range(B):
                        n = 2 * t + b
                        pe.wait_ge(q_in, n + 1)
                        pe.wait_ge(probs_ready, n + 1)
                        for c in range(2):
                            mm = nc.tensor.matmul(s_ps[:, b, c * W:(c + 1) * W], q_now[:, b, :],
                                                  kT[:, b * S + c * W:b * S + (c + 1) * W], start=True, stop=True)
                        mm.then_inc(scores_full, 1)
                    for b in range(B):
                        n = 2 * t + b
                        pe.wait_ge(probs_ready, n + 3)
                        pe.wait_ge(copied, n + 1)
                        for c in range(TB):
                            mm = nc.tensor.transpose(t_ps[:, c * P:(c + 1) * P], probs[:, b, c * P:(c + 1) * P],
                                                     ident[:])
                        mm.then_inc(turned, 1)
                        pe.wait_ge(copied, n + 2)
                        pe.wait_ge(out_free, n + 1)
                        for c in range(TB):
                            mm = nc.tensor.matmul(o_ps[:, 0:D], probsT[:, c, :], v_tok[:, b * TB + c, :],
                                                  start=(c == 0), stop=(c == TB - 1))
                        mm.then_inc(out_full, 1)
                pe.wait_ge(out_free, 2 * TB + 1)
                for g in range(NG):
                    for c in range(4):
                        t = 4 * g + c
                        mm = nc.tensor.transpose(s_ps[:, g // 2, g % 2 * W + c * P:g % 2 * W + (c + 1) * P],
                                                 xn[:, t, :], ident[:])
                    mm.then_inc(v_turned, 1)

            @block.scalar
            def _(act):
                for b in range(B):
                    act.wait_ge(v_turned, b + 1)
                    nc.scalar.copy(v_tok[:, b * TB:(b + 1) * TB, :].rearrange("p t n -> p (t n)"),
                                   s_ps[:, b, :]).then_inc(v_copied, 1)
                with act.Fori(0, TB) as t:
                    for b in range(B):
                        n = 2 * t + b
                        act.wait_ge(top_ready, n + 1)
                        nc.scalar.activation(probs[:, b, :], s_ps[:, b, :], ACT.Exp, bias=top[:, b, 1:2],
                                             scale=SCALE, accum_out=top[:, b, 2:3]).then_inc(probs_ready, 1)
                    for b in range(B):
                        n = 2 * t + b
                        act.wait_ge(turned, n + 1)
                        act.wait_ge(out_full, n + 1)
                        nc.scalar.copy(probsT[:].rearrange("p c n -> p (c n)"), t_ps[:]).then_inc(copied, 1)
                for g in range(NG):
                    act.wait_ge(v_turned, B + g + 1)
                    nc.scalar.copy(yT[:, g * W:(g + 1) * W], s_ps[:, g // 2, g % 2 * W:(g % 2 + 1) * W])

            @block.vector
            def _(dve):
                dve.sem_inc(probs_ready, 2)
                dve.sem_inc(copied, 1)
                dve.sem_inc(out_full, 1)
                dve.sem_inc(out_free, 1)
                with dve.Fori(0, TB) as t:
                    for b in range(B):
                        n = 2 * t + b
                        dve.wait_ge(scores_full, n + 1)
                        nc.vector.tensor_reduce(top[:, b, 0:1], s_ps[:, b, :], AX_X, ALU.max)
                        dve.drain()
                        nc.vector.tensor_scalar(top[:, b, 1:2], top[:, b, 0:1], -SCALE, None,
                                                ALU.mult).then_inc(top_ready, 1)
                    for b in range(B):
                        n = 2 * t + b
                        dve.wait_ge(probs_ready, n + 3)
                        nc.vector.reciprocal(top[:, b, 3:4], top[:, b, 2:3])
                        dve.drain()
                        dve.wait_ge(out_full, n + 2)
                        tile = xn[:, bass.ds(b * TB + t, 1), :].rearrange("p a n -> p (a n)")
                        nc.vector.scalar_tensor_tensor(tile, o_ps[:, 0:D], top[:, b, 3:4], tile,
                                                       ALU.mult, ALU.add).then_inc(out_free, 1)


def add_transposed(nc, name, x, xn, fT, consts):
    with Scope(nc, name) as m:
        t_ps = m.ps("t_ps", [P, NG, W])
        turned = m.sem("turned")
        with nc.Block() as block:
            @block.tensor
            def _(pe):
                for g in range(NG):
                    for c in range(4):
                        t = 4 * g + c
                        mm = nc.tensor.transpose(t_ps[:, g, c * P:(c + 1) * P], fT[:, t * P:(t + 1) * P],
                                                 consts["ident_sb"][:])
                    mm.then_inc(turned, 1)

            @block.vector
            def _(dve):
                nc.vector.tensor_tensor(x[:], x[:], xn[:], ALU.add)
                dve.drain()
                for g in range(NG):
                    dve.wait_ge(turned, g + 1)
                    xg = x[:, 4 * g:4 * g + 4, :].rearrange("p t n -> p (t n)")
                    nc.vector.tensor_tensor(xg, t_ps[:, g, :], xg, ALU.add)


def constants():
    bf = mybir.dt.np(BF16)
    ident = np.eye(P, dtype=np.float32)
    k, q = np.indices((P, P))
    spread_den = np.zeros((P, P), np.float32)
    for j in range(4):
        spread_den[32 * j + 8, 32 * j:32 * j + 32] = 1.0
    spread_expert = np.zeros((64, 16, P), np.float32)
    for e in range(64):
        spread_expert[e, e // 4, 32 * (e % 4):32 * (e % 4) + 32] = 1.0
    pick = np.zeros((P, 16, P), np.float32)
    for leaf in range(P):
        pick[leaf, leaf // 8, 16 * (leaf % 8):16 * (leaf % 8) + 16] = 1.0
    ranks = np.arange(B * S // 2, dtype=np.float32)
    return {
        "ident": ident,
        "ident_bf": ident.astype(bf),
        "mask_q": np.where(q > k, NEG, 0.0).astype(bf),
        "mask_k": np.where(k > q, NEG, 0.0).astype(bf),
        "spread_den": spread_den,
        "pick": pick.astype(bf),
        "spread_expert": spread_expert,
        "rank_row": np.concatenate([np.tile(ranks, (64, 1)), np.tile(ranks + B * S // 2, (64, 1))]),
        "lower": np.tril(np.ones((8, 8), np.float32), -1),
    }


def pad_heads(wo):
    out = np.zeros((4, P, D), np.float32)
    for h in range(HEADS):
        out[h // 4, 32 * (h % 4):32 * (h % 4) + 8, :] = wo[8 * h:8 * h + 8, :]
    return out


def twice(w):
    return np.ascontiguousarray(np.concatenate([w, w], axis=2))


def with_denominator(wo):
    out = np.zeros((65, HEADS, D + 1), np.float32)
    out[:64, :, :D] = wo.transpose(1, 0, 2)
    out[64, :, D] = 1.0
    return out


def hidden_tiles(w):
    return np.ascontiguousarray(np.pad(w, ((0, 0), (0, 0), (0, 1))))


def program(nc, a, out, stages=range(8)):
    Scope.SPENT = []
    with Scope(nc, "all") as m:
        x = m.sb("x", [P, NT, D])
        ident = m.sb("ident", [P, P])
        x_in = m.sem("x_in")
        x_out = m.sem("x_out")
        consts = dict(a, ident_sb=ident)
        with nc.Block() as block:
            @block.sync
            def _(sp):
                sp.dma_start(x[:], a["x"].rearrange("b (t p) d -> p (b t) d", p=P)).then_inc(x_in, 16)
                sp.dma_start(ident[:], a["ident"]).then_inc(x_in, 16)
                sp.wait_ge(x_in, 32)
        xT_h = m.sb("xT", [P, B * S])
        xn = m.sb("xn", [P, NT, D])
        if 0 in stages:
            layer_norm(nc, "n0", x, xn, ident, xT_h)
            narrow_attention(nc, "a0", x, xT_h, None,
                             [a[k] for k in ("a0_wq", "a0_wk", "a0_wv", "a0_bq", "a0_bk", "a0_bv", "a0_wo", "a0_bo")],
                             consts, causal=True)
        if 1 in stages:
            recycle(nc)
            layer_norm(nc, "n1", x, xn, ident, xT_h)
            routed_experts(nc, "f1", x, xT_h, {k: a["f1_" + k] for k in
                           ("wr", "br", "wup", "wgate", "wdown", "bdown", "bias")}, consts)
        if 2 in stages:
            recycle(nc)
            layer_norm(nc, "n2", x, xn, ident)
            z = xn
            with Scope(nc, "s2") as t:
                ln = t.sb("ln", [P, 2])
                zz = t.sb("zz", [P, NT, D])
                ln_in = t.sem("ln_in")
                with nc.Block() as block:
                    @block.sync
                    def _(sp):
                        sp.dma_start(ln[:, 0:1], a["a2_ln_w"].rearrange("(p a) -> p a", a=1)).then_inc(ln_in, 16)
                        sp.dma_start(ln[:, 1:2], a["a2_ln_b"].rearrange("(p a) -> p a", a=1)).then_inc(ln_in, 16)
                        sp.wait_ge(ln_in, 32)
                layer_norm(nc, "n2b", z, zz, ident, xT_h, affine=ln)
            narrow_attention(nc, "a2", x, xT_h, z,
                             [a[k] for k in ("a2_wq", "a2_wk", "a2_wv", "a2_bq", "a2_bk", "a2_bv", "a2_wo", "a2_bo")],
                             consts, causal=False)
        if 3 in stages:
            recycle(nc)
            layer_norm(nc, "n3", x, xn, ident)
            layer_norm(nc, "n3b", xn, xn, ident, xT_h, root_of_deviation=True)
            with Scope(nc, "s3") as t:
                heads = [t.sb(f"{k}T", [P, B * S]) for k in "qkv"]
                for k, dst in zip("qkv", heads):
                    leaf_layers(nc, "f3" + k, xT_h, dst, {n: a[f"f3_{k}_{n}"] for n in ("nw", "nb", "w1", "w2", "b2")},
                                ACT.Relu, consts)
                single_attention(nc, "a3", xn, xT_h, *heads, consts)
                leaf_layers(nc, "f3f", xT_h, heads[0], {n: a[f"f3_f_{n}"] for n in ("nw", "nb", "w1", "w2", "b2")},
                            ACT.Gelu, consts)
                add_transposed(nc, "f3a", x, xn, heads[0], consts)
        if 4 in stages:
            recycle(nc)
            layer_norm(nc, "n4", x, xn, ident, xT_h)
            wide_attention(nc, "a4", x, xT_h, [a[k] for k in ("a4_wq", "a4_wk", "a4_wv", "a4_wo", "a4_bo")],
                           consts, shared_keys=False)
        if 5 in stages:
            recycle(nc)
            layer_norm(nc, "n5", x, xn, ident, xT_h)
            top2_experts(nc, "f5", x, xT_h, a["f5_wg"], a["f5_w1"], a["f5_w2"], a["f5_w3"], a["lower"])
        if 6 in stages:
            recycle(nc)
            layer_norm(nc, "n6", x, xn, ident, xT_h)
            wide_attention(nc, "a6", x, xT_h, [a[k] for k in ("a6_wq", "a6_wk", "a6_wv", "a6_wo", "a6_bo")],
                           consts, shared_keys=True)
        if 7 in stages:
            recycle(nc)
            layer_norm(nc, "n7", x, xn, ident, xT_h)
            binary_linear(nc, "f7", x, xT_h, a["f7_w"], a["f7_scale"], a["f7_bias"])
        with nc.Block() as block:
            @block.sync
            def _(sp):
                sp.dma_start(out.rearrange("b (t p) d -> p (b t) d", p=P), x[:]).then_inc(x_out, 16)
                sp.wait_ge(x_out, 16)


def layout(i):
    c = np.ascontiguousarray
    i = {k: np.asarray(v) for k, v in i.items()}
    a = {"x": i["L0_attn_x"]}
    kv = i["L0_attn_Wkv"]
    a.update(a0_wq=i["L0_attn_Wq"], a0_wk=c(kv[:, :D]), a0_wv=c(kv[:, D:]), a0_bq=i["L0_attn_bq"],
             a0_bk=c(i["L0_attn_bkv"][:D]), a0_bv=c(i["L0_attn_bkv"][D:]), a0_wo=pad_heads(i["L0_attn_Wo"]),
             a0_bo=i["L0_attn_bo"])
    w, wb = i["L1_attn_W_qkv"], i["L1_attn_b_qkv"]
    a.update(a2_ln_w=i["L1_attn_ln_w"], a2_ln_b=i["L1_attn_ln_b"],
             a2_wq=c(w[:, :D]), a2_wk=c(w[:, D:2 * D]), a2_wv=c(w[:, 2 * D:]),
             a2_bq=c(wb[:D]), a2_bk=c(wb[D:2 * D]), a2_bv=c(wb[2 * D:]),
             a2_wo=pad_heads(i["L1_attn_W_proj"]), a2_bo=i["L1_attn_b_proj"])
    wkv = i["L2_attn_Wkv"]
    a.update(a4_wq=twice(i["L2_attn_Wq"].reshape(D, HEADS, 64)), a4_wk=twice(wkv[:, :1024].reshape(D, HEADS, 64)),
             a4_wv=c(wkv[:, 1024:].reshape(D, HEADS, 64)),
             a4_wo=with_denominator(i["L2_attn_Wo"].reshape(HEADS, 64, D)), a4_bo=i["L2_attn_bo"])
    a.update(a6_wq=twice(i["L3_attn_query_proj"].transpose(2, 0, 1)),
             a6_wk=twice(i["L3_attn_key_proj"].reshape(D, 1, 64)), a6_wv=c(i["L3_attn_value_proj"].reshape(D, 1, 64)),
             a6_wo=with_denominator(i["L3_attn_output_proj"].transpose(1, 2, 0)), a6_bo=np.zeros(D, np.float32))
    up, gate = i["L0_ffn_Wup"], i["L0_ffn_Wgate"]
    a.update(f1_wr=i["L0_ffn_Wr"], f1_br=i["L0_ffn_br"], f1_wup=c(up.transpose(1, 0, 2).reshape(D, 2048)),
             f1_wgate=c(gate.transpose(1, 0, 2).reshape(D, 2048)),
             f1_wdown=c(i["L0_ffn_Wdown"].reshape(16, P, D).transpose(1, 0, 2)), f1_bdown=i["L0_ffn_bdown"],
             f1_bias=c(np.stack([i["L0_ffn_bup"].reshape(16, P).T, i["L0_ffn_bgate"].reshape(16, P).T], axis=1)))
    a.update(f5_wg=c(i["L2_ffn_Wg"].T), f5_w1=hidden_tiles(i["L2_ffn_W1"].transpose(0, 2, 1)),
             f5_w2=hidden_tiles(i["L2_ffn_W2"].transpose(0, 2, 1)),
             f5_w3=c(hidden_tiles(i["L2_ffn_W3"]).transpose(0, 2, 1).reshape(8, 3, 114, D).transpose(0, 2, 1, 3)))
    a.update(f7_w=c(i["L3_ffn_weights"].T), f7_scale=i["L3_ffn_scale"], f7_bias=i["L3_ffn_bias"])
    for k in "qkvf":
        nw, w1, w2 = i[f"L1_ffn_{k}_nw"], i[f"L1_ffn_{k}_w1"], i[f"L1_ffn_{k}_w2"]
        a.update({
            f"f3_{k}_nw": c(np.pad(nw.T, ((0, 0), (0, 1)))), f"f3_{k}_nb": c(np.pad(i[f"L1_ffn_{k}_nb"], (0, 1))),
            f"f3_{k}_w1": np.concatenate([w1.reshape(32, 8, D, 16).transpose(0, 2, 1, 3).reshape(32, D, P),
                                          i[f"L1_ffn_{k}_b1"].reshape(32, P, 1)], axis=2),
            f"f3_{k}_w2": c(w2.reshape(32, P, D)),
            f"f3_{k}_b2": c(i[f"L1_ffn_{k}_b2"].reshape(2, P, D).transpose(1, 0, 2)),
        })
    a.update(constants())
    return a


def kernel(**inputs):
    import concourse.bacc as bacc
    from concourse.bass_utils import run_bass_kernel_spmd

    nc = bacc.Bacc("TRN2", target_bir_lowering=False, num_devices=1)
    arrays = {f"in_{k}": np.ascontiguousarray(v) for k, v in layout(inputs).items()}
    args = {k[3:]: nc.dram_tensor(k, v.shape, mybir.dt.from_np(v.dtype), kind="ExternalInput").ap()
            for k, v in arrays.items()}
    out = nc.dram_tensor("out_x", (B, S, D), F32, kind="ExternalOutput").ap()
    program(nc, args, out)
    r = run_bass_kernel_spmd(nc, [arrays], core_ids=[0])
    return r.results[0]["out_x"]
```

```python
from contextlib import ExitStack

import numpy as np
import concourse.bass as bass
from concourse import mybir
from concourse.alu_op_type import AluOpType as ALU

ACT = mybir.ActivationFunctionType
F32 = mybir.dt.float32
BF16 = mybir.dt.bfloat16
AX_X = mybir.AxisListType.X

P = 128
B, S, D = 2, 1024, 128
NT = B * S // P
TB = S // P
W = 512
NG = B * S // W
HEADS = 16
NEG = -1e30


class Scope:

    SPENT = []

    def __init__(self, nc, name):
        self.nc, self.name, self.ctx, self.sems = nc, name, ExitStack(), []

    def __enter__(self):
        return self

    def __exit__(self, *e):
        Scope.SPENT += self.sems
        return self.ctx.__exit__(*e)

    def sb(self, name, shape, dt=F32):
        return self.ctx.enter_context(self.nc.sbuf_tensor(f"{self.name}_{name}", shape, dt))

    def ps(self, name, shape, dt=F32):
        return self.ctx.enter_context(self.nc.psum_tensor(f"{self.name}_{name}", shape, dt))

    def sem(self, name):
        self.sems.append(self.nc.alloc_semaphore(f"{self.name}_{name}"))
        return self.sems[-1]


def recycle(nc):
    nc.clear_and_free_semaphores(Scope.SPENT)
    Scope.SPENT = []
    nc.all_engine_barrier()


def layer_norm(nc, name, src, dst, ident, xT=None, affine=None, root_of_deviation=False, eps=1e-5):
    with Scope(nc, name) as m:
        stats = m.sb("stats", [P, NT, 6])
        moments = m.sb("moments", [P, NT, 2])
        power = m.sb("power", [P, 2, NT])
        spread = m.sb("spread", [P, NT])
        turned = m.ps("turned", [P, NG, W])
        moments_ready = m.sem("moments_ready")
        rstd_ready = m.sem("rstd_ready")
        tile_normed = m.sem("tile_normed")
        group_turned = m.sem("group_turned")

        with nc.Block() as block:
            @block.vector
            def _(dve):
                for t in range(NT):
                    nc.vector.bn_stats(stats[:, t, :], src[:, t, :])
                dve.drain()
                for t in range(NT):
                    last = nc.vector.bn_aggr(moments[:, t, :], stats[:, t, :])
                last.then_inc(moments_ready, 1)
                dve.wait_ge(rstd_ready, 1)
                for t in range(NT):
                    nc.vector.tensor_scalar(dst[:, t, :], src[:, t, :], moments[:, t, 0:1], spread[:, t:t + 1],
                                            ALU.subtract, ALU.mult).then_inc(tile_normed, 1)

            @block.gpsimd
            def _(pool):
                nc.gpsimd.memset(power[:, 0, :], -0.5)
                nc.gpsimd.memset(power[:, 1, :], 0.5)
                pool.wait_ge(moments_ready, 1)
                if root_of_deviation:
                    nc.gpsimd.tensor_scalar(spread[:], moments[:, :, 1], D / (D - 1.0), None, ALU.mult)
                    pool.drain()
                    nc.gpsimd.tensor_tensor(spread[:], spread[:], power[:, 1, :], ALU.pow)
                    pool.drain()
                    nc.gpsimd.tensor_scalar(spread[:], spread[:], eps, None, ALU.add)
                else:
                    nc.gpsimd.tensor_scalar(spread[:], moments[:, :, 1], eps, None, ALU.add)
                pool.drain()
                nc.gpsimd.tensor_tensor(spread[:], spread[:], power[:, 0, :], ALU.pow).then_inc(rstd_ready, 1)

            if xT is not None:
                @block.tensor
                def _(pe):
                    for g in range(NG):
                        pe.wait_ge(tile_normed, 4 * g + 4)
                        for c in range(4):
                            last = nc.tensor.transpose(turned[:, g, c * P:(c + 1) * P], dst[:, 4 * g + c, :], ident[:])
                        last.then_inc(group_turned, 1)

                @block.scalar
                def _(act):
                    for g in range(NG):
                        act.wait_ge(group_turned, g + 1)
                        to, frm = xT[:, g * W:(g + 1) * W], turned[:, g, :]
                        if affine is None:
                            nc.scalar.copy(to, frm)
                        else:
                            nc.scalar.activation(to, frm, ACT.Identity, bias=affine[:, 1:2], scale=affine[:, 0:1])


def narrow_attention(nc, name, x, xT, residual, weights, consts, causal):
    DH, HG = 8, 4
    G = HEADS // HG
    ROWS, STACK = 9 * DH, 96
    SCALE = DH ** -0.5
    wq, wk, wv, bq, bk, bv, wo, bo = weights
    q_dram = nc.dram_tensor(f"{name}_q_parts", [P, 3, B * S], BF16, kind="Internal").ap()
    k_dram = nc.dram_tensor(f"{name}_k_parts", [P, 3, B * S], BF16, kind="Internal").ap()
    with Scope(nc, name) as outer:
        v_tok = outer.sb("v_tok", [P, NT, P])
        wo_sb = outer.sb("wo_sb", [P, P])
        attended = outer.sb("attended", [P, NT, P])

        with Scope(nc, name + "p") as m:
            w_sb = m.sb("w_sb", [P, 3, P])
            b_col = m.sb("b_col", [P, 2])
            b_row = m.sb("b_row", [P, 2, P])
            full = m.sb("full", [P, 2, B * S])
            rest = m.sb("rest", [P, B * S])
            parts = m.sb("parts", [P, 2, 3, B * S], BF16)
            qk_ps = m.ps("qk_ps", [P, 4, W])
            v_ps = m.ps("v_ps", [P, NG, W])
            loaded = m.sem("loaded")
            qk_made = m.sem("qk_made")
            qk_moved = m.sem("qk_moved")
            v_made = m.sem("v_made")
            parts_ready = m.sem("parts_ready")
            stored = m.sem("stored")
            with nc.Block() as block:
                @block.sync
                def _(sp):
                    for n, w in enumerate((wq, wk, wv)):
                        sp.dma_start(w_sb[:, n, :], w).then_inc(loaded, 16)
                    for n, b in enumerate((bq, bk)):
                        sp.dma_start(b_col[:, n:n + 1], b.rearrange("(p a) -> p a", a=1)).then_inc(loaded, 16)
                    for n, b in enumerate((bv, bo)):
                        sp.dma_start(b_row[:, n, :], b.partition_broadcast(P)).then_inc(loaded, 16)
                    sp.dma_start(wo_sb[:], wo).then_inc(loaded, 16)
                    sp.wait_ge(loaded, 16 * 8)
                    for n, dram in enumerate((q_dram, k_dram)):
                        sp.wait_ge(parts_ready, n + 1)
                        sp.dma_start(dram, parts[:, n, :, :]).then_inc(stored, 16)
                    sp.wait_ge(stored, 32)

                @block.tensor
                def _(pe):
                    pe.wait_ge(loaded, 16 * 8)
                    for n in range(2):
                        for g in range(NG):
                            if n:
                                pe.wait_ge(qk_moved, g + 1)
                            nc.tensor.matmul(qk_ps[:, g, :], w_sb[:, n, :], xT[:, g * W:(g + 1) * W],
                                             start=True, stop=True).then_inc(qk_made, 1)
                    for t in range(NT):
                        nc.tensor.matmul(v_ps[:, t // 4, t % 4 * P:(t % 4 + 1) * P], xT[:, t * P:(t + 1) * P],
                                         w_sb[:, 2, :], start=True, stop=True).then_inc(v_made, 1)

                @block.scalar
                def _(act):
                    act.wait_ge(loaded, 16 * 8)
                    for n in range(2):
                        for g in range(NG):
                            act.wait_ge(qk_made, NG * n + g + 1)
                            nc.scalar.activation(full[:, n, g * W:(g + 1) * W], qk_ps[:, g, :], ACT.Identity,
                                                 bias=b_col[:, n:n + 1]).then_inc(qk_moved, 1)

                @block.vector
                def _(dve):
                    dve.wait_ge(loaded, 16 * 8)
                    wide_bo = b_row[:, 1:2, :].to_broadcast([P, NT, P])
                    nc.vector.tensor_tensor(x[:], x[:], wide_bo, ALU.add)
                    if residual is not None:
                        dve.drain()
                        nc.vector.tensor_tensor(x[:], x[:], residual[:], ALU.add)
                    for n in range(2):
                        dve.wait_ge(qk_moved, NG * (n + 1))
                        high, mid, low = (parts[:, n, c, :] for c in range(3))
                        nc.vector.tensor_copy(high, full[:, n, :])
                        dve.drain()
                        nc.vector.tensor_tensor(rest[:], full[:, n, :], high, ALU.subtract)
                        dve.drain()
                        nc.vector.tensor_copy(mid, rest[:])
                        dve.drain()
                        nc.vector.tensor_tensor(low, rest[:], mid, ALU.subtract).then_inc(parts_ready, 1)
                        dve.drain()
                    for g in range(NG):
                        dve.wait_ge(v_made, 4 * g + 4)
                        nc.vector.tensor_tensor(v_tok[:, 4 * g:4 * g + 4, :],
                                                v_ps[:, g, :].rearrange("p (t n) -> p t n", n=P),
                                                b_row[:, 0:1, :].to_broadcast([P, 4, P]), ALU.add)

        NQ = S // W
        steps = [(Q, k) for Q in range(NQ) for k in range(4 * Q + 4 if causal else TB)]
        NS = len(steps)
        chunks = [(j, qt, c) for j in range(HG) for qt in range(TB) for c in range(2)
                  if not causal or c * W < (qt + 1) * P]
        NCH = len(chunks)
        n_steps = NS - 3
        share = -(-NCH // n_steps)
        R = 4
        with Scope(nc, name + "m") as m:
            qs = [m.sb(f"qs{r}", [STACK, HG, S], BF16) for r in range(R)]
            ks = [m.sb(f"ks{r}", [STACK, HG, S], BF16) for r in range(R)]
            vb = [m.sb(f"vb{b}", [P, TB, HG, 32]) for b in range(B)]
            plain = m.sb("plain", [3, 2, HG * S], BF16)
            mask = m.sb("mask", [P, 3, P], BF16)
            probs = m.sb("probs", [P, 2, HG, W])
            part_max = m.sb("part_max", [P, 2, HG * TB])
            neg_max = m.sb("neg_max", [P, HG * TB])
            shift = m.sb("shift", [HG * TB, 2, P])
            shift_parts = m.sb("shift_parts", [HG * TB, 3, P], BF16)
            sums = m.sb("sums", [P, W])
            recip = m.sb("recip", [P, 4, HG])
            s_ps = m.ps("s_ps", [P, HG, W])
            m_ps = m.ps("m_ps", [P, 2, W])
            o_ps = m.ps("o_ps", [P, W])
            misc = m.ps("misc", [P, W])
            stacks_cleared = m.sem("stacks_cleared")
            constants_in = m.sem("constants_in")
            stacks_in = [m.sem(f"stacks_in{r}") for r in range(R)]
            shift_in = m.sem("shift_in")
            v_in = m.sem("v_in")
            scores_ready = m.sem("scores_ready")
            probs_ready = m.sem("probs_ready")
            probs_free = m.sem("probs_free")
            max_full = m.sem("max_full")
            max_free = m.sem("max_free")
            neg_max_ready = m.sem("neg_max_ready")
            shift_ready = m.sem("shift_ready")
            out_full = m.sem("out_full")
            out_free = m.sem("out_free")
            misc_full = m.sem("misc_full")
            misc_free = m.sem("misc_free")

            def load_unit(sp, u, r, b, g):
                if not (isinstance(u, int) and u < R):
                    sp.wait_ge(probs_free, (u - R + 1) * NS + 2)
                for j in range(HG):
                    at = bass.ds(g * (HG * DH) + j * DH, DH)
                    for a in range(3):
                        src = q_dram[at, a, b * S:(b + 1) * S]
                        sp.dma_start(qs[r][3 * DH * a:3 * DH * (a + 1), j, :],
                                     src[:, None, :].to_broadcast([DH, 3, S])).then_inc(stacks_in[r], 16)
                    src = k_dram[at, :, b * S:(b + 1) * S].rearrange("d c n -> (d c) n")
                    sp.dma_start(ks[r][0:ROWS, j, :],
                                 src[None, :, :].to_broadcast([3, 3 * DH, S])).then_inc(stacks_in[r], 16)
                sp.dma_start(qs[r][ROWS:ROWS + 3, :, :].rearrange("p h n -> p (h n)"),
                             plain[:, 0, :]).then_inc(stacks_in[r], 16)

            N_LOADS = 4 * HG + 1

            def load_shift(sp, u, r):
                sp.wait_ge(shift_ready, u + 1)
                for c in range(3):
                    sp.dma_start(qs[r][ROWS + c:ROWS + c + 1, :, :].rearrange("p h n -> p (h n)"),
                                 shift_parts[:, c, :]).then_inc(shift_in, 16)

            def pe_max(pe, u, r, which):
                for i, (j, qt, c) in which:
                    pe.wait_ge(max_free, u * NCH + i + 1)
                    end = min(W, (qt + 1) * P - c * W) if causal else W
                    diagonal = causal and c * W <= qt * P < (c + 1) * W
                    mm = nc.tensor.matmul(m_ps[:, i % 2, 0:end], qs[r][:, j, qt * P:(qt + 1) * P],
                                          ks[r][:, j, c * W:c * W + end], start=True, stop=not diagonal)
                    if diagonal:
                        mm = nc.tensor.matmul(m_ps[:, i % 2, end - P:end], mask[:, 0, :], mask[:, 1, :],
                                              start=False, stop=True)
                    mm.then_inc(max_full, 1)

            def dve_max(dve, u, which):
                for i, (j, qt, c) in which:
                    dve.wait_ge(max_full, u * NCH + i + 1)
                    end = min(W, (qt + 1) * P - c * W) if causal else W
                    col = j * TB + qt
                    nc.vector.tensor_reduce(part_max[:, c, col:col + 1], m_ps[:, i % 2, 0:end], AX_X,
                                            ALU.max).then_inc(max_free, 1)

            def pe_turn_max(pe, u, use):
                pe.wait_ge(neg_max_ready, u + 1)
                pe.wait_ge(misc_free, use + 1)
                nc.tensor.transpose(misc[0:HG * TB, 0:P], neg_max[:], consts["ident_sb"][:]).then_inc(misc_full, 1)

            def dve_neg_max(dve, u):
                dve.drain()
                nc.vector.tensor_tensor(neg_max[:], part_max[:, 0, :], part_max[:, 1, :], ALU.max)
                dve.drain()
                nc.vector.tensor_scalar(neg_max[:], neg_max[:], -1.0, None, ALU.mult).then_inc(neg_max_ready, 1)

            def dve_split_shift(dve, u, use):
                dve.wait_ge(misc_full, use + 1)
                dve.wait_ge(shift_in, 48 * u + 48)
                nc.vector.tensor_copy(shift[:, 0, :], misc[0:HG * TB, 0:P]).then_inc(misc_free, 1)
                dve.drain()
                nc.vector.tensor_copy(shift_parts[:, 0, :], shift[:, 0, :])
                dve.drain()
                nc.vector.tensor_tensor(shift[:, 1, :], shift[:, 0, :], shift_parts[:, 0, :], ALU.subtract)
                dve.drain()
                nc.vector.tensor_copy(shift_parts[:, 1, :], shift[:, 1, :])
                dve.drain()
                nc.vector.tensor_tensor(shift_parts[:, 2, :], shift[:, 1, :], shift_parts[:, 1, :],
                                        ALU.subtract).then_inc(shift_ready, 1)

            def pe_scores(pe, u, r, n, j):
                Q, k = steps[n]
                lo = max(0, k - 4 * Q) * P if causal else 0
                if n:
                    pe.wait_ge(probs_ready, (u * NS + n - 1) * HG + j + 1)
                diagonal = causal and k >= 4 * Q
                mm = nc.tensor.matmul(s_ps[:, j, lo:W], ks[r][:, j, k * P:(k + 1) * P],
                                      qs[r][:, j, Q * W + lo:(Q + 1) * W], start=True, stop=not diagonal)
                if diagonal:
                    mm = nc.tensor.matmul(s_ps[:, j, lo:lo + P], mask[:, 0, :], mask[:, 2, :],
                                          start=False, stop=True)
                mm.then_inc(scores_ready, 1)

            def pe_sums(pe, u, b, n):
                Q, k = steps[n]
                lo = max(0, k - 4 * Q) * P if causal else 0
                last_k = n + 1 == NS or steps[n + 1][0] != Q
                if k == 0:
                    pe.wait_ge(out_free, u * NQ + Q + 1)
                for j in range(HG):
                    pe.wait_ge(probs_ready, (u * NS + n) * HG + j + 1)
                    mm = nc.tensor.matmul(o_ps[32 * j:32 * j + 32, lo:W], vb[b][:, k, j, :], probs[:, n % 2, j, lo:W],
                                          start=(k == 0), stop=last_k)
                mm.then_inc(probs_free, 1)

            def dve_evacuate(dve, u, Q):
                dve.wait_ge(probs_free, u * NS + q_end[Q] + 1 + 2)
                nc.vector.tensor_copy(sums[:], o_ps[:]).then_inc(out_free, 1)

            def pe_turn_sums(pe, u, Q, use):
                pe.wait_ge(out_free, u * NQ + Q + 2)
                pe.wait_ge(misc_free, use + 1)
                for c in range(4):
                    mm = nc.tensor.transpose(misc[:, c * P:(c + 1) * P], sums[:, c * P:(c + 1) * P],
                                             consts["ident_sb"][:])
                mm.then_inc(misc_full, 1)

            def dve_normalize(dve, b, g, Q, use):
                dve.wait_ge(misc_full, use + 1)
                by_head = misc[:].rearrange("p (t j n) -> p t j n", t=4, j=HG)
                nc.vector.reciprocal(recip[:], by_head[:, :, :, DH])
                dve.drain()
                at = attended[:, b * TB + 4 * Q:b * TB + 4 * Q + 4, :]
                at = at[:, :, g * HG * DH:(g + 1) * HG * DH] if isinstance(g, int) else \
                    at[:, :, bass.ds(g * (HG * DH), HG * DH)]
                nc.vector.tensor_tensor(at.rearrange("p t (j n) -> p t j n", j=HG), by_head[:, :, :, 0:DH],
                                        recip[:, :, :, None].to_broadcast([P, 4, HG, DH]),
                                        ALU.mult).then_inc(misc_free, 1)

            q_end = [max(n for n in range(NS) if steps[n][0] == Q) for Q in range(NQ)]
            numbered = [list(enumerate(chunks))[i * share:(i + 1) * share] for i in range(n_steps)]

            def misc_use(u, i):
                return 3 * u + i

            def all_slots(engine, slot):
                def round_of(i, last):
                    for r in range(R):
                        nxt = None if last and r == R - 1 else ((r + 1) % R, i + (r + 1) // R)
                        slot(R * i + r, r, r % B, (R // B) * i + r // B, nxt)

                with engine.Fori(0, B * G // R - 1) as i:
                    round_of(i, False)
                round_of(B * G // R - 1, True)

            with nc.Block() as block:
                @block.sync
                def _(sp):
                    sp.dma_start(mask[:, 0, :], consts["ident_bf"]).then_inc(constants_in, 16)
                    sp.dma_start(mask[:, 1, :], consts["mask_q"]).then_inc(constants_in, 16)
                    sp.dma_start(mask[:, 2, :], consts["mask_k"]).then_inc(constants_in, 16)
                    sp.wait_ge(stacks_cleared, 1)
                    load_unit(sp, 0, 0, 0, 0)
                    sp.wait_ge(stacks_cleared, R)
                    for r in range(R):
                        sp.dma_start(ks[r][ROWS:ROWS + 3, :, :].rearrange("p h n -> p (h n)"),
                                     plain[:, 1, :]).then_inc(constants_in, 16)
                    load_unit(sp, 1, 1, 1, 0)
                    load_shift(sp, 0, 0)

                    def slot(u, r, b, g, nxt):
                        if nxt and not (isinstance(u, int) and u == B * G - 2):
                            load_unit(sp, u + 2, (r + 2) % R, b, g + 1)
                        if nxt:
                            load_shift(sp, u + 1, nxt[0])

                    all_slots(sp, slot)

                @block.gpsimd
                def _(pool):
                    for b in range(B):
                        nc.gpsimd.memset(vb[b][:, :, :, DH + 1:32], 0.0)
                        nc.gpsimd.memset(vb[b][:, :, :, DH:DH + 1], 1.0)
                    pool.drain()
                    def fill(u, b, g):
                        for j in range(HG):
                            nc.gpsimd.tensor_copy(vb[b][:, :, j, 0:DH],
                                                         v_tok[:, b * TB:(b + 1) * TB,
                                                               bass.ds(g * (HG * DH) + j * DH, DH)])
                        pool.drain()
                        pool.sem_inc(v_in, 1)

                    for b in range(B):
                        fill(b, b, 0)
                    with pool.Fori(1, G) as g:
                        for b in range(B):
                            pool.wait_ge(probs_free, (2 * g + b - 1) * NS + 2)
                            fill(2 * g + b, b, g)

                @block.tensor
                def _(pe):
                    pe.sem_inc(probs_free, 2)
                    pe.wait_ge(constants_in, 16 * (R + 3))
                    pe.wait_ge(stacks_in[0], 16 * N_LOADS)
                    pe_max(pe, 0, 0, list(enumerate(chunks)))
                    pe_turn_max(pe, 0, misc_use(0, 0))

                    def slot(u, r, b, g, nxt):
                        if nxt:
                            pe.wait_ge(stacks_in[nxt[0]], 16 * N_LOADS * (nxt[1] + 1))
                            pe_max(pe, u + 1, nxt[0], numbered[0])
                        pe.wait_ge(shift_in, 48 * u + 96)
                        for j in range(HG):
                            pe_scores(pe, u, r, 0, j)
                        pe.wait_ge(v_in, u + 1)
                        for n in range(NS):
                            maxima = numbered[n + 1] if nxt and n + 1 < n_steps else []
                            for j in range(HG):
                                if n + 1 < NS:
                                    pe_scores(pe, u, r, n + 1, j)
                                pe_max(pe, u + 1, nxt and nxt[0], maxima[j:j + 1])
                            if n == 1 and not (isinstance(u, int) and u == 0):
                                pe_turn_sums(pe, u - 1, NQ - 1, misc_use(u, 0))
                            if n == q_end[0] + 2:
                                pe_turn_sums(pe, u, 0, misc_use(u, 1))
                            pe_sums(pe, u, b, n)
                            if nxt:
                                pe_max(pe, u + 1, nxt[0], maxima[HG:])
                                if n == n_steps - 1:
                                    pe_turn_max(pe, u + 1, misc_use(u, 2))

                    all_slots(pe, slot)
                    pe_turn_sums(pe, B * G - 1, NQ - 1, misc_use(B * G - 1, 2))

                @block.scalar
                def _(act):
                    def slot(u):
                        for n, (Q, k) in enumerate(steps):
                            lo = max(0, k - 4 * Q) * P if causal else 0
                            act.wait_ge(probs_free, u * NS + n + 1)
                            for j in range(HG):
                                act.wait_ge(scores_ready, (u * NS + n) * HG + j + 1)
                                nc.scalar.activation(probs[:, n % 2, j, lo:W], s_ps[:, j, lo:W], ACT.Exp,
                                                     scale=SCALE).then_inc(probs_ready, 1)

                    with act.Fori(0, B * G) as u:
                        slot(u)

                @block.vector
                def _(dve):
                    nc.vector.memset(plain[:, 0, :], 0.0)
                    nc.vector.memset(plain[:, 1, :], 1.0)
                    for r in range(R):
                        nc.vector.memset(qs[r][64:STACK, :, :], 0.0)
                        nc.vector.memset(ks[r][64:STACK, :, :], 0.0).then_inc(stacks_cleared, 1)
                    nc.vector.memset(part_max[:], NEG)
                    dve.sem_inc(max_free, 2)
                    dve.sem_inc(misc_free, 1)
                    dve.sem_inc(out_free, 1)
                    dve.sem_inc(shift_in, 48)
                    dve.drain()
                    dve_max(dve, 0, list(enumerate(chunks)))
                    dve_neg_max(dve, 0)
                    dve_split_shift(dve, 0, misc_use(0, 0))

                    def slot(u, r, b, g, nxt):
                        before = None if isinstance(u, int) and u == 0 else (1 - b, g if b else g - 1)
                        if nxt:
                            dve_max(dve, u + 1, numbered[0])
                        for n in range(NS):
                            maxima = numbered[n + 1] if nxt and n + 1 < n_steps else []
                            dve_max(dve, u + 1, maxima[0:1])
                            if n == 0 and before:
                                dve_evacuate(dve, u - 1, NQ - 1)
                            if n == q_end[0] + 1:
                                dve_evacuate(dve, u, 0)
                            dve_max(dve, u + 1, maxima[1:])
                            if n == 1 and before:
                                dve_normalize(dve, *before, NQ - 1, misc_use(u, 0))
                            if n == q_end[0] + 2:
                                dve_normalize(dve, b, g, 0, misc_use(u, 1))
                            if nxt and n == n_steps - 2:
                                dve_neg_max(dve, u + 1)
                            if nxt and n == n_steps - 1:
                                dve_split_shift(dve, u + 1, misc_use(u, 2))

                    all_slots(dve, slot)
                    dve_evacuate(dve, B * G - 1, NQ - 1)
                    dve_normalize(dve, B - 1, G - 1, NQ - 1, misc_use(B * G - 1, 2))

        with Scope(nc, name + "o") as m:
            t_ps = m.ps("t_ps", [P, 4, W])
            y_ps = m.ps("y_ps", [P, NG, W])
            turned = m.sem("turned")
            copied = m.sem("copied")
            projected = m.sem("projected")
            with nc.Block() as block:
                @block.tensor
                def _(pe):
                    for g in range(NG):
                        for c in range(4):
                            mm = nc.tensor.transpose(t_ps[:, g, c * P:(c + 1) * P], attended[:, 4 * g + c, :],
                                                     consts["ident_sb"][:])
                        mm.then_inc(turned, 1)
                    for g in range(NG):
                        pe.wait_ge(copied, g + 1)
                        for c in range(4):
                            t = 4 * g + c
                            mm = nc.tensor.matmul(y_ps[:, g, c * P:(c + 1) * P], xT[:, t * P:(t + 1) * P], wo_sb[:],
                                                  start=True, stop=True)
                        mm.then_inc(projected, 1)

                @block.scalar
                def _(act):
                    for g in range(NG):
                        act.wait_ge(turned, g + 1)
                        nc.scalar.copy(xT[:, g * W:(g + 1) * W], t_ps[:, g, :]).then_inc(copied, 1)

                @block.vector
                def _(dve):
                    for g in range(NG):
                        dve.wait_ge(projected, g + 1)
                        xg = x[:, 4 * g:4 * g + 4, :].rearrange("p t n -> p (t n)")
                        nc.vector.tensor_tensor(xg, y_ps[:, g, :], xg, ALU.add)


def wide_attention(nc, name, x, xT, weights, consts, shared_keys):
    DH = 64
    SCALE = DH ** -0.5
    wq, wk, wv, wo, bo = weights
    NH_K, NH_V = (1, 1) if shared_keys else (HEADS, HEADS // 2)
    NB = 8
    NQ = S // W
    steps = [(Q, k) for Q in range(NQ) for k in range(TB)]
    NS = len(steps)
    chunks = [(qt, c) for qt in range(TB) for c in range(2)]
    NCH = len(chunks)
    MAX_AT = 5
    TURN_AT = MAX_AT + 8
    AHEAD = 2
    OWN_AT = (TB + 2, NS - 1)
    with Scope(nc, name) as m:
        wq_all = m.sb("wq_all", [P, HEADS, P])
        wk_all = m.sb("wk_all", [P, NH_K, P])
        wv_all = m.sb("wv_all", [P, NH_V, 2 * DH])
        wo_all = m.sb("wo_all", [P, HEADS, D])
        ones = m.sb("ones", [P, P])
        w_now = m.sb("w_now", [P, 2, P])
        bo_row = m.sb("bo_row", [P, D])
        qf = [m.sb(f"qf{b}", [P, S]) for b in range(B)]
        kf = [m.sb(f"kf{b}", [P, S]) for b in range(B)]
        qm = [m.sb(f"qm{b}", [P, S], BF16) for b in range(B)]
        kh = [m.sb(f"kh{b}", [P, S], BF16) for b in range(B)]
        km = [m.sb(f"km{b}", [P, S], BF16) for b in range(B)]
        vb = [m.sb(f"vb{b}", [P, TB, 2, DH]) for b in range(B)]
        probs = m.sb("probs", [P, NB, W])
        added = m.sb("added", [P, 2, W])
        den = m.sb("den", [P, W])
        part_max = m.sb("part_max", [P, 2, TB])
        neg_max = m.sb("neg_max", [P, TB])
        shift = m.sb("shift", [TB, P])
        sums = m.sb("sums", [P, W])
        recip = m.sb("recip", [P, 2])
        s_ps = m.ps("s_ps", [P, 2, W])
        m_ps = m.ps("m_ps", [P, 2, W])
        o_ps = m.ps("o_ps", [P, W])
        p_ps = m.ps("p_ps", [P, 2, W])
        misc = m.ps("misc", [P, W])
        loaded = m.sem("loaded")
        constants_set = m.sem("constants_set")
        weights_now = m.sem("weights_now")
        proj_full = m.sem("proj_full")
        proj_free = m.sem("proj_free")
        unit_made = m.sem("unit_made")
        shift_ready = m.sem("shift_ready")
        shift_in = m.sem("shift_in")
        scores_ready = m.sem("scores_ready")
        probs_ready = m.sem("probs_ready")
        probs_free = m.sem("probs_free")
        probs_added = m.sem("probs_added")
        den_ready = m.sem("den_ready")
        max_full = m.sem("max_full")
        max_free = m.sem("max_free")
        neg_max_ready = m.sem("neg_max_ready")
        out_free = m.sem("out_free")
        misc_full = m.sem("misc_full")
        misc_free = m.sem("misc_free")

        def jobs(first, e):
            made = [("q", c) for c in range(NQ)]
            if first or not shared_keys:
                made += [("k", c) for c in range(NQ)]
            if first or (not shared_keys and e == 0):
                made += [("v", c) for c in range(2)]
            return made

        def job_index(hp, e, b, i):
            if shared_keys:
                u = 4 * hp + 2 * e + b
                return 6 * u + i if isinstance(hp, int) and u < 2 else 8 + 2 * u + i
            return 20 * hp + (0, 6, 12, 16)[2 * e + b] + i

        def misc_use(u, i):
            return 5 * u - 1 + i

        with nc.Block() as block:
            @block.sync
            def _(sp):
                for dst, src in ((wq_all, wq), (wk_all, wk), (wv_all, wv), (wo_all, wo)):
                    sp.dma_start(dst[:], src).then_inc(loaded, 16)
                sp.dma_start(bo_row[:], bo.partition_broadcast(P)).then_inc(loaded, 16)
                with sp.Fori(0, HEADS) as h:
                    for b in range(B):
                        sp.wait_ge(shift_ready, 2 * h + b + 1)
                        sp.dma_start(qf[b][DH:DH + 1, :], shift[:]).then_inc(shift_in, 16)

            @block.gpsimd
            def _(pool):
                nc.gpsimd.memset(ones[:], 1.0)
                pool.drain()
                for b in range(B):
                    nc.gpsimd.memset(qf[b][DH:P, :], 0.0)
                    pool.drain()
                    nc.gpsimd.memset(kf[b][DH:P, :], 0.0)
                    pool.drain()
                    nc.gpsimd.memset(kf[b][DH:DH + 1, :], 1.0)
                    pool.drain()
                pool.sem_inc(constants_set, 1)
                pool.wait_ge(loaded, 80)

                def fetch(h):
                    for n, w in enumerate((wq_all, wk_all)):
                        if n == 0 or not shared_keys or (isinstance(h, int) and h == 0):
                            nc.gpsimd.tensor_copy(w_now[:, n, :], w[:, h, :] if isinstance(h, int)
                                                  else w[:, bass.ds(h, 1), :].rearrange("p a n -> p (a n)"))
                    pool.drain()
                    pool.sem_inc(weights_now, 1)

                def after(hp, e):
                    pool.wait_ge(proj_full, job_index(hp, e, 0, 0))
                    fetch(2 * hp + e)

                fetch(0)
                after(0, 1)
                with pool.Fori(1, HEADS // 2) as hp:
                    after(hp, 0)
                    after(hp, 1)

            def pe_job(pe, hp, e, b, i, what, c):
                pe.wait_ge(proj_free, job_index(hp, e, b, i) + 1)
                bank = p_ps[:, i % 2, :]
                cols = slice(b * S + c * W, b * S + (c + 1) * W)
                if what in "qk":
                    nc.tensor.matmul(bank, w_now[:, "qk".index(what), :], xT[:, cols],
                                     start=True, stop=True).then_inc(proj_full, 1)
                else:
                    hv = 0 if shared_keys else hp
                    for j in range(4):
                        t = b * TB + 4 * c + j
                        rhs = wv_all[:, hv, :] if isinstance(hv, int) else \
                            wv_all[:, bass.ds(hv, 1), :].rearrange("p a n -> p (a n)")
                        mm = nc.tensor.matmul(bank[:, j * P:(j + 1) * P], xT[:, t * P:(t + 1) * P],
                                              rhs, start=True, stop=True)
                    mm.then_inc(proj_full, 1)

            def act_job(act, hp, e, b, i, what, c):
                act.wait_ge(proj_full, job_index(hp, e, b, i) + 1)
                bank = p_ps[:, i % 2, :]
                if what == "v":
                    nc.scalar.copy(vb[b][:, 4 * c:4 * c + 4, :, :].rearrange("p t e n -> p (t e n)"),
                                   bank).then_inc(unit_made, 1)
                else:
                    full = (qf if what == "q" else kf)[b]
                    high = (qm if what == "q" else kh)[b]
                    nc.scalar.copy(full[0:DH, c * W:(c + 1) * W], bank[0:DH, :])
                    nc.scalar.copy(high[:, c * W:(c + 1) * W], bank).then_inc(unit_made, 1)

            def dve_job(dve, hp, e, b, i, what, c):
                n = job_index(hp, e, b, i)
                if what == "v":
                    dve.drain()
                dve.wait_ge(unit_made, n + 1)
                bank = p_ps[:, i % 2, :]
                cols = slice(c * W, (c + 1) * W)
                if what == "q":
                    nc.vector.tensor_tensor(qm[b][DH:P, cols], bank[DH:P, :], qm[b][DH:P, cols],
                                            ALU.subtract).then_inc(proj_free, 1)
                elif what == "k":
                    nc.vector.tensor_tensor(km[b][:, cols], bank, kh[b][:, cols], ALU.subtract).then_inc(proj_free, 1)
                else:
                    dve.sem_inc(proj_free, 1)

            def pe_max(pe, u, b, which):
                for i in which:
                    qt, c = chunks[i]
                    pe.wait_ge(max_free, u * NCH + i + 1)
                    q = qm[b][:, qt * P:(qt + 1) * P]
                    nc.tensor.matmul(m_ps[:, i % 2, :], q, kh[b][:, c * W:(c + 1) * W], start=True, stop=False)
                    nc.tensor.matmul(m_ps[:, i % 2, :], q, km[b][:, c * W:(c + 1) * W],
                                     start=False, stop=True).then_inc(max_full, 1)

            def dve_max(dve, u, which):
                for i in which:
                    qt, c = chunks[i]
                    dve.wait_ge(max_full, u * NCH + i + 1)
                    nc.vector.tensor_reduce(part_max[:, c, qt:qt + 1], m_ps[:, i % 2, :], AX_X,
                                            ALU.max).then_inc(max_free, 1)

            def dve_neg_max(dve):
                dve.drain()
                nc.vector.tensor_tensor(neg_max[:], part_max[:, 0, :], part_max[:, 1, :], ALU.max)
                dve.drain()
                nc.vector.tensor_scalar(neg_max[:], neg_max[:], -1.0, None, ALU.mult).then_inc(neg_max_ready, 1)

            def pe_turn_max(pe, u, use):
                pe.wait_ge(neg_max_ready, u + 1)
                pe.wait_ge(misc_free, use + 1)
                nc.tensor.transpose(misc[0:TB, 0:P], neg_max[:], consts["ident_sb"][:]).then_inc(misc_full, 1)

            def dve_shift(dve, u, use):
                dve.wait_ge(misc_full, use + 1)
                dve.wait_ge(shift_in, 16 * u + 16)
                nc.vector.tensor_copy(shift[:], misc[0:TB, 0:P])
                dve.drain()
                dve.sem_inc(misc_free, 1)
                dve.sem_inc(shift_ready, 1)

            def pe_scores(pe, u, b, n):
                Q, k = steps[n]
                if n >= 2:
                    pe.wait_ge(probs_ready, u * NS + n - 1)
                nc.tensor.matmul(s_ps[:, n % 2, :], kf[b][:, k * P:(k + 1) * P], qf[b][:, Q * W:(Q + 1) * W],
                                 start=True, stop=True).then_inc(scores_ready, 1)

            def pe_sums(pe, u, e, b, n):
                Q, k = steps[n]
                if k == 0:
                    pe.wait_ge(out_free, u * NQ + Q + 1)
                pe.wait_ge(probs_ready, u * NS + n + 2)
                for j in range(2):
                    mm = nc.tensor.matmul(o_ps[j * DH:(j + 1) * DH, :], vb[b][:, k + j, e, :],
                                          probs[:, (n + j) % NB, :], start=(k == 0), stop=(k == TB - 2))
                mm.then_inc(probs_free, 1)

            def dve_denominator(dve, u, n):
                Q, k = steps[n]
                if k == 0:
                    return
                before = probs[:, (n - 2) % NB:(n - 2) % NB + 2, :] if k == 2 else added[:]
                dve.drain()
                dve.wait_ge(probs_ready, u * NS + n + 2)
                nc.vector.tensor_tensor(added[:], before, probs[:, n % NB:n % NB + 2, :],
                                        ALU.add).then_inc(probs_added, 2 if k == 2 else 1)

            def dve_fold(dve):
                nc.vector.tensor_tensor(den[:], added[:, 0, :], added[:, 1, :], ALU.add).then_inc(den_ready, 1)

            def dve_evacuate(dve, u, Q):
                dve.wait_ge(probs_free, u * (NS // 2) + (Q + 1) * (TB // 2) + NB // 2)
                nc.vector.tensor_copy(sums[:], o_ps[:]).then_inc(out_free, 1)

            def pe_project(pe, u, h, Q, half, use):
                pe.wait_ge(out_free, u * NQ + Q + 2)
                pe.wait_ge(den_ready, u * NQ + Q + 1)
                pe.wait_ge(misc_free, use + 1)
                rhs = wo_all[:, h, :] if isinstance(h, int) else \
                    wo_all[:, bass.ds(h, 1), :].rearrange("p a n -> p (a n)")
                for c in range(2):
                    cols = slice((2 * half + c) * P, (2 * half + c + 1) * P)
                    nc.tensor.matmul(misc[:, 2 * c * P:(2 * c + 1) * P], sums[:, cols], rhs, start=True, stop=True)
                    mm = nc.tensor.matmul(misc[:, (2 * c + 1) * P:(2 * c + 2) * P], den[:, cols], ones[:],
                                          start=True, stop=True)
                mm.then_inc(misc_full, 1)

            def dve_add(dve, b, Q, half, use):
                dve.wait_ge(misc_full, use + 1)
                for c in range(2):
                    nc.vector.reciprocal(recip[:, c:c + 1], misc[:, (2 * c + 1) * P:(2 * c + 1) * P + 1])
                dve.drain()
                for c in range(2):
                    t = b * TB + 4 * Q + 2 * half + c
                    nc.vector.scalar_tensor_tensor(x[:, t, :], misc[:, 2 * c * P:(2 * c + 1) * P],
                                                   recip[:, c:c + 1], x[:, t, :], ALU.mult, ALU.add)
                dve.drain()
                dve.sem_inc(misc_free, 1)

            at_max = {MAX_AT + n: [2 * n, 2 * n + 1] for n in range(NCH // 2)}

            def all_slots(engine, slot):
                def pair(hp, first, last):
                    slot(hp, 0, 0, (hp, 0, 1), shared_keys and first)
                    slot(hp, 0, 1, (hp, 1, 0), False)
                    slot(hp, 1, 0, (hp, 1, 1), False)
                    slot(hp, 1, 1, None if last else (hp + 1, 0, 0), False)

                pair(0, True, False)
                with engine.Fori(1, HEADS // 2 - 1) as hp:
                    pair(hp, False, False)
                pair(HEADS // 2 - 1, False, True)

            @block.tensor
            def _(pe):
                pe.wait_ge(loaded, 80)
                pe.wait_ge(constants_set, 1)
                pe.wait_ge(weights_now, 1)
                for i, (what, c) in enumerate(jobs(True, 0)):
                    pe_job(pe, 0, 0, 0, i, what, c)
                pe.wait_ge(proj_free, len(jobs(True, 0)) + 2)
                pe_max(pe, 0, 0, range(NCH))
                pe_turn_max(pe, 0, 0)

                def slot(hp, e, b, nxt, first):
                    u, h, nb = 4 * hp + 2 * e + b, 2 * hp + e, 1 - b
                    made = jobs(first, nxt[1]) if nxt else []
                    if nxt and b == 1:
                        pe.wait_ge(weights_now, h + 2)
                    for n in range(AHEAD if nxt else 0):
                        pe_job(pe, *nxt, n, *made[n])
                    pe.wait_ge(shift_in, 16 * u + 32)
                    pe_scores(pe, u, b, 0)
                    for n in range(NS):
                        if n + 1 < NS:
                            pe_scores(pe, u, b, n + 1)
                        if n + AHEAD < len(made):
                            pe_job(pe, *nxt, n + AHEAD, *made[n + AHEAD])
                        if nxt and n in at_max:
                            if n == MAX_AT:
                                pe.wait_ge(proj_free, job_index(*nxt, [w for w, _ in made].count("q")
                                                                + [w for w, _ in made].count("k") - 1) + 3)
                            pe_max(pe, u + 1, nb, at_max[n][:1])
                        if n in (2, 4) and not (isinstance(u, int) and u == 0):
                            pe_project(pe, u - 1, h if b else h - 1, NQ - 1, n // 2 - 1, misc_use(u, n // 2 - 1))
                        if n in OWN_AT:
                            half = OWN_AT.index(n)
                            pe_project(pe, u, h, 0, half, misc_use(u, 2 + 2 * half if nxt else 2 + half))
                        if nxt and n == TURN_AT:
                            pe_turn_max(pe, u + 1, misc_use(u, 3))
                        if n % 2:
                            pe_sums(pe, u, e, b, n - 1)
                        if nxt and n in at_max:
                            pe_max(pe, u + 1, nb, at_max[n][1:])

                all_slots(pe, slot)
                for half in range(2):
                    pe_project(pe, 2 * HEADS - 1, HEADS - 1, NQ - 1, half, misc_use(2 * HEADS - 1, 4 + half))

            @block.scalar
            def _(act):
                act.wait_ge(constants_set, 1)
                for i, (what, c) in enumerate(jobs(True, 0)):
                    act_job(act, 0, 0, 0, i, what, c)

                def slot(hp, e, b, nxt, first):
                    u = 4 * hp + 2 * e + b
                    made = jobs(first, nxt[1]) if nxt else []
                    for n in range(AHEAD if nxt else 0):
                        act_job(act, *nxt, n, *made[n])
                    for n in range(NS):
                        act.wait_ge(scores_ready, u * NS + n + 1)
                        if n % 2 == 0:
                            act.wait_ge(probs_free, u * (NS // 2) + n // 2 + 1)
                            act.wait_ge(probs_added, u * (NS // 2) + n // 2 + 1)
                        nc.scalar.activation(probs[:, n % NB, :], s_ps[:, n % 2, :], ACT.Exp,
                                             scale=SCALE).then_inc(probs_ready, 1)
                        if n + AHEAD < len(made):
                            act_job(act, *nxt, n + AHEAD, *made[n + AHEAD])

                all_slots(act, slot)

            @block.vector
            def _(dve):
                dve.sem_inc(proj_free, 2)
                dve.sem_inc(probs_free, NB // 2)
                dve.sem_inc(probs_added, NB // 2)
                dve.sem_inc(max_free, 2)
                dve.sem_inc(out_free, 1)
                dve.sem_inc(misc_free, 1)
                dve.sem_inc(shift_in, 16)
                dve.wait_ge(loaded, 80)
                nc.vector.tensor_tensor(x[:], x[:], bo_row[:, None, :].to_broadcast([P, NT, D]), ALU.add)
                for i, (what, c) in enumerate(jobs(True, 0)):
                    dve_job(dve, 0, 0, 0, i, what, c)
                dve_max(dve, 0, range(NCH))
                dve_neg_max(dve)
                dve_shift(dve, 0, 0)

                def slot(hp, e, b, nxt, first):
                    u = 4 * hp + 2 * e + b
                    made = jobs(first, nxt[1]) if nxt else []
                    for n in range(AHEAD if nxt else 0):
                        dve_job(dve, *nxt, n, *made[n])
                    for n in range(NS):
                        if n + AHEAD < len(made):
                            dve_job(dve, *nxt, n + AHEAD, *made[n + AHEAD])
                        if nxt and n in at_max:
                            dve_max(dve, u + 1, at_max[n][:1])
                        if n in (2, 4) and not (isinstance(u, int) and u == 0):
                            dve_add(dve, 1 - b, NQ - 1, n // 2 - 1, misc_use(u, n // 2 - 1))
                        if n in OWN_AT:
                            half = OWN_AT.index(n)
                            dve_add(dve, b, 0, half, misc_use(u, 2 + 2 * half if nxt else 2 + half))
                        if nxt and n == TURN_AT:
                            dve_shift(dve, u + 1, misc_use(u, 3))
                        if n % 2:
                            dve_denominator(dve, u, n - 1)
                        if nxt and n in at_max:
                            dve_max(dve, u + 1, at_max[n][1:])
                            if n == max(at_max):
                                dve_neg_max(dve)
                        if n % TB == TB - 1:
                            dve_evacuate(dve, u, n // TB)
                            dve.drain()
                            dve_fold(dve)

                all_slots(dve, slot)
                for half in range(2):
                    dve_add(dve, 1, NQ - 1, half, misc_use(2 * HEADS - 1, 4 + half))


def binary_linear(nc, name, x, xT, wT, scale, bias):
    TOP = 100.0
    with Scope(nc, name) as m:
        w_sb = m.sb("w_sb", [P, D])
        signs = m.sb("signs", [P, D])
        rows = m.sb("rows", [P, 2, D])
        y = m.sb("y", [P, NG, 4, D])
        y_ps = m.ps("y_ps", [P, NG, W])
        loaded = m.sem("loaded")
        signs_ready = m.sem("signs_ready")
        made = m.sem("made")
        with nc.Block() as block:
            @block.sync
            def _(sp):
                sp.dma_start(w_sb[:], wT).then_inc(loaded, 16)
                sp.dma_start(rows[:, 0, :], scale.partition_broadcast(P)).then_inc(loaded, 16)
                sp.dma_start(rows[:, 1, :], bias.partition_broadcast(P)).then_inc(loaded, 16)

            @block.tensor
            def _(pe):
                pe.wait_ge(signs_ready, 1)
                for g in range(NG):
                    for c in range(4):
                        t = 4 * g + c
                        mm = nc.tensor.matmul(y_ps[:, g, c * P:(c + 1) * P], xT[:, t * P:(t + 1) * P], signs[:],
                                              start=True, stop=True)
                    mm.then_inc(made, 1)

            @block.vector
            def _(dve):
                dve.wait_ge(loaded, 48)
                nc.vector.tensor_scalar(signs[:], w_sb[:], 0.0, 2.0, ALU.is_ge, ALU.mult)
                dve.drain()
                nc.vector.tensor_scalar(signs[:], signs[:], -1.0, None, ALU.add).then_inc(signs_ready, 1)
                for g in range(NG):
                    dve.wait_ge(made, g + 1)
                    yg = y[:, g, :, :]
                    nc.vector.tensor_tensor(yg, y_ps[:, g, :].rearrange("p (t n) -> p t n", n=D),
                                            rows[:, 0:1, :].to_broadcast([P, 4, D]), ALU.mult)
                    dve.drain()
                    nc.vector.tensor_tensor(yg, yg, rows[:, 1:2, :].to_broadcast([P, 4, D]), ALU.add)
                    dve.drain()
                    nc.vector.tensor_scalar(yg, yg, TOP, -TOP, ALU.min, ALU.max)
                    dve.drain()
                    xg = x[:, 4 * g:4 * g + 4, :]
                    nc.vector.tensor_tensor(xg, xg, yg, ALU.add)


def top2_experts(nc, name, x, xT, wg, w1, w2, w3, lower):
    E, HT, HP = 8, 3, 114
    with Scope(nc, name) as m:
        wg_sb = m.sb("wg_sb", [P, E])
        lower_sb = m.sb("lower_sb", [P, E, E])
        logits = m.sb("logits", [P, NT, E])
        gating = m.sb("gating", [P, NT, E])
        gate_now = m.sb("gate_now", [P, 2, NT])
        above = m.sb("above", [P, NT, E, E])
        ties = m.sb("ties", [P, NT, E, E])
        rank = m.sb("rank", [P, NT, E])
        stat = m.sb("stat", [P, NT])
        w12 = m.sb("w12", [P, 2, 2, HT * HP])
        w3_sb = m.sb("w3_sb", [HP, 2, HT, D])
        silu = m.sb("silu", [HP, 2, W])
        hidden = m.sb("hidden", [HP, 2, HT, W])
        g_ps = m.ps("g_ps", [P, W])
        up_ps = m.ps("up_ps", [P, 2, W])
        lin_ps = m.ps("lin_ps", [P, 2, W])
        y_ps = m.ps("y_ps", [P, 2, W])
        loaded = m.sem("loaded")
        logits_made = m.sem("logits_made")
        shifted = m.sem("shifted")
        exps_ready = m.sem("exps_ready")
        weights_in = [m.sem(f"weights_in{r}") for r in range(2)]
        up_full = m.sem("up_full")
        lin_full = m.sem("lin_full")
        silu_done = m.sem("silu_done")
        hidden_ready = m.sem("hidden_ready")
        y_full = m.sem("y_full")
        y_free = m.sem("y_free")

        with nc.Block() as block:
            @block.sync
            def _(sp):
                sp.dma_start(wg_sb[:], wg).then_inc(loaded, 16)
                sp.dma_start(lower_sb[:], lower.partition_broadcast(P)).then_inc(loaded, 16)

                def load(e, r):
                    one = bass.ds(e, 1)
                    sp.dma_start(w12[:, r, 0, :], w1[one, :, :].rearrange("a p n -> p (a n)")).then_inc(weights_in[r], 16)
                    sp.dma_start(w12[:, r, 1, :], w2[one, :, :].rearrange("a p n -> p (a n)")).then_inc(weights_in[r], 16)
                    sp.dma_start(w3_sb[:, r, :, :], w3[one, :, :, :].rearrange("a p t n -> p (a t) n")
                                 ).then_inc(weights_in[r], 16)

                load(0, 0)
                load(1, 1)
                with sp.Fori(1, E // 2) as pair:
                    for r in range(2):
                        sp.wait_ge(y_full, (2 * pair + r - 1) * NG + 2)
                        load(2 * pair + r, r)

            @block.tensor
            def _(pe):
                pe.wait_ge(loaded, 32)
                for t in range(NT):
                    mm = nc.tensor.matmul(g_ps[:, t * E:(t + 1) * E], xT[:, t * P:(t + 1) * P], wg_sb[:],
                                          start=True, stop=True)
                mm.then_inc(logits_made, 1)

                def up(e, r, g, i):
                    n = (e * NG + g) * HT + i
                    k = (g * HT + i) % 2
                    for ps, j, full, freed in ((up_ps, 0, up_full, silu_done), (lin_ps, 1, lin_full, hidden_ready)):
                        pe.wait_ge(freed, n + 1)
                        nc.tensor.matmul(ps[0:HP, k, :], w12[:, r, j, i * HP:(i + 1) * HP],
                                         xT[:, g * W:(g + 1) * W], start=True, stop=True).then_inc(full, 1)

                def down(e, r, g):
                    n = e * NG + g
                    pe.wait_ge(y_free, n + 1)
                    pe.wait_ge(hidden_ready, (n + 1) * HT + 2)
                    for c in range(4):
                        for i in range(HT):
                            mm = nc.tensor.matmul(y_ps[:, g % 2, c * P:(c + 1) * P],
                                                  hidden[:, g % 2, i, c * P:(c + 1) * P], w3_sb[:, r, i, :],
                                                  start=(i == 0), stop=(i == HT - 1))
                    mm.then_inc(y_full, 1)

                with pe.Fori(0, E // 2) as pair:
                    for r in range(2):
                        e = 2 * pair + r
                        pe.wait_ge(weights_in[r], 48 * (pair + 1))
                        for g in range(NG):
                            for i in range(HT):
                                up(e, r, g, i)
                                if i == 1 and g:
                                    down(e, r, g - 1)
                        down(e, r, NG - 1)

            @block.scalar
            def _(act):
                act.wait_ge(shifted, 1)
                nc.scalar.activation(gating[:], gating[:], ACT.Exp).then_inc(exps_ready, 1)
                with act.Fori(0, E // 2) as pair:
                    for r in range(2):
                        for g in range(NG):
                            for i in range(HT):
                                n = ((2 * pair + r) * NG + g) * HT + i
                                k = (g * HT + i) % 2
                                act.wait_ge(up_full, n + 1)
                                act.wait_ge(hidden_ready, n + 1)
                                nc.scalar.activation(silu[:, k, :], up_ps[0:HP, k, :],
                                                     ACT.Silu).then_inc(silu_done, 1)

            @block.vector
            def _(dve):
                dve.sem_inc(silu_done, 2)
                dve.sem_inc(hidden_ready, 2)
                dve.sem_inc(y_full, 2)
                dve.sem_inc(y_free, 2)
                dve.wait_ge(logits_made, 1)
                nc.vector.tensor_copy(logits[:], g_ps[:, 0:NT * E].rearrange("p (t e) -> p t e", e=E))
                dve.drain()
                nc.vector.tensor_reduce(stat[:], logits[:], AX_X, ALU.max)
                dve.drain()
                nc.vector.tensor_tensor(gating[:], logits[:], stat[:, :, None].to_broadcast([P, NT, E]),
                                        ALU.subtract).then_inc(shifted, 1)
                for t in range(NT):
                    other = logits[:, t, None, :].to_broadcast([P, E, E])
                    own = logits[:, t, :, None].to_broadcast([P, E, E])
                    nc.vector.tensor_tensor(above[:, t, :, :], other, own, ALU.is_gt)
                    nc.vector.tensor_tensor(ties[:, t, :, :], other, own, ALU.is_equal)
                dve.drain()
                nc.vector.tensor_tensor(ties[:].rearrange("p t a b -> p t (a b)"),
                                        ties[:].rearrange("p t a b -> p t (a b)"),
                                        lower_sb[:].rearrange("p a b -> p (a b)")[:, None, :]
                                        .to_broadcast([P, NT, E * E]), ALU.mult)
                dve.drain()
                nc.vector.tensor_tensor(above[:], above[:], ties[:], ALU.add)
                dve.drain()
                nc.vector.tensor_reduce(rank[:], above[:], AX_X, ALU.add)
                dve.drain()
                nc.vector.tensor_scalar(rank[:], rank[:], 1.5, None, ALU.is_lt)
                dve.wait_ge(exps_ready, 1)
                dve.drain()
                nc.vector.tensor_tensor(gating[:], gating[:], rank[:], ALU.mult)
                dve.drain()
                nc.vector.tensor_reduce(stat[:], gating[:], AX_X, ALU.add)
                dve.drain()
                nc.vector.reciprocal(stat[:], stat[:])
                dve.drain()
                nc.vector.tensor_tensor(gating[:], gating[:], stat[:, :, None].to_broadcast([P, NT, E]), ALU.mult)
                dve.drain()

                def product(e, g, i):
                    n = (e * NG + g) * HT + i
                    k = (g * HT + i) % 2
                    if i == 0:
                        dve.wait_ge(y_full, e * NG + g + 1)
                    dve.wait_ge(lin_full, n + 1)
                    dve.wait_ge(silu_done, n + 3)
                    nc.vector.tensor_tensor(hidden[:, g % 2, i, :], silu[:, k, :], lin_ps[0:HP, k, :],
                                            ALU.mult).then_inc(hidden_ready, 1)

                def add(e, r, g):
                    dve.wait_ge(y_full, e * NG + g + 3)
                    for c in range(4):
                        t = 4 * g + c
                        last = nc.vector.scalar_tensor_tensor(x[:, t, :], y_ps[:, g % 2, c * P:(c + 1) * P],
                                                              gate_now[:, r, t:t + 1], x[:, t, :], ALU.mult, ALU.add)
                    last.then_inc(y_free, 1)

                with dve.Fori(0, E // 2) as pair:
                    for r in range(2):
                        e = 2 * pair + r
                        nc.vector.tensor_copy(gate_now[:, r, :],
                                              gating[:, :, bass.ds(e, 1)].rearrange("p t a -> p (t a)"))
                        for g in range(NG):
                            for i in range(HT):
                                product(e, g, i)
                                if i == 2 and g:
                                    add(e, r, g - 1)
                        add(e, r, NG - 1)
                        dve.drain()


def routed_experts(nc, name, x, xT, w, consts):
    E, H, GS, BUDGET = 64, 32, 64, (B * S // 64) * 16
    N = B * S
    HT = E * H // P
    EARLY = 2
    BIG = 1e30
    with Scope(nc, name) as outer:
        fsT = outer.sb("fsT", [E, N])
        recip = outer.sb("recip", [P, NT])
        wup = outer.sb("up_weights", [P, E * H])
        wgate = outer.sb("gate_weights", [P, E * H])
        bias = outer.sb("biases", [P, 2, HT])
        early = outer.sb("early", [P, EARLY, HT, W])
        wdown = outer.sb("down_weights", [P, HT, D])
        bdown = outer.sb("down_biases", [E, D])
        spread = outer.sb("spread", [E, HT, P])

        with Scope(nc, name + "r") as m:
            wr = m.sb("wr", [P, E])
            br = m.sb("br", [P, E])
            rank_row = m.sb("rank_row", [P, N // 2])
            ones = m.sb("ones", [P, P])
            score = m.sb("score", [P, NT, E])
            stat = m.sb("stat", [P, NT])
            sT = m.sb("sT", [E, N])
            halves = m.sb("halves", [P, 2, N // 2])
            other = m.sb("other", [E, N // 2])
            sums = m.sb("sums", [P, 16])
            all_sums = m.sb("all_sums", [P, N])
            greater = m.sb("greater", [P, N])
            ties = m.sb("ties", [P, N])
            so_far = m.sb("so_far", [E, N])
            always = m.sb("always", [E, N])
            counts = m.sb("counts", [P, 16])
            one = m.sb("one", [P, 8])
            per_expert = m.sb("per_expert", [E, E])
            silu = m.sb("silu", [P, 2, W])
            gate = m.sb("gate", [P, 2, W])
            t_ps = m.ps("t_ps", [P, 4, W])
            l_ps = m.ps("l_ps", [P, 2, W])
            up_ps = m.ps("up_ps", [P, W])
            gate_ps = m.ps("gate_ps", [P, W])
            loaded = m.sem("loaded")
            weights_in = m.sem("weights_in")
            down_in = m.sem("down_in")
            up_full = m.sem("up_full")
            up_moved = m.sem("up_moved")
            gate_full = m.sem("gate_full")
            gate_moved = m.sem("gate_moved")
            early_done = m.sem("early_done")
            logits_made = m.sem("logits_made")
            shifted = m.sem("shifted")
            exps_ready = m.sem("exps_ready")
            scores_ready = m.sem("scores_ready")
            turned = m.sem("turned")
            sums_ready = m.sem("sums_ready")
            sums_turned = m.sem("sums_turned")
            least_ready = m.sem("least_ready")
            least_turned = m.sem("least_turned")
            fs_ready = m.sem("fs_ready")
            totals_made = m.sem("totals_made")

            with nc.Block() as block:
                @block.sync
                def _(sp):
                    sp.dma_start(wr[:], w["wr"]).then_inc(loaded, 16)
                    sp.dma_start(br[:], w["br"].partition_broadcast(P)).then_inc(loaded, 16)
                    sp.dma_start(rank_row[:], consts["rank_row"]).then_inc(loaded, 16)
                    for dst, src in ((wup, "wup"), (wgate, "wgate"), (bias, "bias")):
                        sp.dma_start(dst[:], w[src]).then_inc(weights_in, 16)
                    for dst, src in ((wdown, w["wdown"]), (bdown, w["bdown"]), (spread, consts["spread_expert"])):
                        sp.dma_start(dst[:], src).then_inc(down_in, 16)
                    sp.wait_ge(down_in, 48)

                @block.tensor
                def _(pe):
                    ident = consts["ident_sb"]
                    pe.wait_ge(loaded, 48)
                    for t in range(NT):
                        at = 2 * (t % TB) + t // TB
                        mm = nc.tensor.matmul(l_ps[:, at // 8, at % 8 * E:(at % 8 + 1) * E], xT[:, t * P:(t + 1) * P],
                                              wr[:], start=True, stop=True)
                    mm.then_inc(logits_made, 1)
                    pe.wait_ge(scores_ready, 1)
                    for t in range(TB):
                        mm = nc.tensor.transpose(t_ps[:, t // 4, t % 4 * P:(t % 4 + 1) * P],
                                                 score[:, 2 * t:2 * t + 2, :].rearrange("p h e -> p (h e)"), ident[:])
                    mm.then_inc(turned, 1)
                    pe.wait_ge(weights_in, 48)
                    for k in range(EARLY * HT):
                        i, tokens = k % HT, xT[:, k // HT * W:(k // HT + 1) * W]
                        if k:
                            pe.wait_ge(up_moved, k)
                        nc.tensor.matmul(up_ps[:], wup[:, i * P:(i + 1) * P], tokens,
                                         start=True, stop=True).then_inc(up_full, 1)
                        if k:
                            pe.wait_ge(gate_moved, k)
                        nc.tensor.matmul(gate_ps[:], wgate[:, i * P:(i + 1) * P], tokens,
                                         start=True, stop=True).then_inc(gate_full, 1)
                    pe.wait_ge(sums_ready, 1)
                    for c in range(16):
                        mm = nc.tensor.transpose(t_ps[:, c // 4, c % 4 * P:(c % 4 + 1) * P],
                                                 sums[:, c:c + 1].to_broadcast([P, P]), ident[:])
                    mm.then_inc(sums_turned, 1)
                    pe.wait_ge(least_ready, 1)
                    nc.tensor.transpose(l_ps[:, 0, 0:P], one[:, 0:1].to_broadcast([P, P]),
                                        ident[:]).then_inc(least_turned, 1)
                    pe.wait_ge(fs_ready, 1)
                    for t in range(NT):
                        mm = nc.tensor.matmul(t_ps[:, t // 4, t % 4 * P:(t % 4 + 1) * P], fsT[:, t * P:(t + 1) * P],
                                              ones[0:E, :], start=True, stop=True)
                    mm.then_inc(totals_made, 1)

                @block.scalar
                def _(act):
                    act.wait_ge(shifted, 1)
                    nc.scalar.activation(score[:], score[:], ACT.Exp).then_inc(exps_ready, 1)
                    act.wait_ge(weights_in, 48)
                    for k in range(EARLY * HT):
                        i = k % HT
                        act.wait_ge(up_full, k + 1)
                        if k >= 2:
                            act.wait_ge(early_done, k - 1)
                        nc.scalar.activation(silu[:, k % 2, :], up_ps[:], ACT.Silu,
                                             bias=bias[:, 0, i:i + 1]).then_inc(up_moved, 1)
                        act.wait_ge(gate_full, k + 1)
                        nc.scalar.activation(gate[:, k % 2, :], gate_ps[:], ACT.Identity,
                                             bias=bias[:, 1, i:i + 1]).then_inc(gate_moved, 1)

                @block.gpsimd
                def _(pool):
                    for k in range(EARLY * HT):
                        pool.wait_ge(gate_moved, k + 1)
                        nc.gpsimd.tensor_tensor(early[:, k // HT, k % HT, :], silu[:, k % 2, :], gate[:, k % 2, :],
                                                ALU.mult).then_inc(early_done, 1)

                @block.vector
                def _(dve):
                    tt, ts = nc.vector.tensor_tensor, nc.vector.tensor_scalar
                    nc.vector.memset(ones[:], 1.0)
                    nc.vector.memset(always[:], 1.0)
                    dve.wait_ge(loaded, 48)
                    dve.wait_ge(logits_made, 1)
                    for h in range(2):
                        tt(score[:, 8 * h:8 * h + 8, :], l_ps[:, h, :].rearrange("p (t e) -> p t e", e=E),
                           br[:, None, :].to_broadcast([P, 8, E]), ALU.add)
                    dve.drain()
                    nc.vector.tensor_reduce(stat[:], score[:], AX_X, ALU.max)
                    dve.drain()
                    wide = stat[:, :, None].to_broadcast([P, NT, E])
                    tt(score[:], score[:], wide, ALU.subtract).then_inc(shifted, 1)
                    dve.wait_ge(exps_ready, 1)
                    nc.vector.tensor_reduce(stat[:], score[:], AX_X, ALU.add)
                    dve.drain()
                    nc.vector.reciprocal(stat[:], stat[:])
                    dve.drain()
                    tt(score[:], score[:], wide, ALU.mult).then_inc(scores_ready, 1)

                    dve.wait_ge(turned, 1)
                    for h in range(2):
                        at = slice(h * W, (h + 1) * W)
                        nc.vector.tensor_copy(sT[:, at], t_ps[0:E, h, :])
                        nc.vector.tensor_copy(sT[:, N // 2 + h * W:N // 2 + (h + 1) * W], t_ps[E:P, h, :])
                        nc.vector.tensor_copy(halves[0:E, 0, at], t_ps[0:E, h, :])
                        ts(halves[E:P, 0, at], t_ps[E:P, h, :], -1.0, None, ALU.mult)
                    dve.drain()

                    src = 0
                    n = N // 2

                    def exchange(frm, to, k, j):
                        turns = 2 if k < n else 1
                        views = [halves[:, v, :].rearrange("p (a d b s j) -> p a d b s j", d=turns, b=k // (2 * j),
                                                           s=2, j=j) for v in (frm, to)]
                        for d in range(turns):
                            lo, hi = (views[0][:, :, d, :, s, :] for s in range(2))
                            for s in range(2):
                                tt(views[1][:, :, d, :, s, :], lo, hi, ALU.max if s == d else ALU.min)
                        dve.drain()

                    k = 2
                    while k <= n:
                        j = k // 2
                        while j:
                            exchange(src, 1 - src, k, j)
                            src = 1 - src
                            j //= 2
                        k *= 2
                    ts(other[:], halves[E:P, src, :], -1.0, None, ALU.mult)
                    dve.drain()
                    tt(halves[0:E, 1 - src, :], halves[0:E, src, :], other[:], ALU.max)
                    tt(halves[E:P, 1 - src, :], halves[0:E, src, :], other[:], ALU.min)
                    dve.drain()
                    src = 1 - src
                    j = n // 2
                    while j:
                        exchange(src, 1 - src, n, j)
                        src = 1 - src
                        j //= 2
                    ranked = halves[:, src, :]

                    nc.vector.tensor_reduce(sums[:], ranked.rearrange("p (g n) -> p g n", n=GS), AX_X,
                                            ALU.add).then_inc(sums_ready, 1)
                    dve.wait_ge(sums_turned, 1)
                    flat = all_sums[:].rearrange("p (h c e) -> p c h e", h=2, e=E)
                    for c in range(16):
                        nc.vector.tensor_copy(flat[:, c, :, :], t_ps[:, c // 4, c % 4 * P:(c % 4 + 1) * P]
                                              .rearrange("p (h e) -> p h e", e=E))
                    dve.drain()
                    for c in range(16):
                        ts(greater[:], all_sums[:], sums[:, c:c + 1], 0.0, ALU.is_gt, ALU.add,
                           accum_out=counts[:, c:c + 1])
                        dve.drain()
                    ts(counts[:], counts[:], BUDGET - 0.5, BIG, ALU.is_gt, ALU.mult)
                    dve.drain()
                    tt(counts[:], counts[:], sums[:], ALU.add)
                    dve.drain()
                    nc.vector.tensor_reduce(one[:, 0:1], counts[:], AX_X, ALU.min).then_inc(least_ready, 1)
                    dve.wait_ge(least_turned, 1)
                    nc.vector.tensor_reduce(one[:, 1:2], l_ps[:, 0, 0:P], AX_X, ALU.min)
                    dve.drain()

                    def keep(values, least, budget, room, rows):
                        gr, ti = greater[0:rows, :], ties[0:rows, :]
                        ts(gr, values, least, 0.0, ALU.is_gt, ALU.add, accum_out=room)
                        dve.drain()
                        if isinstance(budget, float):
                            ts(room, room, -1.0, budget, ALU.mult, ALU.add)
                        else:
                            tt(room, budget, room, ALU.subtract)
                        ts(ti, values, least, None, ALU.is_equal)
                        dve.drain()
                        nc.vector.tensor_tensor_scan(so_far[0:rows, :], always[0:rows, :], ti, 0.0,
                                                     ALU.mult, ALU.add)
                        dve.drain()
                        ts(so_far[0:rows, :], so_far[0:rows, :], room, None, ALU.is_le)
                        dve.drain()
                        tt(ti, ti, so_far[0:rows, :], ALU.mult)
                        dve.drain()
                        tt(gr, gr, ti, ALU.add)
                        dve.drain()

                    keep(all_sums[0:E, :], one[0:E, 1:2], float(BUDGET), one[0:E, 2:3], E)
                    nc.vector.tensor_reduce(per_expert[:], greater[0:E, :].rearrange("p (g e) -> p e g", e=E), AX_X,
                                            ALU.add)
                    dve.drain()
                    tt(per_expert[:], per_expert[:], consts["ident_sb"][0:E, 0:E], ALU.mult)
                    dve.drain()
                    nc.vector.tensor_reduce(one[0:E, 3:4], per_expert[:], AX_X, ALU.add)
                    dve.drain()
                    ts(one[0:E, 4:5], one[0:E, 3:4], float(GS), None, ALU.mult)
                    ts(one[E:P, 4:5], one[0:E, 3:4], float(GS), None, ALU.mult)
                    dve.drain()
                    ts(halves[:, 1 - src, :], rank_row[:], one[:, 4:5], BIG, ALU.is_ge, ALU.mult)
                    dve.drain()
                    tt(halves[:, 1 - src, :], halves[:, 1 - src, :], ranked, ALU.add)
                    dve.drain()
                    nc.vector.tensor_reduce(one[:, 5:6], halves[:, 1 - src, :], AX_X, ALU.min)
                    dve.drain()
                    nc.vector.tensor_copy(one[0:E, 6:7], one[E:P, 5:6])
                    dve.drain()
                    tt(one[0:E, 5:6], one[0:E, 5:6], one[0:E, 6:7], ALU.min)
                    dve.drain()
                    keep(sT[:], one[0:E, 5:6], one[0:E, 4:5], one[0:E, 7:8], E)
                    tt(fsT[:], sT[:], greater[0:E, :], ALU.mult).then_inc(fs_ready, 1)
                    dve.wait_ge(totals_made, 1)
                    totals = t_ps[:].rearrange("p g (c n) -> p (g c) n", n=P)[:, :, 0]
                    ts(recip[:], totals, 1e-6, None, ALU.add)
                    dve.drain()
                    nc.vector.reciprocal(recip[:], recip[:])

        with Scope(nc, name + "f") as m:
            fs_now = m.sb("fs_now", [E, W])
            silu = m.sb("silu", [P, 2, W])
            prod = m.sb("prod", [P, 2, W])
            hidden = m.sb("hidden", [P, HT, W])
            up_ps = m.ps("up_ps", [P, 2, W])
            gate_ps = m.ps("gate_ps", [P, 2, W])
            fs_ps = m.ps("fs_ps", [P, 2, W])
            y_ps = m.ps("y_ps", [P, W])
            up_full = m.sem("up_full")
            gate_full = m.sem("gate_full")
            fs_full = m.sem("fs_full")
            silu_done = m.sem("silu_done")
            prod_done = m.sem("prod_done")
            hidden_ready = m.sem("hidden_ready")
            fs_copied = m.sem("fs_copied")
            y_full = m.sem("y_full")
            y_free = m.sem("y_free")
            with nc.Block() as block:
                @block.tensor
                def _(pe):
                    def spread_fs(n, i):
                        pe.wait_ge(hidden_ready, n + 1)
                        nc.tensor.matmul(fs_ps[:, i % 2, :], spread[:, i, :], fs_now[:],
                                         start=True, stop=True).then_inc(fs_full, 1)

                    def down(g, units):
                        pe.wait_ge(y_free, g + 1)
                        pe.wait_ge(hidden_ready, (g + 1) * HT + 2)
                        for c in range(4):
                            cols = slice(c * P, (c + 1) * P)
                            for i in range(HT):
                                nc.tensor.matmul(y_ps[:, cols], units[:, i, cols], wdown[:, i, :],
                                                 start=(i == 0), stop=False)
                            mm = nc.tensor.matmul(y_ps[:, cols], fs_now[:, cols], bdown[:], start=False, stop=True)
                        mm.then_inc(y_full, 1)

                    for g in range(EARLY):
                        pe.wait_ge(fs_copied, g + 1)
                        for i in range(HT):
                            spread_fs(g * HT + i, i)
                        down(g, early[:, g, :, :])
                    with pe.Fori(EARLY, NG) as g:
                        for i in range(HT):
                            n = (g - EARLY) * HT + i
                            tokens = xT[:, bass.ds(g * W, W)]
                            pe.wait_ge(silu_done, n + 1)
                            nc.tensor.matmul(up_ps[:, i % 2, :], wup[:, i * P:(i + 1) * P], tokens,
                                             start=True, stop=True).then_inc(up_full, 1)
                            pe.wait_ge(prod_done, n + 1)
                            nc.tensor.matmul(gate_ps[:, i % 2, :], wgate[:, i * P:(i + 1) * P], tokens,
                                             start=True, stop=True).then_inc(gate_full, 1)
                            if i == 0:
                                pe.wait_ge(fs_copied, g + 1)
                            spread_fs(g * HT + i, i)
                        down(g, hidden)

                @block.scalar
                def _(act):
                    def copy_fs(g):
                        act.wait_ge(y_full, g + 1)
                        nc.scalar.copy(fs_now[:], fsT[:, bass.ds(g * W, W)]).then_inc(fs_copied, 1)

                    for g in range(EARLY):
                        copy_fs(g)
                    with act.Fori(EARLY, NG) as g:
                        copy_fs(g)
                        for i in range(HT):
                            n = (g - EARLY) * HT + i
                            act.wait_ge(up_full, n + 1)
                            act.wait_ge(prod_done, n + 1)
                            nc.scalar.activation(silu[:, i % 2, :], up_ps[:, i % 2, :], ACT.Silu,
                                                 bias=bias[:, 0, i:i + 1]).then_inc(silu_done, 1)

                @block.vector
                def _(dve):
                    def times_fs(g, i, to, frm):
                        dve.wait_ge(fs_full, g * HT + i + 1)
                        nc.vector.tensor_tensor(to, frm, fs_ps[:, i % 2, :], ALU.mult).then_inc(hidden_ready, 1)

                    def add(g):
                        dve.wait_ge(y_full, g + 2)
                        for c in range(4):
                            t = 4 * g + c
                            row = x[:, bass.ds(t, 1), :].rearrange("p a n -> p (a n)")
                            last = nc.vector.scalar_tensor_tensor(row, y_ps[:, c * P:(c + 1) * P],
                                                                  recip[:, bass.ds(t, 1)], row, ALU.mult, ALU.add)
                        last.then_inc(y_free, 1)
                        dve.drain()

                    for s, k in ((silu_done, 2), (prod_done, 2), (hidden_ready, 2), (y_full, 1), (y_free, 1)):
                        dve.sem_inc(s, k)
                    for g in range(EARLY):
                        for i in range(HT):
                            times_fs(g, i, early[:, g, i, :], early[:, g, i, :])
                        add(g)
                    with dve.Fori(EARLY, NG) as g:
                        for i in range(HT + 1):
                            n = (g - EARLY) * HT + i
                            if i < HT:
                                dve.wait_ge(gate_full, n + 1)
                                dve.wait_ge(silu_done, n + 3)
                                dve.wait_ge(hidden_ready, g * HT + i + 1)
                                nc.vector.scalar_tensor_tensor(prod[:, i % 2, :], gate_ps[:, i % 2, :],
                                                               bias[:, 1, i:i + 1], silu[:, i % 2, :],
                                                               ALU.add, ALU.mult).then_inc(prod_done, 1)
                            if i:
                                dve.wait_ge(prod_done, n + 2)
                                times_fs(g, i - 1, hidden[:, i - 1, :], prod[:, (i - 1) % 2, :])
                        add(g)


def leaf_layers(nc, name, y_tok, yT, outs, w, act_fn, consts):
    DEPTH, NL, LW = 8, 256, 16
    TILES, SUB = NL * LW // P, P // LW
    BLOCKS = NT + TILES
    GROUPS = len(outs) * BLOCKS // 4
    ROW = D + SUB
    T = len(outs)
    I32 = mybir.dt.int32
    slots = nc.dram_tensor(f"{name}_slots", [T * BLOCKS * P, ROW], F32, kind="Internal").ap()
    results = nc.dram_tensor(f"{name}_results", [T * BLOCKS * P, D], F32, kind="Internal").ap()
    with Scope(nc, name) as outer:
        rows = outer.sb("rows", [P, T, NT, ROW])
        slot_of = outer.sb("slot_of", [P, T, NT], I32)
        leaf_of = outer.sb("leaf_of", [P, T, NT], I32)
        tile_of = outer.sb("tile_of", [1, T * BLOCKS], I32)

        with Scope(nc, name + "t") as m:
            nw = m.sb("nw", [P, T, NL])
            nb = m.sb("nb", [P, T, NL])
            zeros = m.sb("zeros", [P, BLOCKS // 4 * ROW])
            iota = m.sb("iota", [P, BLOCKS])
            before = m.sb("before", [P, 2, P], BF16)
            right = m.sb("right", [P, NT, NL], BF16)
            ways = m.sb("ways", [P, 2, NT, NL], BF16)
            in_tile = m.sb("in_tile", [P, T, NT, TILES], BF16)
            over = m.sb("over", [P, TILES, NT])
            some = m.sb("some", [P, 4, TILES])
            table = m.sb("table", [1, BLOCKS, TILES])
            short = m.sb("short", [1, BLOCKS])
            place = m.sb("place", [P, NT, TILES])
            spot = m.sb("spot", [P, 3, NT])
            by_sub = m.sb("by_sub", [P, NT, SUB])
            l_ps = m.ps("l_ps", [P, 4, W])
            rank_ps = m.ps("rank_ps", [P, 2, W])
            count_ps = m.ps("count_ps", [P, 2, W])
            loaded = m.sem("loaded")
            cleared = m.sem("cleared")
            zeros_ready = m.sem("zeros_ready")
            logits_full = m.sem("logits_full")
            logits_free = m.sem("logits_free")
            tile_ready = m.sem("tile_ready")
            rank_full = m.sem("rank_full")
            rows_copied = m.sem("rows_copied")
            routed = m.sem("routed")
            moved = m.sem("moved")
            with nc.Block() as block:
                @block.sync
                def _(sp):
                    sp.dma_start(nw[:], w["nw"].rearrange("t p n -> p t n")).then_inc(loaded, 16)
                    sp.dma_start(nb[:], w["nb"].partition_broadcast(P)).then_inc(loaded, 16)
                    sp.dma_start(iota[:], consts["iota"].partition_broadcast(P)).then_inc(loaded, 16)
                    sp.dma_start(before[:], consts["before"]).then_inc(loaded, 16)
                    sp.wait_ge(zeros_ready, 1)
                    wide = slots.rearrange("(p q r) c -> p q (r c)", p=P, q=4 * T)
                    for q in range(4 * T):
                        sp.dma_start(wide[:, q, :], zeros[:]).then_inc(cleared, 16)
                    sp.wait_ge(cleared, 16 * 4 * T)

                @block.tensor
                def _(pe):
                    pe.wait_ge(loaded, 64)
                    for n in range(T):
                        for t in range(NT):
                            s = 8 * n + t // 2
                            if s >= 4 and t % 2 == 0:
                                pe.wait_ge(logits_free, s - 3)
                            mm = nc.tensor.matmul(l_ps[:, s % 4, t % 2 * NL:(t % 2 + 1) * NL],
                                                  yT[:, t * P:(t + 1) * P], nw[:, n, :], start=True, stop=True)
                            if t % 2:
                                mm.then_inc(logits_full, 1)
                        pe.wait_ge(tile_ready, n + 1)
                        if n >= 2:
                            pe.wait_ge(routed, n - 1)
                        ones = in_tile[:, n, :, :].rearrange("p t e -> p (t e)")
                        nc.tensor.matmul(rank_ps[:, n % 2, :], before[:, 0, :], ones, start=True, stop=False)
                        for s in range(1, NT):
                            nc.tensor.matmul(rank_ps[:, n % 2, s * TILES:W], before[:, 1, :],
                                             ones[:, 0:W - s * TILES], start=False, stop=(s == NT - 1))
                        for t in range(NT):
                            mm = nc.tensor.matmul(count_ps[:, n % 2, 0:TILES], before[:, 1, :],
                                                  in_tile[:, n, t, :], start=(t == 0), stop=(t == NT - 1))
                        mm.then_inc(rank_full, 1)

                @block.scalar
                def _(act):
                    for n in range(T):
                        nc.scalar.copy(rows[:, n, :, 0:D], y_tok[:]).then_inc(rows_copied, 1)

                @block.vector
                def _(dve):
                    nc.vector.memset(zeros[:], 0.0).then_inc(zeros_ready, 1)
                    nc.vector.memset(some[:, 3, :], 1.0)
                    dve.wait_ge(loaded, 64)
                    nc.vector.tensor_scalar(nb[:], nb[:], -1.0, None, ALU.mult)
                    dve.drain()
                    tile_step = DEPTH - SUB.bit_length() + 1
                    for n in range(T):
                        for s in range(NT // 2):
                            dve.wait_ge(logits_full, 8 * n + s + 1)
                            nc.vector.tensor_tensor(right[:, 2 * s:2 * s + 2, :],
                                                    l_ps[:, s % 4, :].rearrange("p (t n) -> p t n", n=NL),
                                                    nb[:, n:n + 1, :].to_broadcast([P, 2, NL]),
                                                    ALU.is_gt).then_inc(logits_free, 1)
                        nc.vector.memset(ways[:, 0, :, 0:1], 1.0)
                        for level in range(DEPTH):
                            k = 2 ** level
                            now = in_tile[:, n, :, :] if level == tile_step else ways[:, level % 2, :, 0:k]
                            nxt = in_tile[:, n, :, :] if level == tile_step - 1 else \
                                ways[:, 1 - level % 2, :, 0:2 * k]
                            nxt = nxt.rearrange("p t (j s) -> p t j s", s=2)
                            dve.drain()
                            nc.vector.tensor_tensor(nxt[:, :, :, 1], now, right[:, :, k - 1:2 * k - 1], ALU.mult)
                            dve.drain()
                            last = nc.vector.tensor_tensor(nxt[:, :, :, 0], now, nxt[:, :, :, 1], ALU.subtract)
                            if level == tile_step - 1:
                                last.then_inc(tile_ready, 1)
                        dve.drain()
                        sub = rows[:, n, :, D:ROW]
                        nc.vector.tensor_reduce(sub, ways[:, DEPTH % 2, :, :].rearrange("p t (j s) -> p t s j", s=SUB),
                                                AX_X, ALU.add)
                        nc.vector.tensor_tensor(place[:], in_tile[:, n, :, :],
                                                iota[:, None, 0:TILES].to_broadcast([P, NT, TILES]), ALU.mult)
                        dve.drain()
                        nc.vector.tensor_tensor(by_sub[:], sub, iota[:, None, 0:SUB].to_broadcast([P, NT, SUB]),
                                                ALU.mult)
                        nc.vector.tensor_reduce(spot[:, 0, :], place[:], AX_X, ALU.add)
                        dve.wait_ge(rank_full, n + 1)
                        nc.vector.tensor_scalar(some[:, 0, :], count_ps[:, n % 2, 0:TILES], 1.0 / P, None, ALU.mult)
                        dve.drain()
                        nc.vector.tensor_tensor(over[:], some[:, 0, :, None].to_broadcast([P, TILES, NT]),
                                                iota[:, None, 0:NT].to_broadcast([P, TILES, NT]), ALU.is_gt)
                        nc.vector.tensor_reduce(spot[:, 1, :], by_sub[:], AX_X, ALU.add)
                        dve.drain()
                        nc.vector.tensor_reduce(some[:, 1, :], over[:], AX_X, ALU.add)
                        nc.vector.tensor_scalar(spot[:, 0, :], spot[:, 0, :], float(SUB), float(n * NL),
                                                ALU.mult, ALU.add)
                        dve.drain()
                        nc.vector.tensor_tensor(leaf_of[:, n, :], spot[:, 0, :], spot[:, 1, :], ALU.add)
                        nc.vector.tensor_tensor_scan(some[:, 2, :], some[:, 3, :], some[:, 1, :], 0.0,
                                                     ALU.mult, ALU.add)
                        dve.drain()
                        nc.vector.tensor_tensor(some[:, 0, :], some[:, 2, :], some[:, 1, :], ALU.subtract)
                        nc.vector.tensor_tensor(table[:], some[0:1, 2:3, :].to_broadcast([1, BLOCKS, TILES]),
                                                iota[0:1, 0:BLOCKS, None].to_broadcast([1, BLOCKS, TILES]), ALU.is_le)
                        dve.drain()
                        nc.vector.tensor_scalar(some[:, 0, :], some[:, 0, :], float(P), float(n * BLOCKS * P),
                                                ALU.mult, ALU.add)
                        nc.vector.tensor_reduce(short[:], table[:], AX_X, ALU.add)
                        dve.drain()
                        nc.vector.tensor_tensor(place[:], rank_ps[:, n % 2, :].rearrange("p (t e) -> p t e", e=TILES),
                                                some[:, 0:1, :].to_broadcast([P, NT, TILES]), ALU.add)
                        nc.vector.tensor_scalar(short[:], short[:], TILES - 1.0, float(n * TILES), ALU.min, ALU.add)
                        dve.drain()
                        nc.vector.tensor_tensor(place[:], place[:], in_tile[:, n, :, :], ALU.mult)
                        nc.vector.tensor_copy(tile_of[:, n * BLOCKS:(n + 1) * BLOCKS], short[:])
                        dve.drain()
                        nc.vector.tensor_reduce(spot[:, 2, :], place[:], AX_X, ALU.add)
                        dve.drain()
                        nc.vector.tensor_copy(slot_of[:, n, :], spot[:, 2, :]).then_inc(routed, 1)

                @block.gpsimd
                def _(pool):
                    pool.wait_ge(rows_copied, T)
                    for n in range(T):
                        pool.wait_ge(routed, n + 1)
                        pool.wait_ge(cleared, 16 * 4 * T)
                        for t in range(NT):
                            nc.gpsimd.indirect_dma_start(slots,
                                                         bass.IndirectOffsetOnAxis(slot_of[:, n, t:t + 1], 0),
                                                         rows[:, n, t, :], None).then_inc(moved, 16)
                    pool.wait_ge(moved, 16 * NT * T)

        with Scope(nc, name + "l") as m:
            R, Q = 2, 4
            block_rows = m.sb("block_rows", [P, Q, 4, ROW])
            w12 = m.sb("w12", [P, Q, 4, 2 * P + 1])
            ident_bf = m.sb("ident_bf", [P, P], BF16)
            widen = m.sb("widen", [4 * SUB, 4, P], BF16)
            turned_rows = m.sb("turned_rows", [P, R, W])
            sub_ones = m.sb("sub_ones", [P, R, 4, SUB], BF16)
            sub_turned = m.sb("sub_turned", [4 * SUB, R, P], BF16)
            active = m.sb("active", [P, R, W])
            own = m.sb("own", [P, R, W])
            result = m.sb("result", [P, R, 4, D])
            y_ps = m.ps("y_ps", [P, W])
            s_ps = m.ps("s_ps", [4 * SUB, 2 * W], BF16)
            m_ps = m.ps("m_ps", [P, R, W])
            h_ps = m.ps("h_ps", [P, R, W])
            o_ps = m.ps("o_ps", [P, R, W])
            const_in = m.sem("const_in")
            rows_in = [m.sem(f"rows_in{q}") for q in range(Q)]
            weights_in = [m.sem(f"weights_in{q}") for q in range(Q)]
            sub_ready = m.sem("sub_ready")
            y_turned = m.sem("y_turned")
            y_copied = m.sem("y_copied")
            sub_out = m.sem("sub_out")
            sub_copied = m.sem("sub_copied")
            hidden_full = m.sem("hidden_full")
            mask_full = m.sem("mask_full")
            active_done = m.sem("active_done")
            own_done = m.sem("own_done")
            out_full = m.sem("out_full")
            out_copied = m.sem("out_copied")
            stored = [m.sem(f"stored{r}") for r in range(R)]
            gathered = [m.sem(f"gathered{n}") for n in range(T)]
            LOOPS = GROUPS // Q
            with nc.Block() as block:
                @block.sync
                def _(sp):
                    def load(k, q):
                        sp.wait_ge(out_full, k + 1)
                        sp.dma_start(block_rows[:, q, :, :],
                                     slots[bass.ds(k * 4 * P, 4 * P), :].rearrange("(c p) n -> p c n", p=P)
                                     ).then_inc(rows_in[q], 16)
                        for c in range(4):
                            tile = sp.value_load(tile_of[0:1, bass.ds(4 * k + c, 1)], min_val=0,
                                                 max_val=T * TILES - 1)
                            sp.dma_start(w12[:, q, c, :],
                                         w["w12"][bass.ds(tile, 1), :, :].rearrange("a p n -> p (a n)")
                                         ).then_inc(weights_in[q], 16)

                    def store(k, r):
                        sp.wait_ge(out_copied, k + 1 + R)
                        sp.dma_start(results[bass.ds(k * 4 * P, 4 * P), :].rearrange("(c p) n -> p c n", p=P),
                                     result[:, r, :, :]).then_inc(stored[r], 16)

                    sp.dma_start(ident_bf[:], consts["ident_bf"]).then_inc(const_in, 16)
                    sp.dma_start(widen[:], consts["widen"]).then_inc(const_in, 16)
                    for q in range(Q):
                        load(q, q)
                    with sp.Fori(1, LOOPS) as i:
                        for q in range(Q):
                            load(Q * i + q, q)
                            store(Q * i + q - Q, q % R)
                    for q in range(Q):
                        store(GROUPS - Q + q, q % R)

                @block.tensor
                def _(pe):
                    def turn(k, i, q):
                        pe.wait_ge(rows_in[q], 16 * (i + 1))
                        pe.wait_ge(y_copied, k + 1)
                        for c in range(4):
                            mm = nc.tensor.transpose(y_ps[:, c * P:(c + 1) * P], block_rows[:, q, c, 0:D],
                                                     consts["ident_sb"][:])
                        mm.then_inc(y_turned, 1)
                        pe.wait_ge(sub_ready, k + 1)
                        nc.tensor.transpose(s_ps[:, 0:P], sub_ones[:, q % R, :, :].rearrange("p c s -> p (c s)"),
                                            ident_bf[:]).then_inc(sub_out, 1)

                    def hidden(k, i, q):
                        r = q % R
                        pe.wait_ge(own_done, k + 1)
                        pe.wait_ge(y_copied, k + 2)
                        pe.wait_ge(weights_in[q], 64 * (i + 1))
                        for c in range(4):
                            mm = nc.tensor.matmul(h_ps[:, r, c * P:(c + 1) * P], w12[:, q, c, 0:P],
                                                  turned_rows[:, r, c * P:(c + 1) * P], start=True, stop=True)
                        mm.then_inc(hidden_full, 1)
                        pe.wait_ge(sub_copied, k + 1)
                        for c in range(4):
                            mm = nc.tensor.matmul(m_ps[:, r, c * P:(c + 1) * P], widen[:, c, :],
                                                  sub_turned[:, r, :], start=True, stop=True)
                        mm.then_inc(mask_full, 1)

                    def down(k, q):
                        r = q % R
                        pe.wait_ge(own_done, k + 1 + R)
                        pe.wait_ge(out_copied, k + 1)
                        for c in range(4):
                            mm = nc.tensor.matmul(o_ps[:, r, c * P:(c + 1) * P], own[:, r, c * P:(c + 1) * P],
                                                  w12[:, q, c, P:2 * P], start=True, stop=True)
                        mm.then_inc(out_full, 1)

                    def body(i, first):
                        for q in range(Q):
                            k = Q * i + q
                            turn(k, i, q)
                            if not (first and q == 0):
                                hidden(k - 1, i if q else i - 1, (q - 1) % Q)
                            if not (first and q < 2):
                                down(k - 2, (q - 2) % Q)

                    pe.wait_ge(const_in, 32)
                    body(0, True)
                    with pe.Fori(1, LOOPS) as i:
                        body(i, False)
                    hidden(GROUPS - 1, LOOPS - 1, Q - 1)
                    down(GROUPS - 2, Q - 2)
                    down(GROUPS - 1, Q - 1)

                @block.scalar
                def _(act):
                    def act_y(k, q):
                        act.wait_ge(y_turned, k + 1)
                        nc.scalar.copy(turned_rows[:, q % R, :], y_ps[:]).then_inc(y_copied, 1)

                    def act_hidden(k, q):
                        r = q % R
                        act.wait_ge(hidden_full, k + 1)
                        act.wait_ge(own_done, k + 1)
                        for c in range(4):
                            last = nc.scalar.activation(active[:, r, c * P:(c + 1) * P], h_ps[:, r, c * P:(c + 1) * P],
                                                        act_fn, bias=w12[:, q, c, 2 * P:2 * P + 1])
                        last.then_inc(active_done, 1)

                    def body(i, first):
                        for q in range(Q):
                            act_y(Q * i + q, q)
                            if not (first and q == 0):
                                act_hidden(Q * i + q - 1, (q - 1) % Q)

                    body(0, True)
                    with act.Fori(1, LOOPS) as i:
                        body(i, False)
                    act_hidden(GROUPS - 1, Q - 1)

                @block.vector
                def _(dve):
                    def dve_sub(k, i, q):
                        dve.wait_ge(rows_in[q], 16 * (i + 1))
                        nc.vector.tensor_copy(sub_ones[:, q % R, :, :],
                                              block_rows[:, q, :, D:ROW]).then_inc(sub_ready, 1)

                    def dve_turned(k, q):
                        dve.wait_ge(sub_out, k + 1)
                        nc.vector.tensor_copy(sub_turned[:, q % R, :], s_ps[:, 0:P]).then_inc(sub_copied, 1)

                    def dve_own(k, q):
                        r = q % R
                        dve.wait_ge(active_done, k + 1 + R)
                        dve.wait_ge(mask_full, k + 1)
                        dve.wait_ge(out_full, k + 1 + Q - R)
                        nc.vector.tensor_tensor(own[:, r, :], active[:, r, :], m_ps[:, r, :],
                                                ALU.mult).then_inc(own_done, 1)

                    def dve_out(k, times, q):
                        r = q % R
                        dve.wait_ge(out_full, k + 1 + Q)
                        if not (isinstance(times, int) and times == 0):
                            dve.wait_ge(stored[r], 16 * times)
                        nc.vector.tensor_copy(result[:, r, :, :].rearrange("p c n -> p (c n)"),
                                              o_ps[:, r, :]).then_inc(out_copied, 1)

                    def body(i, first):
                        for q in range(Q):
                            k = Q * i + q
                            dve_sub(k, i, q)
                            dve_turned(k, q)
                            if not (first and q == 0):
                                dve_own(k - 1, (q - 1) % Q)
                            if not (first and q < 2):
                                dve_out(k - 2, 2 * i + q // 2 - 1, (q - 2) % Q)

                    dve.sem_inc(active_done, R)
                    dve.sem_inc(own_done, R)
                    dve.sem_inc(out_full, Q)
                    dve.sem_inc(out_copied, R)
                    dve.sem_inc(y_copied, 1)
                    body(0, True)
                    with dve.Fori(1, LOOPS) as i:
                        body(i, False)
                    dve_own(GROUPS - 1, Q - 1)
                    dve_out(GROUPS - 2, GROUPS // 2 - 1, Q - 2)
                    dve_out(GROUPS - 1, GROUPS // 2 - 1, Q - 1)
                    for n in range(T):
                        dve.wait_ge(gathered[n], 32 * NT)
                        nc.vector.tensor_tensor(outs[n][:], outs[n][:], rows[:, n, :, 0:D], ALU.add)

                @block.gpsimd
                def _(pool):
                    for n in range(T):
                        for t in range(NT):
                            nc.gpsimd.indirect_dma_start(outs[n][:, t, :], None, w["b2"],
                                                         bass.IndirectOffsetOnAxis(leaf_of[:, n, t:t + 1], 0)
                                                         ).then_inc(gathered[n], 16)
                        for r in range(R):
                            pool.wait_ge(stored[r], 16 * (BLOCKS // 4 // R) * (n + 1))
                        for t in range(NT):
                            nc.gpsimd.indirect_dma_start(rows[:, n, t, 0:D], None, results[0:(n + 1) * BLOCKS * P, :],
                                                         bass.IndirectOffsetOnAxis(slot_of[:, n, t:t + 1], 0)
                                                         ).then_inc(gathered[n], 16)


def single_attention(nc, name, xn, yT, q_tok, k_tok, v_tok, consts):
    SCALE = D ** -0.5
    with Scope(nc, name) as m:
        qT = m.sb("qT", [P, B * S])
        kT = m.sb("kT", [P, B * S])
        q_now = m.sb("q_now", [P, B, P])
        probs = m.sb("probs", [P, 2, S])
        probsT = m.sb("probsT", [P, TB, P])
        top = m.sb("top", [P, 2, 4])
        s_ps = m.ps("s_ps", [P, B, S])
        t_ps = m.ps("t_ps", [P, TB * P])
        o_ps = m.ps("o_ps", [P, W])
        qk_turned = m.sem("qk_turned")
        qk_copied = m.sem("qk_copied")
        q_in = m.sem("q_in")
        scores_full = m.sem("scores_full")
        top_ready = m.sem("top_ready")
        probs_ready = m.sem("probs_ready")
        turned = m.sem("turned")
        copied = m.sem("copied")
        out_full = m.sem("out_full")
        out_free = m.sem("out_free")
        ident = consts["ident_sb"]
        with nc.Block() as block:
            @block.gpsimd
            def _(pool):
                pool.wait_ge(qk_copied, B)
                with pool.Fori(0, TB) as t:
                    for b in range(B):
                        pool.wait_ge(probs_ready, 2 * t + 1 + b)
                        nc.gpsimd.tensor_copy(q_now[:, b, :], qT[:, bass.ds(b * S + t * P, P)])
                        pool.drain()
                        pool.sem_inc(q_in, 1)

            @block.tensor
            def _(pe):
                for n, tok in enumerate((q_tok, k_tok)):
                    for b in range(B):
                        if n:
                            pe.wait_ge(qk_copied, b + 1)
                        for t in range(TB):
                            mm = nc.tensor.transpose(s_ps[:, b, t * P:(t + 1) * P], tok[:, b * TB + t, :], ident[:])
                        mm.then_inc(qk_turned, 1)
                pe.wait_ge(qk_copied, 2 * B)
                with pe.Fori(0, TB) as t:
                    for b in range(B):
                        n = 2 * t + b
                        pe.wait_ge(q_in, n + 1)
                        pe.wait_ge(probs_ready, n + 1)
                        for c in range(2):
                            mm = nc.tensor.matmul(s_ps[:, b, c * W:(c + 1) * W], q_now[:, b, :],
                                                  kT[:, b * S + c * W:b * S + (c + 1) * W], start=True, stop=True)
                        mm.then_inc(scores_full, 1)
                    for b in range(B):
                        n = 2 * t + b
                        pe.wait_ge(probs_ready, n + 3)
                        pe.wait_ge(copied, n + 1)
                        for c in range(TB):
                            mm = nc.tensor.transpose(t_ps[:, c * P:(c + 1) * P], probs[:, b, c * P:(c + 1) * P],
                                                     ident[:])
                        mm.then_inc(turned, 1)
                        pe.wait_ge(copied, n + 2)
                        pe.wait_ge(out_free, n + 1)
                        for c in range(TB):
                            mm = nc.tensor.matmul(o_ps[:, 0:D], probsT[:, c, :], v_tok[:, b * TB + c, :],
                                                  start=(c == 0), stop=(c == TB - 1))
                        mm.then_inc(out_full, 1)
                pe.wait_ge(out_free, 2 * TB + 1)
                for g in range(NG):
                    for c in range(4):
                        t = 4 * g + c
                        mm = nc.tensor.transpose(s_ps[:, g // 2, g % 2 * W + c * P:g % 2 * W + (c + 1) * P],
                                                 xn[:, t, :], ident[:])
                    mm.then_inc(qk_turned, 1)

            @block.scalar
            def _(act):
                for n, turned_to in enumerate((qT, kT)):
                    for b in range(B):
                        act.wait_ge(qk_turned, B * n + b + 1)
                        nc.scalar.copy(turned_to[:, b * S:(b + 1) * S], s_ps[:, b, :]).then_inc(qk_copied, 1)
                with act.Fori(0, TB) as t:
                    for b in range(B):
                        n = 2 * t + b
                        act.wait_ge(top_ready, n + 1)
                        nc.scalar.activation(probs[:, b, :], s_ps[:, b, :], ACT.Exp, bias=top[:, b, 1:2],
                                             scale=SCALE, accum_out=top[:, b, 2:3]).then_inc(probs_ready, 1)
                    for b in range(B):
                        n = 2 * t + b
                        act.wait_ge(turned, n + 1)
                        act.wait_ge(out_full, n + 1)
                        nc.scalar.copy(probsT[:].rearrange("p c n -> p (c n)"), t_ps[:]).then_inc(copied, 1)
                for g in range(NG):
                    act.wait_ge(qk_turned, 2 * B + g + 1)
                    nc.scalar.copy(yT[:, g * W:(g + 1) * W], s_ps[:, g // 2, g % 2 * W:(g % 2 + 1) * W])

            @block.vector
            def _(dve):
                dve.sem_inc(probs_ready, 2)
                dve.sem_inc(copied, 1)
                dve.sem_inc(out_full, 1)
                dve.sem_inc(out_free, 1)
                with dve.Fori(0, TB) as t:
                    for b in range(B):
                        n = 2 * t + b
                        dve.wait_ge(scores_full, n + 1)
                        nc.vector.tensor_reduce(top[:, b, 0:1], s_ps[:, b, :], AX_X, ALU.max)
                        dve.drain()
                        nc.vector.tensor_scalar(top[:, b, 1:2], top[:, b, 0:1], -SCALE, None,
                                                ALU.mult).then_inc(top_ready, 1)
                    for b in range(B):
                        n = 2 * t + b
                        dve.wait_ge(probs_ready, n + 3)
                        nc.vector.reciprocal(top[:, b, 3:4], top[:, b, 2:3])
                        dve.drain()
                        dve.wait_ge(out_full, n + 2)
                        tile = xn[:, bass.ds(b * TB + t, 1), :].rearrange("p a n -> p (a n)")
                        nc.vector.scalar_tensor_tensor(tile, o_ps[:, 0:D], top[:, b, 3:4], tile,
                                                       ALU.mult, ALU.add).then_inc(out_free, 1)


def constants():
    bf = mybir.dt.np(BF16)
    ident = np.eye(P, dtype=np.float32)
    k, q = np.indices((P, P))
    spread_expert = np.zeros((64, 16, P), np.float32)
    for e in range(64):
        spread_expert[e, e // 4, 32 * (e % 4):32 * (e % 4) + 32] = 1.0
    widen = np.zeros((32, 4, P), np.float32)
    for leaf in range(32):
        widen[leaf, leaf // 8, 16 * (leaf % 8):16 * (leaf % 8) + 16] = 1.0
    ranks = np.arange(B * S // 2, dtype=np.float32)
    return {
        "ident": ident,
        "ident_bf": ident.astype(bf),
        "mask_q": np.where(q > k, NEG, 0.0).astype(bf),
        "mask_k": np.where(k > q, NEG, 0.0).astype(bf),
        "widen": widen.astype(bf),
        "iota": np.arange(48, dtype=np.float32),
        "before": np.stack([k < q, k < P], axis=1).astype(bf),
        "spread_expert": spread_expert,
        "rank_row": np.concatenate([np.tile(ranks, (64, 1)), np.tile(ranks + B * S // 2, (64, 1))]),
        "lower": np.tril(np.ones((8, 8), np.float32), -1),
    }


def twice(w):
    return np.ascontiguousarray(np.concatenate([w, w], axis=2))


def stacked(wo):
    return np.ascontiguousarray(np.concatenate([wo, wo], axis=1).transpose(1, 0, 2))


def hidden_tiles(w):
    return np.ascontiguousarray(np.pad(w, ((0, 0), (0, 0), (0, 1))))


def program(nc, a, out, stages=range(8)):
    Scope.SPENT = []
    with Scope(nc, "all") as m:
        x = m.sb("x", [P, NT, D])
        ident = m.sb("ident", [P, P])
        x_in = m.sem("x_in")
        x_out = m.sem("x_out")
        consts = dict(a, ident_sb=ident)
        with nc.Block() as block:
            @block.sync
            def _(sp):
                sp.dma_start(x[:], a["x"].rearrange("b (t p) d -> p (b t) d", p=P)).then_inc(x_in, 16)
                sp.dma_start(ident[:], a["ident"]).then_inc(x_in, 16)
                sp.wait_ge(x_in, 32)
        xT_h = m.sb("xT", [P, B * S])
        xn = m.sb("xn", [P, NT, D])
        if 0 in stages:
            layer_norm(nc, "n0", x, xn, ident, xT_h)
            narrow_attention(nc, "a0", x, xT_h, None,
                             [a[k] for k in ("a0_wq", "a0_wk", "a0_wv", "a0_bq", "a0_bk", "a0_bv", "a0_wo", "a0_bo")],
                             consts, causal=True)
        if 1 in stages:
            recycle(nc)
            layer_norm(nc, "n1", x, xn, ident, xT_h)
            routed_experts(nc, "f1", x, xT_h, {k: a["f1_" + k] for k in
                           ("wr", "br", "wup", "wgate", "wdown", "bdown", "bias")}, consts)
        if 2 in stages:
            recycle(nc)
            layer_norm(nc, "n2", x, xn, ident)
            z = xn
            with Scope(nc, "s2") as t:
                ln = t.sb("ln", [P, 2])
                zz = t.sb("zz", [P, NT, D])
                ln_in = t.sem("ln_in")
                with nc.Block() as block:
                    @block.sync
                    def _(sp):
                        sp.dma_start(ln[:, 0:1], a["a2_ln_w"].rearrange("(p a) -> p a", a=1)).then_inc(ln_in, 16)
                        sp.dma_start(ln[:, 1:2], a["a2_ln_b"].rearrange("(p a) -> p a", a=1)).then_inc(ln_in, 16)
                        sp.wait_ge(ln_in, 32)
                layer_norm(nc, "n2b", z, zz, ident, xT_h, affine=ln)
            narrow_attention(nc, "a2", x, xT_h, z,
                             [a[k] for k in ("a2_wq", "a2_wk", "a2_wv", "a2_bq", "a2_bk", "a2_bv", "a2_wo", "a2_bo")],
                             consts, causal=False)
        if 3 in stages:
            recycle(nc)
            layer_norm(nc, "n3", x, xn, ident)
            layer_norm(nc, "n3b", xn, xn, ident, xT_h, root_of_deviation=True)
            with Scope(nc, "s3") as t:
                q, k, v = (t.sb(f"{k}_tok", [P, NT, D]) for k in "qkv")
                trees = [{n: a[f"f3_{k}_{n}"] for n in ("nw", "nb", "w12", "b2")} for k in ("qkv", "f")]
                leaf_layers(nc, "f3q", xn, xT_h, (q, k, v), trees[0], ACT.Relu, consts)
                single_attention(nc, "a3", xn, xT_h, q, k, v, consts)
                leaf_layers(nc, "f3f", xn, xT_h, (q,), trees[1], ACT.Gelu, consts)
                with nc.Block() as block:
                    @block.vector
                    def _(dve):
                        nc.vector.tensor_tensor(x[:], x[:], xn[:], ALU.add)
                        dve.drain()
                        nc.vector.tensor_tensor(x[:], x[:], q[:], ALU.add)
        if 4 in stages:
            recycle(nc)
            layer_norm(nc, "n4", x, xn, ident, xT_h)
            wide_attention(nc, "a4", x, xT_h, [a[k] for k in ("a4_wq", "a4_wk", "a4_wv", "a4_wo", "a4_bo")],
                           consts, shared_keys=False)
        if 5 in stages:
            recycle(nc)
            layer_norm(nc, "n5", x, xn, ident, xT_h)
            top2_experts(nc, "f5", x, xT_h, a["f5_wg"], a["f5_w1"], a["f5_w2"], a["f5_w3"], a["lower"])
        if 6 in stages:
            recycle(nc)
            layer_norm(nc, "n6", x, xn, ident, xT_h)
            wide_attention(nc, "a6", x, xT_h, [a[k] for k in ("a6_wq", "a6_wk", "a6_wv", "a6_wo", "a6_bo")],
                           consts, shared_keys=True)
        if 7 in stages:
            recycle(nc)
            layer_norm(nc, "n7", x, xn, ident, xT_h)
            binary_linear(nc, "f7", x, xT_h, a["f7_w"], a["f7_scale"], a["f7_bias"])
        with nc.Block() as block:
            @block.sync
            def _(sp):
                sp.dma_start(out.rearrange("b (t p) d -> p (b t) d", p=P), x[:]).then_inc(x_out, 16)
                sp.wait_ge(x_out, 16)


def layout(i):
    c = np.ascontiguousarray
    i = {k: np.asarray(v) for k, v in i.items()}
    a = {"x": i["L0_attn_x"]}
    kv = i["L0_attn_Wkv"]
    a.update(a0_wq=i["L0_attn_Wq"], a0_wk=c(kv[:, :D]), a0_wv=c(kv[:, D:]), a0_bq=i["L0_attn_bq"],
             a0_bk=c(i["L0_attn_bkv"][:D]), a0_bv=c(i["L0_attn_bkv"][D:]), a0_wo=i["L0_attn_Wo"],
             a0_bo=i["L0_attn_bo"])
    w, wb = i["L1_attn_W_qkv"], i["L1_attn_b_qkv"]
    a.update(a2_ln_w=i["L1_attn_ln_w"], a2_ln_b=i["L1_attn_ln_b"],
             a2_wq=c(w[:, :D]), a2_wk=c(w[:, D:2 * D]), a2_wv=c(w[:, 2 * D:]),
             a2_bq=c(wb[:D]), a2_bk=c(wb[D:2 * D]), a2_bv=c(wb[2 * D:]),
             a2_wo=i["L1_attn_W_proj"], a2_bo=i["L1_attn_b_proj"])
    wkv = i["L2_attn_Wkv"]
    a.update(a4_wq=twice(i["L2_attn_Wq"].reshape(D, HEADS, 64)), a4_wk=twice(wkv[:, :1024].reshape(D, HEADS, 64)),
             a4_wv=c(wkv[:, 1024:].reshape(D, HEADS // 2, P)),
             a4_wo=stacked(i["L2_attn_Wo"].reshape(HEADS, 64, D)), a4_bo=i["L2_attn_bo"])
    a.update(a6_wq=twice(i["L3_attn_query_proj"].transpose(2, 0, 1)),
             a6_wk=twice(i["L3_attn_key_proj"].reshape(D, 1, 64)), a6_wv=twice(i["L3_attn_value_proj"].reshape(D, 1, 64)),
             a6_wo=stacked(i["L3_attn_output_proj"].transpose(1, 2, 0)), a6_bo=np.zeros(D, np.float32))
    up, gate = i["L0_ffn_Wup"], i["L0_ffn_Wgate"]
    a.update(f1_wr=i["L0_ffn_Wr"], f1_br=i["L0_ffn_br"], f1_wup=c(up.transpose(1, 0, 2).reshape(D, 2048)),
             f1_wgate=c(gate.transpose(1, 0, 2).reshape(D, 2048)),
             f1_wdown=c(i["L0_ffn_Wdown"].reshape(16, P, D).transpose(1, 0, 2)), f1_bdown=i["L0_ffn_bdown"],
             f1_bias=c(np.stack([i["L0_ffn_bup"].reshape(16, P).T, i["L0_ffn_bgate"].reshape(16, P).T], axis=1)))
    a.update(f5_wg=c(i["L2_ffn_Wg"].T), f5_w1=hidden_tiles(i["L2_ffn_W1"].transpose(0, 2, 1)),
             f5_w2=hidden_tiles(i["L2_ffn_W2"].transpose(0, 2, 1)),
             f5_w3=c(hidden_tiles(i["L2_ffn_W3"]).transpose(0, 2, 1).reshape(8, 3, 114, D).transpose(0, 2, 1, 3)))
    a.update(f7_w=c(i["L3_ffn_weights"].T), f7_scale=i["L3_ffn_scale"], f7_bias=i["L3_ffn_bias"])
    for trees in ("qkv", "f"):
        def stack(part):
            return np.stack([i[f"L1_ffn_{k}_{part}"] for k in trees])
        n = len(trees)
        w1 = stack("w1").reshape(n * 32, 8, D, 16).transpose(0, 2, 1, 3).reshape(n * 32, D, P)
        a.update({
            f"f3_{trees}_nw": c(np.pad(stack("nw").transpose(0, 2, 1), ((0, 0), (0, 0), (0, 1)))),
            f"f3_{trees}_nb": c(np.pad(stack("nb"), ((0, 0), (0, 1)))),
            f"f3_{trees}_w12": np.concatenate([w1, stack("w2").reshape(n * 32, P, D),
                                               stack("b1").reshape(n * 32, P, 1)], axis=2),
            f"f3_{trees}_b2": c(stack("b2").reshape(n * 256, D)),
        })
    a.update(constants())
    return a


def kernel(**inputs):
    import concourse.bacc as bacc
    from concourse.bass_utils import run_bass_kernel_spmd

    nc = bacc.Bacc("TRN2", target_bir_lowering=False, num_devices=1)
    arrays = {f"in_{k}": np.ascontiguousarray(v) for k, v in layout(inputs).items()}
    args = {k[3:]: nc.dram_tensor(k, v.shape, mybir.dt.from_np(v.dtype), kind="ExternalInput").ap()
            for k, v in arrays.items()}
    out = nc.dram_tensor("out_x", (B, S, D), F32, kind="ExternalOutput").ap()
    program(nc, args, out)
    r = run_bass_kernel_spmd(nc, [arrays], core_ids=[0])
    return r.results[0]["out_x"]
```

```python
from contextlib import ExitStack

import numpy as np
import concourse.bass as bass
from concourse import mybir
from concourse.alu_op_type import AluOpType as ALU

ACT = mybir.ActivationFunctionType
F32 = mybir.dt.float32
BF16 = mybir.dt.bfloat16
AX_X = mybir.AxisListType.X

P = 128
B, S, D = 2, 1024, 128
NT = B * S // P
TB = S // P
W = 512
NG = B * S // W
HEADS = 16
NEG = -1e30


class Scope:

    SPENT = []

    def __init__(self, nc, name):
        self.nc, self.name, self.ctx, self.sems = nc, name, ExitStack(), []

    def __enter__(self):
        return self

    def __exit__(self, *e):
        Scope.SPENT += self.sems
        return self.ctx.__exit__(*e)

    def sb(self, name, shape, dt=F32):
        return self.ctx.enter_context(self.nc.sbuf_tensor(f"{self.name}_{name}", shape, dt))

    def ps(self, name, shape, dt=F32):
        return self.ctx.enter_context(self.nc.psum_tensor(f"{self.name}_{name}", shape, dt))

    def sem(self, name):
        self.sems.append(self.nc.alloc_semaphore(f"{self.name}_{name}"))
        return self.sems[-1]


def recycle(nc):
    nc.clear_and_free_semaphores(Scope.SPENT)
    Scope.SPENT = []
    nc.all_engine_barrier()


def layer_norm(nc, name, src, dst, ident, xT=None, affine=None, root_of_deviation=False, loads=(),
               eps=1e-5):
    HALF = NT // 2
    with Scope(nc, name) as m:
        stats = m.sb("stats", [P, NT, 6])
        moments = m.sb("moments", [P, NT, 2])
        power = m.sb("power", [P, 2, NT])
        spread = m.sb("spread", [P, NT])
        turned = m.ps("turned", [P, NG, W])
        moments_ready = m.sem("moments_ready")
        rstd_ready = m.sem("rstd_ready")
        tile_normed = m.sem("tile_normed")
        group_turned = m.sem("group_turned")
        loads_in = m.sem("loads_in")

        with nc.Block() as block:
            if loads:
                @block.sync
                def _(sp):
                    for to, frm in loads:
                        sp.dma_start(to, frm).then_inc(loads_in, 16)
                    sp.wait_ge(loads_in, 16 * len(loads))

            @block.vector
            def _(dve):
                for h in range(2):
                    tiles = range(h * HALF, (h + 1) * HALF)
                    for t in tiles:
                        nc.vector.bn_stats(stats[:, t, :], src[:, t, :])
                    dve.drain()
                    for t in tiles:
                        last = nc.vector.bn_aggr(moments[:, t, :], stats[:, t, :])
                    last.then_inc(moments_ready, 1)
                for h in range(2):
                    dve.wait_ge(rstd_ready, h + 1)
                    for t in range(h * HALF, (h + 1) * HALF):
                        nc.vector.tensor_scalar(dst[:, t, :], src[:, t, :], moments[:, t, 0:1], spread[:, t:t + 1],
                                                ALU.subtract, ALU.mult).then_inc(tile_normed, 1)

            @block.gpsimd
            def _(pool):
                nc.gpsimd.memset(power[:, 0, :], -0.5)
                nc.gpsimd.memset(power[:, 1, :], 0.5)
                for h in range(2):
                    half = slice(h * HALF, (h + 1) * HALF)
                    to, variance = spread[:, half], moments[:, half, 1]
                    pool.drain()
                    pool.wait_ge(moments_ready, h + 1)
                    if root_of_deviation:
                        nc.gpsimd.tensor_scalar(to, variance, D / (D - 1.0), None, ALU.mult)
                        pool.drain()
                        nc.gpsimd.tensor_tensor(to, to, power[:, 1, half], ALU.pow)
                        pool.drain()
                        nc.gpsimd.tensor_scalar(to, to, eps, None, ALU.add)
                    else:
                        nc.gpsimd.tensor_scalar(to, variance, eps, None, ALU.add)
                    pool.drain()
                    nc.gpsimd.tensor_tensor(to, to, power[:, 0, half], ALU.pow).then_inc(rstd_ready, 1)

            if xT is not None:
                @block.tensor
                def _(pe):
                    for g in range(NG):
                        pe.wait_ge(tile_normed, 4 * g + 4)
                        for c in range(4):
                            last = nc.tensor.transpose(turned[:, g, c * P:(c + 1) * P], dst[:, 4 * g + c, :], ident[:])
                        last.then_inc(group_turned, 1)

                @block.scalar
                def _(act):
                    for g in range(NG):
                        act.wait_ge(group_turned, g + 1)
                        to, frm = xT[:, g * W:(g + 1) * W], turned[:, g, :]
                        if affine is None:
                            nc.scalar.copy(to, frm)
                        else:
                            nc.scalar.activation(to, frm, ACT.Identity, bias=affine[:, 1:2], scale=affine[:, 0:1])


def narrow_attention(nc, name, x, xT, residual, weights, consts, causal, norm):
    DH, HG = 8, 4
    G = HEADS // HG
    ROWS, STACK = 9 * DH, 96
    SCALE = DH ** -0.5
    wq, wk, wv, bq, bk, bv, wo, bo = weights
    q_dram = nc.dram_tensor(f"{name}_q_parts", [P, 3, B * S], BF16, kind="Internal").ap()
    k_dram = nc.dram_tensor(f"{name}_k_parts", [P, 3, B * S], BF16, kind="Internal").ap()
    with Scope(nc, name) as outer:
        v_tok = outer.sb("v_tok", [P, NT, P])
        wo_sb = outer.sb("wo_sb", [P, P])
        attended = outer.sb("attended", [P, NT, P])

        with Scope(nc, name + "p") as m:
            w_sb = m.sb("w_sb", [P, 3, P])
            b_col = m.sb("b_col", [P, 2])
            b_row = m.sb("b_row", [P, 2, P])
            full = m.sb("full", [P, 2, B * S])
            rest = m.sb("rest", [P, B * S])
            parts = m.sb("parts", [P, 2, 3, B * S], BF16)
            norm([(w_sb[:, n, :], w) for n, w in enumerate((wq, wk, wv))]
                 + [(b_col[:, n:n + 1], b.rearrange("(p a) -> p a", a=1)) for n, b in enumerate((bq, bk))]
                 + [(b_row[:, n, :], b.partition_broadcast(P)) for n, b in enumerate((bv, bo))] + [(wo_sb[:], wo)])
            qk_ps = m.ps("qk_ps", [P, 4, W])
            v_ps = m.ps("v_ps", [P, NG, W])
            qk_made = m.sem("qk_made")
            qk_moved = m.sem("qk_moved")
            v_made = m.sem("v_made")
            parts_ready = m.sem("parts_ready")
            stored = m.sem("stored")
            with nc.Block() as block:
                @block.sync
                def _(sp):
                    for n, dram in enumerate((q_dram, k_dram)):
                        sp.wait_ge(parts_ready, n + 1)
                        sp.dma_start(dram, parts[:, n, :, :]).then_inc(stored, 16)
                    sp.wait_ge(stored, 32)

                @block.tensor
                def _(pe):
                    for n in range(2):
                        for g in range(NG):
                            if n:
                                pe.wait_ge(qk_moved, g + 1)
                            nc.tensor.matmul(qk_ps[:, g, :], w_sb[:, n, :], xT[:, g * W:(g + 1) * W],
                                             start=True, stop=True).then_inc(qk_made, 1)
                    for t in range(NT):
                        nc.tensor.matmul(v_ps[:, t // 4, t % 4 * P:(t % 4 + 1) * P], xT[:, t * P:(t + 1) * P],
                                         w_sb[:, 2, :], start=True, stop=True).then_inc(v_made, 1)

                @block.scalar
                def _(act):
                    for n in range(2):
                        for g in range(NG):
                            act.wait_ge(qk_made, NG * n + g + 1)
                            nc.scalar.activation(full[:, n, g * W:(g + 1) * W], qk_ps[:, g, :], ACT.Identity,
                                                 bias=b_col[:, n:n + 1]).then_inc(qk_moved, 1)

                @block.vector
                def _(dve):
                    wide_bo = b_row[:, 1:2, :].to_broadcast([P, NT, P])
                    nc.vector.tensor_tensor(x[:], x[:], wide_bo, ALU.add)
                    if residual is not None:
                        dve.drain()
                        nc.vector.tensor_tensor(x[:], x[:], residual[:], ALU.add)
                    for n in range(2):
                        dve.wait_ge(qk_moved, NG * (n + 1))
                        high, mid, low = (parts[:, n, c, :] for c in range(3))
                        nc.vector.tensor_copy(high, full[:, n, :])
                        dve.drain()
                        nc.vector.tensor_tensor(rest[:], full[:, n, :], high, ALU.subtract)
                        dve.drain()
                        nc.vector.tensor_copy(mid, rest[:])
                        dve.drain()
                        nc.vector.tensor_tensor(low, rest[:], mid, ALU.subtract).then_inc(parts_ready, 1)
                        dve.drain()
                    for g in range(NG):
                        dve.wait_ge(v_made, 4 * g + 4)
                        nc.vector.tensor_tensor(v_tok[:, 4 * g:4 * g + 4, :],
                                                v_ps[:, g, :].rearrange("p (t n) -> p t n", n=P),
                                                b_row[:, 0:1, :].to_broadcast([P, 4, P]), ALU.add)

        NQ = S // W
        steps = [(Q, k) for Q in range(NQ) for k in range(4 * Q + 4 if causal else TB)]
        NS = len(steps)
        chunks = [(j, qt, c) for j in range(HG) for qt in range(TB) for c in range(2)
                  if not causal or c * W < (qt + 1) * P]
        NCH = len(chunks)
        n_steps = NS - 3
        share = -(-NCH // n_steps)
        R = 4
        with Scope(nc, name + "m") as m:
            qs = [m.sb(f"qs{r}", [STACK, HG, S], BF16) for r in range(R)]
            ks = [m.sb(f"ks{r}", [STACK, HG, S], BF16) for r in range(R)]
            vb = [m.sb(f"vb{b}", [P, TB, HG, 32]) for b in range(B)]
            plain = m.sb("plain", [3, 2, HG * S], BF16)
            mask = m.sb("mask", [P, 3, P], BF16)
            probs = m.sb("probs", [P, 2, HG, W])
            part_max = m.sb("part_max", [P, 2, HG * TB])
            neg_max = m.sb("neg_max", [P, HG * TB])
            shift = m.sb("shift", [HG * TB, 2, P])
            shift_parts = m.sb("shift_parts", [HG * TB, 3, P], BF16)
            sums = m.sb("sums", [P, W])
            recip = m.sb("recip", [P, 4, HG])
            s_ps = m.ps("s_ps", [P, HG, W])
            m_ps = m.ps("m_ps", [P, 2, W])
            o_ps = m.ps("o_ps", [P, W])
            misc = m.ps("misc", [P, W])
            stacks_cleared = m.sem("stacks_cleared")
            plain_set = m.sem("plain_set")
            constants_in = m.sem("constants_in")
            stacks_in = [m.sem(f"stacks_in{r}") for r in range(R)]
            shift_in = m.sem("shift_in")
            v_in = m.sem("v_in")
            scores_ready = m.sem("scores_ready")
            probs_ready = m.sem("probs_ready")
            probs_free = m.sem("probs_free")
            max_full = m.sem("max_full")
            max_free = m.sem("max_free")
            neg_max_ready = m.sem("neg_max_ready")
            shift_ready = m.sem("shift_ready")
            out_full = m.sem("out_full")
            out_free = m.sem("out_free")
            misc_full = m.sem("misc_full")
            misc_free = m.sem("misc_free")

            def load_unit(sp, u, r, b, g):
                if not (isinstance(u, int) and u < R):
                    sp.wait_ge(probs_free, (u - R + 1) * NS + 2)
                for j in range(HG):
                    at = bass.ds(g * (HG * DH) + j * DH, DH)
                    for a in range(3):
                        src = q_dram[at, a, b * S:(b + 1) * S]
                        sp.dma_start(qs[r][3 * DH * a:3 * DH * (a + 1), j, :],
                                     src[:, None, :].to_broadcast([DH, 3, S])).then_inc(stacks_in[r], 16)
                    src = k_dram[at, :, b * S:(b + 1) * S].rearrange("d c n -> (d c) n")
                    sp.dma_start(ks[r][0:ROWS, j, :],
                                 src[None, :, :].to_broadcast([3, 3 * DH, S])).then_inc(stacks_in[r], 16)
                if isinstance(u, int) and u == 0:
                    sp.wait_ge(plain_set, 1)
                sp.dma_start(qs[r][ROWS:ROWS + 3, :, :].rearrange("p h n -> p (h n)"),
                             plain[:, 0, :]).then_inc(stacks_in[r], 16)

            N_LOADS = 4 * HG + 1

            def load_shift(sp, u, r):
                sp.wait_ge(shift_ready, u + 1)
                for c in range(3):
                    sp.dma_start(qs[r][ROWS + c:ROWS + c + 1, :, :].rearrange("p h n -> p (h n)"),
                                 shift_parts[:, c, :]).then_inc(shift_in, 16)

            def pe_max(pe, u, r, which):
                for i, (j, qt, c) in which:
                    pe.wait_ge(max_free, u * NCH + i + 1)
                    end = min(W, (qt + 1) * P - c * W) if causal else W
                    diagonal = causal and c * W <= qt * P < (c + 1) * W
                    mm = nc.tensor.matmul(m_ps[:, i % 2, 0:end], qs[r][:, j, qt * P:(qt + 1) * P],
                                          ks[r][:, j, c * W:c * W + end], start=True, stop=not diagonal)
                    if diagonal:
                        mm = nc.tensor.matmul(m_ps[:, i % 2, end - P:end], mask[:, 0, :], mask[:, 1, :],
                                              start=False, stop=True)
                    mm.then_inc(max_full, 1)

            def dve_max(dve, u, which):
                for i, (j, qt, c) in which:
                    dve.wait_ge(max_full, u * NCH + i + 1)
                    end = min(W, (qt + 1) * P - c * W) if causal else W
                    col = j * TB + qt
                    nc.vector.tensor_reduce(part_max[:, c, col:col + 1], m_ps[:, i % 2, 0:end], AX_X,
                                            ALU.max).then_inc(max_free, 1)

            def pe_turn_max(pe, u, use):
                pe.wait_ge(neg_max_ready, u + 1)
                pe.wait_ge(misc_free, use + 1)
                nc.tensor.transpose(misc[0:HG * TB, 0:P], neg_max[:], consts["ident_sb"][:]).then_inc(misc_full, 1)

            def dve_neg_max(dve, u):
                dve.drain()
                nc.vector.tensor_tensor(neg_max[:], part_max[:, 0, :], part_max[:, 1, :], ALU.max)
                dve.drain()
                nc.vector.tensor_scalar(neg_max[:], neg_max[:], -1.0, None, ALU.mult).then_inc(neg_max_ready, 1)

            def dve_split_shift(dve, u, use):
                dve.wait_ge(misc_full, use + 1)
                dve.wait_ge(shift_in, 48 * u + 48)
                nc.vector.tensor_copy(shift[:, 0, :], misc[0:HG * TB, 0:P]).then_inc(misc_free, 1)
                dve.drain()
                nc.vector.tensor_copy(shift_parts[:, 0, :], shift[:, 0, :])
                dve.drain()
                nc.vector.tensor_tensor(shift[:, 1, :], shift[:, 0, :], shift_parts[:, 0, :], ALU.subtract)
                dve.drain()
                nc.vector.tensor_copy(shift_parts[:, 1, :], shift[:, 1, :])
                dve.drain()
                nc.vector.tensor_tensor(shift_parts[:, 2, :], shift[:, 1, :], shift_parts[:, 1, :],
                                        ALU.subtract).then_inc(shift_ready, 1)

            def pe_scores(pe, u, r, n, j):
                Q, k = steps[n]
                lo = max(0, k - 4 * Q) * P if causal else 0
                if n:
                    pe.wait_ge(probs_ready, (u * NS + n - 1) * HG + j + 1)
                diagonal = causal and k >= 4 * Q
                mm = nc.tensor.matmul(s_ps[:, j, lo:W], ks[r][:, j, k * P:(k + 1) * P],
                                      qs[r][:, j, Q * W + lo:(Q + 1) * W], start=True, stop=not diagonal)
                if diagonal:
                    mm = nc.tensor.matmul(s_ps[:, j, lo:lo + P], mask[:, 0, :], mask[:, 2, :],
                                          start=False, stop=True)
                mm.then_inc(scores_ready, 1)

            def pe_sums(pe, u, b, n):
                Q, k = steps[n]
                lo = max(0, k - 4 * Q) * P if causal else 0
                last_k = n + 1 == NS or steps[n + 1][0] != Q
                if k == 0:
                    pe.wait_ge(out_free, u * NQ + Q + 1)
                for j in range(HG):
                    pe.wait_ge(probs_ready, (u * NS + n) * HG + j + 1)
                    mm = nc.tensor.matmul(o_ps[32 * j:32 * j + 32, lo:W], vb[b][:, k, j, :], probs[:, n % 2, j, lo:W],
                                          start=(k == 0), stop=last_k)
                mm.then_inc(probs_free, 1)

            def dve_evacuate(dve, u, Q):
                dve.wait_ge(probs_free, u * NS + q_end[Q] + 1 + 2)
                nc.vector.tensor_copy(sums[:], o_ps[:]).then_inc(out_free, 1)

            def pe_turn_sums(pe, u, Q, use):
                pe.wait_ge(out_free, u * NQ + Q + 2)
                pe.wait_ge(misc_free, use + 1)
                for c in range(4):
                    mm = nc.tensor.transpose(misc[:, c * P:(c + 1) * P], sums[:, c * P:(c + 1) * P],
                                             consts["ident_sb"][:])
                mm.then_inc(misc_full, 1)

            def dve_normalize(dve, b, g, Q, use):
                dve.wait_ge(misc_full, use + 1)
                by_head = misc[:].rearrange("p (t j n) -> p t j n", t=4, j=HG)
                nc.vector.reciprocal(recip[:], by_head[:, :, :, DH])
                dve.drain()
                at = attended[:, b * TB + 4 * Q:b * TB + 4 * Q + 4, :]
                at = at[:, :, g * HG * DH:(g + 1) * HG * DH] if isinstance(g, int) else \
                    at[:, :, bass.ds(g * (HG * DH), HG * DH)]
                nc.vector.tensor_tensor(at.rearrange("p t (j n) -> p t j n", j=HG), by_head[:, :, :, 0:DH],
                                        recip[:, :, :, None].to_broadcast([P, 4, HG, DH]),
                                        ALU.mult).then_inc(misc_free, 1)

            q_end = [max(n for n in range(NS) if steps[n][0] == Q) for Q in range(NQ)]
            numbered = [list(enumerate(chunks))[i * share:(i + 1) * share] for i in range(n_steps)]

            def misc_use(u, i):
                return 3 * u + i

            def all_slots(engine, slot):
                def round_of(i, last):
                    for r in range(R):
                        nxt = None if last and r == R - 1 else ((r + 1) % R, i + (r + 1) // R)
                        slot(R * i + r, r, r % B, (R // B) * i + r // B, nxt)

                with engine.Fori(0, B * G // R - 1) as i:
                    round_of(i, False)
                round_of(B * G // R - 1, True)

            with nc.Block() as block:
                @block.sync
                def _(sp):
                    sp.dma_start(mask[:, 0, :], consts["ident_bf"]).then_inc(constants_in, 16)
                    sp.dma_start(mask[:, 1, :], consts["mask_q"]).then_inc(constants_in, 16)
                    sp.dma_start(mask[:, 2, :], consts["mask_k"]).then_inc(constants_in, 16)
                    sp.wait_ge(stacks_cleared, 1)
                    load_unit(sp, 0, 0, 0, 0)
                    sp.wait_ge(stacks_cleared, R - 1)
                    sp.wait_ge(plain_set, 2)
                    for r in range(R):
                        sp.dma_start(ks[r][ROWS:ROWS + 3, :, :].rearrange("p h n -> p (h n)"),
                                     plain[:, 1, :]).then_inc(constants_in, 16)
                    load_unit(sp, 1, 1, 1, 0)
                    load_shift(sp, 0, 0)

                    def slot(u, r, b, g, nxt):
                        if nxt and not (isinstance(u, int) and u == B * G - 2):
                            load_unit(sp, u + 2, (r + 2) % R, b, g + 1)
                        if nxt:
                            load_shift(sp, u + 1, nxt[0])

                    all_slots(sp, slot)

                @block.gpsimd
                def _(pool):
                    nc.gpsimd.memset(plain[:, 0, :], 0.0)
                    nc.gpsimd.memset(plain[:, 1, :], 1.0)
                    pool.drain()
                    pool.sem_inc(plain_set, 1)
                    nc.gpsimd.memset(qs[R - 1][64:STACK, :, :], 0.0)
                    pool.drain()
                    nc.gpsimd.memset(ks[R - 1][64:STACK, :, :], 0.0)
                    pool.drain()
                    pool.sem_inc(plain_set, 1)
                    for b in range(B):
                        nc.gpsimd.memset(vb[b][:, :, :, DH + 1:32], 0.0)
                        nc.gpsimd.memset(vb[b][:, :, :, DH:DH + 1], 1.0)
                    pool.drain()
                    def fill(u, b, g):
                        for j in range(HG):
                            nc.gpsimd.tensor_copy(vb[b][:, :, j, 0:DH],
                                                         v_tok[:, b * TB:(b + 1) * TB,
                                                               bass.ds(g * (HG * DH) + j * DH, DH)])
                        pool.drain()
                        pool.sem_inc(v_in, 1)

                    for b in range(B):
                        fill(b, b, 0)
                    with pool.Fori(1, G) as g:
                        for b in range(B):
                            pool.wait_ge(probs_free, (2 * g + b - 1) * NS + 2)
                            fill(2 * g + b, b, g)

                @block.tensor
                def _(pe):
                    pe.sem_inc(probs_free, 2)
                    pe.wait_ge(constants_in, 16 * (R + 3))
                    pe.wait_ge(stacks_in[0], 16 * N_LOADS)
                    pe_max(pe, 0, 0, list(enumerate(chunks)))
                    pe_turn_max(pe, 0, misc_use(0, 0))

                    def slot(u, r, b, g, nxt):
                        if nxt:
                            pe.wait_ge(stacks_in[nxt[0]], 16 * N_LOADS * (nxt[1] + 1))
                            pe_max(pe, u + 1, nxt[0], numbered[0])
                        pe.wait_ge(shift_in, 48 * u + 96)
                        for j in range(HG):
                            pe_scores(pe, u, r, 0, j)
                        pe.wait_ge(v_in, u + 1)
                        for n in range(NS):
                            maxima = numbered[n + 1] if nxt and n + 1 < n_steps else []
                            for j in range(HG):
                                if n + 1 < NS:
                                    pe_scores(pe, u, r, n + 1, j)
                                pe_max(pe, u + 1, nxt and nxt[0], maxima[j:j + 1])
                            if n == 1 and not (isinstance(u, int) and u == 0):
                                pe_turn_sums(pe, u - 1, NQ - 1, misc_use(u, 0))
                            if n == q_end[0] + 2:
                                pe_turn_sums(pe, u, 0, misc_use(u, 1))
                            pe_sums(pe, u, b, n)
                            if nxt:
                                pe_max(pe, u + 1, nxt[0], maxima[HG:])
                                if n == n_steps - 1:
                                    pe_turn_max(pe, u + 1, misc_use(u, 2))

                    all_slots(pe, slot)
                    pe_turn_sums(pe, B * G - 1, NQ - 1, misc_use(B * G - 1, 2))

                @block.scalar
                def _(act):
                    def slot(u):
                        for n, (Q, k) in enumerate(steps):
                            lo = max(0, k - 4 * Q) * P if causal else 0
                            act.wait_ge(probs_free, u * NS + n + 1)
                            for j in range(HG):
                                act.wait_ge(scores_ready, (u * NS + n) * HG + j + 1)
                                nc.scalar.activation(probs[:, n % 2, j, lo:W], s_ps[:, j, lo:W], ACT.Exp,
                                                     scale=SCALE).then_inc(probs_ready, 1)

                    with act.Fori(0, B * G) as u:
                        slot(u)

                @block.vector
                def _(dve):
                    for r in range(R - 1):
                        nc.vector.memset(qs[r][64:STACK, :, :], 0.0)
                        nc.vector.memset(ks[r][64:STACK, :, :], 0.0).then_inc(stacks_cleared, 1)
                    nc.vector.memset(part_max[:], NEG)
                    dve.sem_inc(max_free, 2)
                    dve.sem_inc(misc_free, 1)
                    dve.sem_inc(out_free, 1)
                    dve.sem_inc(shift_in, 48)
                    dve.drain()
                    dve_max(dve, 0, list(enumerate(chunks)))
                    dve_neg_max(dve, 0)
                    dve_split_shift(dve, 0, misc_use(0, 0))

                    def slot(u, r, b, g, nxt):
                        before = None if isinstance(u, int) and u == 0 else (1 - b, g if b else g - 1)
                        if nxt:
                            dve_max(dve, u + 1, numbered[0])
                        for n in range(NS):
                            maxima = numbered[n + 1] if nxt and n + 1 < n_steps else []
                            dve_max(dve, u + 1, maxima[0:1])
                            if n == 0 and before:
                                dve_evacuate(dve, u - 1, NQ - 1)
                            if n == q_end[0] + 1:
                                dve_evacuate(dve, u, 0)
                            dve_max(dve, u + 1, maxima[1:])
                            if n == 1 and before:
                                dve_normalize(dve, *before, NQ - 1, misc_use(u, 0))
                            if n == q_end[0] + 2:
                                dve_normalize(dve, b, g, 0, misc_use(u, 1))
                            if nxt and n == n_steps - 2:
                                dve_neg_max(dve, u + 1)
                            if nxt and n == n_steps - 1:
                                dve_split_shift(dve, u + 1, misc_use(u, 2))

                    all_slots(dve, slot)
                    dve_evacuate(dve, B * G - 1, NQ - 1)
                    dve_normalize(dve, B - 1, G - 1, NQ - 1, misc_use(B * G - 1, 2))

        with Scope(nc, name + "o") as m:
            t_ps = m.ps("t_ps", [P, 4, W])
            y_ps = m.ps("y_ps", [P, NG, W])
            turned = m.sem("turned")
            copied = m.sem("copied")
            projected = m.sem("projected")
            with nc.Block() as block:
                @block.tensor
                def _(pe):
                    for g in range(NG):
                        for c in range(4):
                            mm = nc.tensor.transpose(t_ps[:, g, c * P:(c + 1) * P], attended[:, 4 * g + c, :],
                                                     consts["ident_sb"][:])
                        mm.then_inc(turned, 1)
                    for g in range(NG):
                        pe.wait_ge(copied, g + 1)
                        for c in range(4):
                            t = 4 * g + c
                            mm = nc.tensor.matmul(y_ps[:, g, c * P:(c + 1) * P], xT[:, t * P:(t + 1) * P], wo_sb[:],
                                                  start=True, stop=True)
                        mm.then_inc(projected, 1)

                @block.scalar
                def _(act):
                    for g in range(NG):
                        act.wait_ge(turned, g + 1)
                        nc.scalar.copy(xT[:, g * W:(g + 1) * W], t_ps[:, g, :]).then_inc(copied, 1)

                @block.vector
                def _(dve):
                    for g in range(NG):
                        dve.wait_ge(projected, g + 1)
                        xg = x[:, 4 * g:4 * g + 4, :].rearrange("p t n -> p (t n)")
                        nc.vector.tensor_tensor(xg, y_ps[:, g, :], xg, ALU.add)


def wide_attention(nc, name, x, xT, weights, consts, shared_keys, norm):
    DH = 64
    SCALE = DH ** -0.5
    wq, wk, wv, wo, bo = weights
    NH_K, NH_V = (1, 1) if shared_keys else (HEADS, HEADS // 2)
    NB = 8
    NQ = S // W
    steps = [(Q, k) for Q in range(NQ) for k in range(TB)]
    NS = len(steps)
    chunks = [(qt, c) for qt in range(TB) for c in range(2)]
    NCH = len(chunks)
    MAX_AT = 5
    TURN_AT = MAX_AT + 8
    AHEAD, JOB_AT = 1, (0, 0, 2, 4)
    OWN_AT = (TB + 2, NS - 1)
    with Scope(nc, name) as m:
        wq_all = m.sb("wq_all", [P, HEADS, DH])
        wk_all = m.sb("wk_all", [P, NH_K, DH])
        wv_all = m.sb("wv_all", [P, NH_V, 2 * DH])
        wo_all = m.sb("wo_all", [P, HEADS, D])
        ones = m.sb("ones", [P, P])
        w_now = m.sb("w_now", [P, 2, DH])
        bo_row = m.sb("bo_row", [P, D])
        qf = [m.sb(f"qf{b}", [P, S]) for b in range(B)]
        kf = [m.sb(f"kf{b}", [P, S]) for b in range(B)]
        qm = [m.sb(f"qm{b}", [P, S], BF16) for b in range(B)]
        kh = [m.sb(f"kh{b}", [P, S], BF16) for b in range(B)]
        km = [m.sb(f"km{b}", [P, S], BF16) for b in range(B)]
        vb = [m.sb(f"vb{b}", [P, TB, 2, DH]) for b in range(B)]
        probs = m.sb("probs", [P, NB, W])
        added = m.sb("added", [P, 2, W])
        den = m.sb("den", [P, W])
        part_max = m.sb("part_max", [P, 2, TB])
        neg_max = m.sb("neg_max", [P, TB])
        shift = m.sb("shift", [TB, P])
        sums = m.sb("sums", [P, W])
        recip = m.sb("recip", [P, 2])
        norm([(wq_all[:], wq), (wk_all[:], wk), (wv_all[:], wv), (wo_all[:], wo),
              (bo_row[:], bo.partition_broadcast(P))])
        s_ps = m.ps("s_ps", [P, 2, W])
        m_ps = m.ps("m_ps", [P, 2, W])
        o_ps = m.ps("o_ps", [P, W])
        p_ps = m.ps("p_ps", [P, 2, W])
        misc = m.ps("misc", [P, W])
        constants_set = m.sem("constants_set")
        weights_now = m.sem("weights_now")
        proj_full = m.sem("proj_full")
        proj_free = m.sem("proj_free")
        pieces_made = m.sem("pieces_made")
        shift_ready = m.sem("shift_ready")
        shift_in = m.sem("shift_in")
        scores_ready = m.sem("scores_ready")
        probs_ready = m.sem("probs_ready")
        probs_free = m.sem("probs_free")
        probs_added = m.sem("probs_added")
        den_ready = m.sem("den_ready")
        max_full = m.sem("max_full")
        max_free = m.sem("max_free")
        neg_max_ready = m.sem("neg_max_ready")
        out_free = m.sem("out_free")
        misc_full = m.sem("misc_full")
        misc_free = m.sem("misc_free")

        def jobs(first, e):
            made = [("q", 0)]
            if first or not shared_keys:
                made += [("k", 0)]
            if first or (not shared_keys and e == 0):
                made += [("v", c) for c in range(2)]
            return made

        def job_index(hp, e, b, i):
            if shared_keys:
                u = 4 * hp + 2 * e + b
                return 4 * u + i if isinstance(hp, int) and u < 2 else 6 + u + i
            return 12 * hp + (0, 4, 8, 10)[2 * e + b] + i

        def pieces(first, e):
            return [p for w, _ in jobs(first, e) if w in "qk" for p in ((w, 0), (w, 1))] \
                + [p for p in jobs(first, e) if p[0] == "v"]

        def piece_index(hp, e, b, p):
            if shared_keys:
                u = 4 * hp + 2 * e + b
                return 6 * u + p if isinstance(hp, int) and u < 2 else 8 + 2 * u + p
            return 20 * hp + (0, 6, 12, 16)[2 * e + b] + p

        def misc_use(u, i):
            return 5 * u - 1 + i

        with nc.Block() as block:
            @block.sync
            def _(sp):
                sp.wait_ge(constants_set, 1)
                with sp.Fori(0, HEADS) as h:
                    for b in range(B):
                        sp.wait_ge(shift_ready, 2 * h + b + 1)
                        sp.dma_start(qf[b][DH:DH + 1, :], shift[:]).then_inc(shift_in, 16)

            @block.gpsimd
            def _(pool):
                def fetch(h):
                    for n, w in enumerate((wq_all, wk_all)):
                        if n == 0 or not shared_keys or (isinstance(h, int) and h == 0):
                            nc.gpsimd.tensor_copy(w_now[:, n, :], w[:, h, :] if isinstance(h, int)
                                                  else w[:, bass.ds(h, 1), :].rearrange("p a n -> p (a n)"))
                    pool.drain()
                    pool.sem_inc(weights_now, 1)

                fetch(0)
                nc.gpsimd.memset(ones[:], 1.0)
                pool.drain()
                for b in range(B):
                    nc.gpsimd.memset(qf[b][DH:P, :], 0.0)
                    pool.drain()
                    nc.gpsimd.memset(kf[b][DH:P, :], 0.0)
                    pool.drain()
                    nc.gpsimd.memset(kf[b][DH:DH + 1, :], 1.0)
                    pool.drain()
                pool.sem_inc(constants_set, 1)

                def after(hp, e):
                    pool.wait_ge(proj_full, job_index(hp, e, 0, 0))
                    fetch(2 * hp + e)

                after(0, 1)
                with pool.Fori(1, HEADS // 2) as hp:
                    after(hp, 0)
                    after(hp, 1)

            def job_bank(hp, e, b, i):
                if shared_keys:
                    u = 2 * e + b
                    return p_ps[:, (i if isinstance(hp, int) and hp == 0 and u < 2 else u + i) % 2, :]
                return p_ps[:, i % 2, :]

            def pe_job(pe, hp, e, b, i, what, c):
                pe.wait_ge(proj_free, job_index(hp, e, b, i) + 1)
                bank = job_bank(hp, e, b, i)
                if what in "qk":
                    for half in range(2):
                        at = b * S + half * W
                        mm = nc.tensor.matmul(bank[half * DH:(half + 1) * DH, :], w_now[:, "qk".index(what), :],
                                              xT[:, at:at + W], start=True, stop=True)
                    mm.then_inc(proj_full, 1)
                else:
                    hv = 0 if shared_keys else hp
                    for j in range(4):
                        t = b * TB + 4 * c + j
                        rhs = wv_all[:, hv, :] if isinstance(hv, int) else \
                            wv_all[:, bass.ds(hv, 1), :].rearrange("p a n -> p (a n)")
                        mm = nc.tensor.matmul(bank[:, j * P:(j + 1) * P], xT[:, t * P:(t + 1) * P],
                                              rhs, start=True, stop=True)
                    mm.then_inc(proj_full, 1)

            def act_piece(act, hp, e, b, p, what, c):
                i = {"q": 0, "k": 1, "v": 2 + c}[what]
                act.wait_ge(proj_full, job_index(hp, e, b, i) + 1)
                bank = job_bank(hp, e, b, i)
                if what == "v":
                    last = nc.scalar.copy(vb[b][:, 4 * c:4 * c + 4, :, :].rearrange("p t e n -> p (t e n)"), bank)
                else:
                    src, cols = bank[c * DH:(c + 1) * DH, :], slice(c * W, (c + 1) * W)
                    nc.scalar.copy((qf if what == "q" else kf)[b][0:DH, cols], src)
                    last = nc.scalar.copy((qm if what == "q" else kh)[b][0:DH, cols], src)
                    if what == "k":
                        last = nc.scalar.copy(kh[b][DH:P, cols], src)
                last.then_inc(pieces_made, 1)

            def dve_piece(dve, hp, e, b, p, what, c):
                if what == "v":
                    dve.drain()
                dve.wait_ge(pieces_made, piece_index(hp, e, b, p) + 1)
                if what == "v":
                    dve.sem_inc(proj_free, 1)
                    return
                bank = job_bank(hp, e, b, "qk".index(what))
                src, cols = bank[c * DH:(c + 1) * DH, :], slice(c * W, (c + 1) * W)
                if what == "q":
                    last = nc.vector.tensor_tensor(qm[b][DH:P, cols], src, qm[b][0:DH, cols], ALU.subtract)
                else:
                    for to in range(2):
                        last = nc.vector.tensor_tensor(km[b][to * DH:(to + 1) * DH, cols], src,
                                                       kh[b][0:DH, cols], ALU.subtract)
                if c:
                    last.then_inc(proj_free, 1)

            def pe_max(pe, u, b, which):
                for i in which:
                    qt, c = chunks[i]
                    pe.wait_ge(max_free, u * NCH + i + 1)
                    q = qm[b][:, qt * P:(qt + 1) * P]
                    nc.tensor.matmul(m_ps[:, i % 2, :], q, kh[b][:, c * W:(c + 1) * W], start=True, stop=False)
                    nc.tensor.matmul(m_ps[:, i % 2, :], q, km[b][:, c * W:(c + 1) * W],
                                     start=False, stop=True).then_inc(max_full, 1)

            def dve_max(dve, u, which):
                for i in which:
                    qt, c = chunks[i]
                    dve.wait_ge(max_full, u * NCH + i + 1)
                    nc.vector.tensor_reduce(part_max[:, c, qt:qt + 1], m_ps[:, i % 2, :], AX_X,
                                            ALU.max).then_inc(max_free, 1)

            def dve_neg_max(dve):
                dve.drain()
                nc.vector.tensor_tensor(neg_max[:], part_max[:, 0, :], part_max[:, 1, :], ALU.max)
                dve.drain()
                nc.vector.tensor_scalar(neg_max[:], neg_max[:], -1.0, None, ALU.mult).then_inc(neg_max_ready, 1)

            def pe_turn_max(pe, u, use):
                pe.wait_ge(neg_max_ready, u + 1)
                pe.wait_ge(misc_free, use + 1)
                nc.tensor.transpose(misc[0:TB, 0:P], neg_max[:], consts["ident_sb"][:]).then_inc(misc_full, 1)

            def dve_shift(dve, u, use):
                dve.wait_ge(misc_full, use + 1)
                dve.wait_ge(shift_in, 16 * u + 16)
                nc.vector.tensor_copy(shift[:], misc[0:TB, 0:P])
                dve.drain()
                dve.sem_inc(misc_free, 1)
                dve.sem_inc(shift_ready, 1)

            def pe_scores(pe, u, b, n):
                Q, k = steps[n]
                if n >= 2:
                    pe.wait_ge(probs_ready, u * NS + n - 1)
                nc.tensor.matmul(s_ps[:, n % 2, :], kf[b][:, k * P:(k + 1) * P], qf[b][:, Q * W:(Q + 1) * W],
                                 start=True, stop=True).then_inc(scores_ready, 1)

            def pe_sums(pe, u, e, b, n):
                Q, k = steps[n]
                if k == 0:
                    pe.wait_ge(out_free, u * NQ + Q + 1)
                pe.wait_ge(probs_ready, u * NS + n + 2)
                for j in range(2):
                    mm = nc.tensor.matmul(o_ps[j * DH:(j + 1) * DH, :], vb[b][:, k + j, e, :],
                                          probs[:, (n + j) % NB, :], start=(k == 0), stop=(k == TB - 2))
                mm.then_inc(probs_free, 1)

            def dve_denominator(dve, u, n):
                Q, k = steps[n]
                if k == 0:
                    return
                before = probs[:, (n - 2) % NB:(n - 2) % NB + 2, :] if k == 2 else added[:]
                dve.drain()
                dve.wait_ge(probs_ready, u * NS + n + 2)
                nc.vector.tensor_tensor(added[:], before, probs[:, n % NB:n % NB + 2, :],
                                        ALU.add).then_inc(probs_added, 2 if k == 2 else 1)

            def dve_fold(dve):
                nc.vector.tensor_tensor(den[:], added[:, 0, :], added[:, 1, :], ALU.add).then_inc(den_ready, 1)

            def dve_evacuate(dve, u, Q):
                dve.wait_ge(probs_free, u * (NS // 2) + (Q + 1) * (TB // 2) + NB // 2)
                nc.vector.tensor_copy(sums[:], o_ps[:]).then_inc(out_free, 1)

            def pe_project(pe, u, h, Q, half, use):
                pe.wait_ge(out_free, u * NQ + Q + 2)
                pe.wait_ge(den_ready, u * NQ + Q + 1)
                pe.wait_ge(misc_free, use + 1)
                rhs = wo_all[:, h, :] if isinstance(h, int) else \
                    wo_all[:, bass.ds(h, 1), :].rearrange("p a n -> p (a n)")
                for c in range(2):
                    cols = slice((2 * half + c) * P, (2 * half + c + 1) * P)
                    nc.tensor.matmul(misc[:, 2 * c * P:(2 * c + 1) * P], sums[:, cols], rhs, start=True, stop=True)
                    mm = nc.tensor.matmul(misc[:, (2 * c + 1) * P:(2 * c + 2) * P], den[:, cols], ones[:],
                                          start=True, stop=True)
                mm.then_inc(misc_full, 1)

            def dve_add(dve, b, Q, half, use):
                dve.wait_ge(misc_full, use + 1)
                for c in range(2):
                    nc.vector.reciprocal(recip[:, c:c + 1], misc[:, (2 * c + 1) * P:(2 * c + 1) * P + 1])
                dve.drain()
                for c in range(2):
                    t = b * TB + 4 * Q + 2 * half + c
                    nc.vector.scalar_tensor_tensor(x[:, t, :], misc[:, 2 * c * P:(2 * c + 1) * P],
                                                   recip[:, c:c + 1], x[:, t, :], ALU.mult, ALU.add)
                dve.drain()
                dve.sem_inc(misc_free, 1)

            at_max = {MAX_AT + n: [2 * n, 2 * n + 1] for n in range(NCH // 2)}

            def all_slots(engine, slot):
                def pair(hp, first, last):
                    slot(hp, 0, 0, (hp, 0, 1), shared_keys and first)
                    slot(hp, 0, 1, (hp, 1, 0), False)
                    slot(hp, 1, 0, (hp, 1, 1), False)
                    slot(hp, 1, 1, None if last else (hp + 1, 0, 0), False)

                pair(0, True, False)
                with engine.Fori(1, HEADS // 2 - 1) as hp:
                    pair(hp, False, False)
                pair(HEADS // 2 - 1, False, True)

            @block.tensor
            def _(pe):
                pe.wait_ge(weights_now, 1)
                for i, (what, c) in enumerate(jobs(True, 0)):
                    pe_job(pe, 0, 0, 0, i, what, c)
                pe.wait_ge(proj_free, len(jobs(True, 0)) + 2)
                pe_max(pe, 0, 0, range(NCH))
                pe_turn_max(pe, 0, 0)
                pe.wait_ge(constants_set, 1)

                def slot(hp, e, b, nxt, first):
                    u, h, nb = 4 * hp + 2 * e + b, 2 * hp + e, 1 - b
                    made = jobs(first, nxt[1]) if nxt else []
                    if nxt and b == 1:
                        pe.wait_ge(weights_now, h + 2)
                    for n in range(min(AHEAD, len(made))):
                        pe_job(pe, *nxt, n, *made[n])
                    pe.wait_ge(shift_in, 16 * u + 32)
                    pe_scores(pe, u, b, 0)
                    for n in range(NS):
                        if n + 1 < NS:
                            pe_scores(pe, u, b, n + 1)
                        for i in range(AHEAD, len(made)):
                            if n == JOB_AT[i]:
                                pe_job(pe, *nxt, i, *made[i])
                        if nxt and n in at_max:
                            if n == MAX_AT:
                                pe.wait_ge(proj_free, job_index(*nxt, [w for w, _ in made].count("q")
                                                                + [w for w, _ in made].count("k") - 1) + 3)
                            pe_max(pe, u + 1, nb, at_max[n][:1])
                        if n in (2, 4) and not (isinstance(u, int) and u == 0):
                            pe_project(pe, u - 1, h if b else h - 1, NQ - 1, n // 2 - 1, misc_use(u, n // 2 - 1))
                        if n in OWN_AT:
                            half = OWN_AT.index(n)
                            pe_project(pe, u, h, 0, half, misc_use(u, 2 + 2 * half if nxt else 2 + half))
                        if n % 2:
                            pe_sums(pe, u, e, b, n - 1)
                        if nxt and n == TURN_AT:
                            pe_turn_max(pe, u + 1, misc_use(u, 3))
                        if nxt and n in at_max:
                            pe_max(pe, u + 1, nb, at_max[n][1:])

                all_slots(pe, slot)
                for half in range(2):
                    pe_project(pe, 2 * HEADS - 1, HEADS - 1, NQ - 1, half, misc_use(2 * HEADS - 1, 4 + half))

            @block.scalar
            def _(act):
                for p, (what, c) in enumerate(pieces(True, 0)):
                    act_piece(act, 0, 0, 0, p, what, c)

                def slot(hp, e, b, nxt, first):
                    u = 4 * hp + 2 * e + b
                    made = pieces(first, nxt[1]) if nxt else []
                    if made:
                        act_piece(act, *nxt, 0, *made[0])
                    for n in range(NS):
                        act.wait_ge(scores_ready, u * NS + n + 1)
                        if n % 2 == 0:
                            act.wait_ge(probs_free, u * (NS // 2) + n // 2 + 1)
                            act.wait_ge(probs_added, u * (NS // 2) + n // 2 + 1)
                        nc.scalar.activation(probs[:, n % NB, :], s_ps[:, n % 2, :], ACT.Exp,
                                             scale=SCALE).then_inc(probs_ready, 1)
                        if n + 1 < len(made):
                            act_piece(act, *nxt, n + 1, *made[n + 1])

                all_slots(act, slot)

            @block.vector
            def _(dve):
                dve.sem_inc(proj_free, 2)
                dve.sem_inc(probs_free, NB // 2)
                dve.sem_inc(probs_added, NB // 2)
                dve.sem_inc(max_free, 2)
                dve.sem_inc(out_free, 1)
                dve.sem_inc(misc_free, 1)
                dve.sem_inc(shift_in, 16)
                nc.vector.tensor_tensor(x[:], x[:], bo_row[:, None, :].to_broadcast([P, NT, D]), ALU.add)
                for p, (what, c) in enumerate(pieces(True, 0)):
                    dve_piece(dve, 0, 0, 0, p, what, c)
                dve_max(dve, 0, range(NCH))
                dve_neg_max(dve)
                dve_shift(dve, 0, 0)

                def slot(hp, e, b, nxt, first):
                    u = 4 * hp + 2 * e + b
                    made = pieces(first, nxt[1]) if nxt else []
                    for n in range(NS):
                        if n < len(made):
                            dve_piece(dve, *nxt, n, *made[n])
                        if nxt and n in at_max:
                            dve_max(dve, u + 1, at_max[n][:1])
                        if n in (2, 4) and not (isinstance(u, int) and u == 0):
                            dve_add(dve, 1 - b, NQ - 1, n // 2 - 1, misc_use(u, n // 2 - 1))
                        if n in OWN_AT:
                            half = OWN_AT.index(n)
                            dve_add(dve, b, 0, half, misc_use(u, 2 + 2 * half if nxt else 2 + half))
                        if n % 2:
                            dve_denominator(dve, u, n - 1)
                        if nxt and n == TURN_AT:
                            dve_shift(dve, u + 1, misc_use(u, 3))
                        if nxt and n in at_max:
                            dve_max(dve, u + 1, at_max[n][1:])
                            if n == max(at_max):
                                dve_neg_max(dve)
                        if n % TB == TB - 1:
                            dve_evacuate(dve, u, n // TB)
                            dve.drain()
                            dve_fold(dve)

                all_slots(dve, slot)
                for half in range(2):
                    dve_add(dve, 1, NQ - 1, half, misc_use(2 * HEADS - 1, 4 + half))


def binary_linear(nc, name, x, xT, wT, scale, bias, norm):
    TOP = 100.0
    with Scope(nc, name) as m:
        w_sb = m.sb("w_sb", [P, D])
        signs = m.sb("signs", [P, D])
        rows = m.sb("rows", [P, 2, D])
        y = m.sb("y", [P, NG, 4, D])
        norm([(w_sb[:], wT), (rows[:, 0, :], scale.partition_broadcast(P)),
              (rows[:, 1, :], bias.partition_broadcast(P))])
        y_ps = m.ps("y_ps", [P, NG, W])
        signs_ready = m.sem("signs_ready")
        made = m.sem("made")
        with nc.Block() as block:
            @block.tensor
            def _(pe):
                pe.wait_ge(signs_ready, 1)
                for g in range(NG):
                    for c in range(4):
                        t = 4 * g + c
                        mm = nc.tensor.matmul(y_ps[:, g, c * P:(c + 1) * P], xT[:, t * P:(t + 1) * P], signs[:],
                                              start=True, stop=True)
                    mm.then_inc(made, 1)

            @block.vector
            def _(dve):
                nc.vector.tensor_scalar(signs[:], w_sb[:], 0.0, 2.0, ALU.is_ge, ALU.mult)
                dve.drain()
                nc.vector.tensor_scalar(signs[:], signs[:], -1.0, None, ALU.add).then_inc(signs_ready, 1)
                for g in range(NG):
                    dve.wait_ge(made, g + 1)
                    yg = y[:, g, :, :]
                    nc.vector.tensor_tensor(yg, y_ps[:, g, :].rearrange("p (t n) -> p t n", n=D),
                                            rows[:, 0:1, :].to_broadcast([P, 4, D]), ALU.mult)
                    dve.drain()
                    nc.vector.tensor_tensor(yg, yg, rows[:, 1:2, :].to_broadcast([P, 4, D]), ALU.add)
                    dve.drain()
                    nc.vector.tensor_scalar(yg, yg, TOP, -TOP, ALU.min, ALU.max)
                    dve.drain()
                    xg = x[:, 4 * g:4 * g + 4, :]
                    nc.vector.tensor_tensor(xg, xg, yg, ALU.add)


def top2_experts(nc, name, x, xT, wg, w1, w2, w3, lower, norm):
    E, HT, HP = 8, 3, 114
    with Scope(nc, name) as m:
        wg_sb = m.sb("wg_sb", [P, E])
        lower_sb = m.sb("lower_sb", [P, E, E])
        logits = m.sb("logits", [P, NT, E])
        gating = m.sb("gating", [P, NT, E])
        gate_now = m.sb("gate_now", [P, 2, NT])
        above = m.sb("above", [P, NT, E, E])
        ties = m.sb("ties", [P, NT, E, E])
        rank = m.sb("rank", [P, NT, E])
        stat = m.sb("stat", [P, NT])
        w12 = m.sb("w12", [P, 2, 2, HT * HP])
        w3_sb = m.sb("w3_sb", [HP, 2, HT, D])
        silu = m.sb("silu", [HP, 2, W])
        hidden = m.sb("hidden", [HP, 2, HT, W])
        norm([(wg_sb[:], wg), (lower_sb[:], lower.partition_broadcast(P))])
        g_ps = m.ps("g_ps", [P, W])
        up_ps = m.ps("up_ps", [P, 2, W])
        lin_ps = m.ps("lin_ps", [P, 2, W])
        y_ps = m.ps("y_ps", [P, 2, W])
        logits_made = m.sem("logits_made")
        shifted = m.sem("shifted")
        exps_ready = m.sem("exps_ready")
        weights_in = [m.sem(f"weights_in{r}") for r in range(2)]
        up_full = m.sem("up_full")
        lin_full = m.sem("lin_full")
        silu_done = m.sem("silu_done")
        hidden_ready = m.sem("hidden_ready")
        y_full = m.sem("y_full")
        y_free = m.sem("y_free")

        with nc.Block() as block:
            @block.sync
            def _(sp):
                def load(e, r):
                    one = bass.ds(e, 1)
                    sp.dma_start(w12[:, r, 0, :], w1[one, :, :].rearrange("a p n -> p (a n)")).then_inc(weights_in[r], 16)
                    sp.dma_start(w12[:, r, 1, :], w2[one, :, :].rearrange("a p n -> p (a n)")).then_inc(weights_in[r], 16)
                    sp.dma_start(w3_sb[:, r, :, :], w3[one, :, :, :].rearrange("a p t n -> p (a t) n")
                                 ).then_inc(weights_in[r], 16)

                load(0, 0)
                load(1, 1)
                with sp.Fori(1, E // 2) as pair:
                    for r in range(2):
                        sp.wait_ge(y_full, (2 * pair + r - 1) * NG + 2)
                        load(2 * pair + r, r)

            @block.tensor
            def _(pe):
                for t in range(NT):
                    mm = nc.tensor.matmul(g_ps[:, t * E:(t + 1) * E], xT[:, t * P:(t + 1) * P], wg_sb[:],
                                          start=True, stop=True)
                mm.then_inc(logits_made, 1)

                def up(e, r, g, i):
                    n = (e * NG + g) * HT + i
                    k = (g * HT + i) % 2
                    for ps, j, full, freed in ((up_ps, 0, up_full, silu_done), (lin_ps, 1, lin_full, hidden_ready)):
                        pe.wait_ge(freed, n + 1)
                        nc.tensor.matmul(ps[0:HP, k, :], w12[:, r, j, i * HP:(i + 1) * HP],
                                         xT[:, g * W:(g + 1) * W], start=True, stop=True).then_inc(full, 1)

                def down(e, r, g):
                    n = e * NG + g
                    pe.wait_ge(y_free, n + 1)
                    pe.wait_ge(hidden_ready, (n + 1) * HT + 2)
                    for c in range(4):
                        for i in range(HT):
                            mm = nc.tensor.matmul(y_ps[:, g % 2, c * P:(c + 1) * P],
                                                  hidden[:, g % 2, i, c * P:(c + 1) * P], w3_sb[:, r, i, :],
                                                  start=(i == 0), stop=(i == HT - 1))
                    mm.then_inc(y_full, 1)

                with pe.Fori(0, E // 2) as pair:
                    for r in range(2):
                        e = 2 * pair + r
                        pe.wait_ge(weights_in[r], 48 * (pair + 1))
                        for g in range(NG):
                            for i in range(HT):
                                up(e, r, g, i)
                                if i == 1 and g:
                                    down(e, r, g - 1)
                        down(e, r, NG - 1)

            @block.scalar
            def _(act):
                act.wait_ge(shifted, 1)
                nc.scalar.activation(gating[:], gating[:], ACT.Exp).then_inc(exps_ready, 1)
                with act.Fori(0, E // 2) as pair:
                    for r in range(2):
                        for g in range(NG):
                            for i in range(HT):
                                n = ((2 * pair + r) * NG + g) * HT + i
                                k = (g * HT + i) % 2
                                act.wait_ge(up_full, n + 1)
                                act.wait_ge(hidden_ready, n + 1)
                                nc.scalar.activation(silu[:, k, :], up_ps[0:HP, k, :],
                                                     ACT.Silu).then_inc(silu_done, 1)

            @block.vector
            def _(dve):
                dve.sem_inc(silu_done, 2)
                dve.sem_inc(hidden_ready, 2)
                dve.sem_inc(y_full, 2)
                dve.sem_inc(y_free, 2)
                dve.wait_ge(logits_made, 1)
                nc.vector.tensor_copy(logits[:], g_ps[:, 0:NT * E].rearrange("p (t e) -> p t e", e=E))
                dve.drain()
                nc.vector.tensor_reduce(stat[:], logits[:], AX_X, ALU.max)
                dve.drain()
                nc.vector.tensor_tensor(gating[:], logits[:], stat[:, :, None].to_broadcast([P, NT, E]),
                                        ALU.subtract).then_inc(shifted, 1)
                for t in range(NT):
                    other = logits[:, t, None, :].to_broadcast([P, E, E])
                    own = logits[:, t, :, None].to_broadcast([P, E, E])
                    nc.vector.tensor_tensor(above[:, t, :, :], other, own, ALU.is_gt)
                    nc.vector.tensor_tensor(ties[:, t, :, :], other, own, ALU.is_equal)
                dve.drain()
                nc.vector.tensor_tensor(ties[:].rearrange("p t a b -> p t (a b)"),
                                        ties[:].rearrange("p t a b -> p t (a b)"),
                                        lower_sb[:].rearrange("p a b -> p (a b)")[:, None, :]
                                        .to_broadcast([P, NT, E * E]), ALU.mult)
                dve.drain()
                nc.vector.tensor_tensor(above[:], above[:], ties[:], ALU.add)
                dve.drain()
                nc.vector.tensor_reduce(rank[:], above[:], AX_X, ALU.add)
                dve.drain()
                nc.vector.tensor_scalar(rank[:], rank[:], 1.5, None, ALU.is_lt)
                dve.wait_ge(exps_ready, 1)
                dve.drain()
                nc.vector.tensor_tensor(gating[:], gating[:], rank[:], ALU.mult)
                dve.drain()
                nc.vector.tensor_reduce(stat[:], gating[:], AX_X, ALU.add)
                dve.drain()
                nc.vector.reciprocal(stat[:], stat[:])
                dve.drain()
                nc.vector.tensor_tensor(gating[:], gating[:], stat[:, :, None].to_broadcast([P, NT, E]), ALU.mult)
                dve.drain()

                def product(e, g, i):
                    n = (e * NG + g) * HT + i
                    k = (g * HT + i) % 2
                    if i == 0:
                        dve.wait_ge(y_full, e * NG + g + 1)
                    dve.wait_ge(lin_full, n + 1)
                    dve.wait_ge(silu_done, n + 3)
                    nc.vector.tensor_tensor(hidden[:, g % 2, i, :], silu[:, k, :], lin_ps[0:HP, k, :],
                                            ALU.mult).then_inc(hidden_ready, 1)

                def add(e, r, g):
                    dve.wait_ge(y_full, e * NG + g + 3)
                    for c in range(4):
                        t = 4 * g + c
                        last = nc.vector.scalar_tensor_tensor(x[:, t, :], y_ps[:, g % 2, c * P:(c + 1) * P],
                                                              gate_now[:, r, t:t + 1], x[:, t, :], ALU.mult, ALU.add)
                    last.then_inc(y_free, 1)

                with dve.Fori(0, E // 2) as pair:
                    for r in range(2):
                        e = 2 * pair + r
                        nc.vector.tensor_copy(gate_now[:, r, :],
                                              gating[:, :, bass.ds(e, 1)].rearrange("p t a -> p (t a)"))
                        for g in range(NG):
                            for i in range(HT):
                                product(e, g, i)
                                if i == 2 and g:
                                    add(e, r, g - 1)
                        add(e, r, NG - 1)
                        dve.drain()


def routed_experts(nc, name, x, xT, w, consts, norm, spare):
    E, H, GS, BUDGET = 64, 32, 64, (B * S // 64) * 16
    N = B * S
    HT = E * H // P
    EARLY = 3
    BIG = 1e30
    with Scope(nc, name) as outer:
        fsT = outer.sb("fsT", [E, N])
        recip = outer.sb("recip", [P, NT])
        wup = outer.sb("up_weights", [P, E * H])
        wgate = outer.sb("gate_weights", [P, E * H])
        bias = outer.sb("biases", [P, 2, HT])
        early = outer.sb("early", [P, EARLY, HT, W])
        wdown = outer.sb("down_weights", [P, HT, D])
        bdown = outer.sb("down_biases", [E, D])
        spread = outer.sb("spread", [E, HT, P])

        with Scope(nc, name + "r") as m:
            wr = m.sb("wr", [P, E])
            br = m.sb("br", [P, E])
            rank_row = m.sb("rank_row", [P, N // 2])
            column = m.sb("column", [P, 16])
            ones = m.sb("ones", [P, P])
            score = m.sb("score", [P, NT, E])
            stat = m.sb("stat", [P, NT])
            sT = m.sb("sT", [E, N])
            halves = m.sb("halves", [P, 2, N // 2])
            other = m.sb("other", [E, N // 2])
            sums = m.sb("sums", [P, 16])
            all_sums = m.sb("all_sums", [P, N])
            greater = m.sb("greater", [P, N])
            ties = spare[:].rearrange("p t n -> p (t n)")
            so_far = fsT
            counts = m.sb("counts", [P, 16])
            one = m.sb("one", [P, 8])
            per_expert = m.sb("per_expert", [E, E])
            silu, gate = (all_sums[:, c * W:(c + 2) * W].rearrange("p (r n) -> p r n", r=2) for c in (0, 2))
            norm([(wr[:], w["wr"]), (br[:], w["br"].partition_broadcast(P)), (rank_row[:], consts["rank_row"]),
                  (column[:], consts["iota"][0:16].partition_broadcast(P))])
            t_ps = m.ps("t_ps", [P, 4, W])
            l_ps = m.ps("l_ps", [P, 2, W])
            up_ps = m.ps("up_ps", [P, W])
            gate_ps = m.ps("gate_ps", [P, W])
            weights_in = m.sem("weights_in")
            down_in = m.sem("down_in")
            up_full = m.sem("up_full")
            up_moved = m.sem("up_moved")
            gate_full = m.sem("gate_full")
            gate_moved = m.sem("gate_moved")
            early_done = m.sem("early_done")
            logits_made = m.sem("logits_made")
            shifted = m.sem("shifted")
            exps_ready = m.sem("exps_ready")
            scores_ready = m.sem("scores_ready")
            turned = m.sem("turned")
            sums_ready = m.sem("sums_ready")
            sums_turned = m.sem("sums_turned")
            least_ready = m.sem("least_ready")
            least_turned = m.sem("least_turned")
            fs_ready = m.sem("fs_ready")
            totals_made = m.sem("totals_made")

            with nc.Block() as block:
                @block.sync
                def _(sp):
                    for dst, src in ((wup, "wup"), (wgate, "wgate"), (bias, "bias")):
                        sp.dma_start(dst[:], w[src]).then_inc(weights_in, 16)
                    for dst, src in ((wdown, w["wdown"]), (bdown, w["bdown"]), (spread, consts["spread_expert"])):
                        sp.dma_start(dst[:], src).then_inc(down_in, 16)
                    sp.wait_ge(down_in, 48)

                @block.tensor
                def _(pe):
                    ident = consts["ident_sb"]
                    for t in range(NT):
                        at = 2 * (t % TB) + t // TB
                        mm = nc.tensor.matmul(l_ps[:, at // 8, at % 8 * E:(at % 8 + 1) * E], xT[:, t * P:(t + 1) * P],
                                              wr[:], start=True, stop=True)
                    mm.then_inc(logits_made, 1)
                    pe.wait_ge(scores_ready, 1)
                    for t in range(TB):
                        mm = nc.tensor.transpose(t_ps[:, t // 4, t % 4 * P:(t % 4 + 1) * P],
                                                 score[:, 2 * t:2 * t + 2, :].rearrange("p h e -> p (h e)"), ident[:])
                    mm.then_inc(turned, 1)
                    pe.wait_ge(weights_in, 48)
                    for k in range(EARLY * HT):
                        i, tokens = k % HT, xT[:, k // HT * W:(k // HT + 1) * W]
                        if k:
                            pe.wait_ge(up_moved, k)
                        nc.tensor.matmul(up_ps[:], wup[:, i * P:(i + 1) * P], tokens,
                                         start=True, stop=True).then_inc(up_full, 1)
                        if k:
                            pe.wait_ge(gate_moved, k)
                        nc.tensor.matmul(gate_ps[:], wgate[:, i * P:(i + 1) * P], tokens,
                                         start=True, stop=True).then_inc(gate_full, 1)
                    pe.wait_ge(sums_ready, 1)
                    for c in range(16):
                        mm = nc.tensor.transpose(t_ps[:, c // 4, c % 4 * P:(c % 4 + 1) * P],
                                                 sums[:, c:c + 1].to_broadcast([P, P]), ident[:])
                    mm.then_inc(sums_turned, 1)
                    pe.wait_ge(least_ready, 1)
                    nc.tensor.transpose(l_ps[:, 0, 0:P], one[:, 0:1].to_broadcast([P, P]),
                                        ident[:]).then_inc(least_turned, 1)
                    pe.wait_ge(fs_ready, 1)
                    for t in range(NT):
                        mm = nc.tensor.matmul(t_ps[:, t // 4, t % 4 * P:(t % 4 + 1) * P], fsT[:, t * P:(t + 1) * P],
                                              ones[0:E, :], start=True, stop=True)
                    mm.then_inc(totals_made, 1)

                @block.scalar
                def _(act):
                    act.wait_ge(shifted, 1)
                    nc.scalar.activation(score[:], score[:], ACT.Exp).then_inc(exps_ready, 1)
                    act.wait_ge(weights_in, 48)
                    for k in range(EARLY * HT):
                        i = k % HT
                        act.wait_ge(up_full, k + 1)
                        if k >= 2:
                            act.wait_ge(early_done, k - 1)
                        nc.scalar.activation(silu[:, k % 2, :], up_ps[:], ACT.Silu,
                                             bias=bias[:, 0, i:i + 1]).then_inc(up_moved, 1)
                        act.wait_ge(gate_full, k + 1)
                        nc.scalar.activation(gate[:, k % 2, :], gate_ps[:], ACT.Identity,
                                             bias=bias[:, 1, i:i + 1]).then_inc(gate_moved, 1)

                @block.gpsimd
                def _(pool):
                    for k in range(EARLY * HT):
                        pool.wait_ge(gate_moved, k + 1)
                        nc.gpsimd.tensor_tensor(early[:, k // HT, k % HT, :], silu[:, k % 2, :], gate[:, k % 2, :],
                                                ALU.mult).then_inc(early_done, 1)

                @block.vector
                def _(dve):
                    tt, ts = nc.vector.tensor_tensor, nc.vector.tensor_scalar
                    nc.vector.memset(ones[:], 1.0)
                    dve.wait_ge(logits_made, 1)
                    for h in range(2):
                        tt(score[:, 8 * h:8 * h + 8, :], l_ps[:, h, :].rearrange("p (t e) -> p t e", e=E),
                           br[:, None, :].to_broadcast([P, 8, E]), ALU.add)
                    dve.drain()
                    nc.vector.tensor_reduce(stat[:], score[:], AX_X, ALU.max)
                    dve.drain()
                    wide = stat[:, :, None].to_broadcast([P, NT, E])
                    tt(score[:], score[:], wide, ALU.subtract).then_inc(shifted, 1)
                    dve.wait_ge(exps_ready, 1)
                    nc.vector.tensor_reduce(stat[:], score[:], AX_X, ALU.add)
                    dve.drain()
                    nc.vector.reciprocal(stat[:], stat[:])
                    dve.drain()
                    tt(score[:], score[:], wide, ALU.mult).then_inc(scores_ready, 1)

                    dve.wait_ge(turned, 1)
                    for h in range(2):
                        at = slice(h * W, (h + 1) * W)
                        nc.vector.tensor_copy(sT[:, at], t_ps[0:E, h, :])
                        nc.vector.tensor_copy(sT[:, N // 2 + h * W:N // 2 + (h + 1) * W], t_ps[E:P, h, :])
                        nc.vector.tensor_copy(halves[0:E, 0, at], t_ps[0:E, h, :])
                        ts(halves[E:P, 0, at], t_ps[E:P, h, :], -1.0, None, ALU.mult)
                    dve.drain()

                    src = 0
                    n = N // 2

                    def exchange(frm, to, k, j):
                        turns = 2 if k < n else 1
                        views = [halves[:, v, :].rearrange("p (a d b s j) -> p a d b s j", d=turns, b=k // (2 * j),
                                                           s=2, j=j) for v in (frm, to)]
                        for d in range(turns):
                            lo, hi = (views[0][:, :, d, :, s, :] for s in range(2))
                            for s in range(2):
                                tt(views[1][:, :, d, :, s, :], lo, hi, ALU.max if s == d else ALU.min)
                        dve.drain()

                    k = 2
                    while k <= n:
                        j = k // 2
                        while j:
                            exchange(src, 1 - src, k, j)
                            src = 1 - src
                            j //= 2
                        k *= 2
                    ts(other[:], halves[E:P, src, :], -1.0, None, ALU.mult)
                    dve.drain()
                    tt(halves[0:E, 1 - src, :], halves[0:E, src, :], other[:], ALU.max)
                    tt(halves[E:P, 1 - src, :], halves[0:E, src, :], other[:], ALU.min)
                    dve.drain()
                    src = 1 - src
                    j = n // 2
                    while j:
                        exchange(src, 1 - src, n, j)
                        src = 1 - src
                        j //= 2
                    ranked = halves[:, src, :]

                    nc.vector.tensor_reduce(sums[:], ranked.rearrange("p (g n) -> p g n", n=GS), AX_X,
                                            ALU.add).then_inc(sums_ready, 1)
                    dve.wait_ge(sums_turned, 1)
                    dve.wait_ge(early_done, EARLY * HT)
                    flat = all_sums[:].rearrange("p (h c e) -> p c h e", h=2, e=E)
                    for c in range(16):
                        nc.vector.tensor_copy(flat[:, c, :, :], t_ps[:, c // 4, c % 4 * P:(c % 4 + 1) * P]
                                              .rearrange("p (h e) -> p h e", e=E))
                    dve.drain()
                    place, trial, value, count = (one[:, c:c + 1] for c in (1, 2, 3, 4))
                    nc.vector.memset(place, 0.0)
                    for step in (8, 4, 2, 1, 1):
                        dve.drain()
                        ts(trial, place, step - 1.0, None, ALU.add)
                        dve.drain()
                        nc.vector.scalar_tensor_tensor(counts[:], column[:], trial, sums[:], ALU.is_equal, ALU.mult,
                                                       accum_out=value)
                        dve.drain()
                        ts(greater[:], all_sums[:], value, 0.0, ALU.is_gt, ALU.add, accum_out=count)
                        dve.drain()
                        ts(trial, count, BUDGET - 0.5, float(step), ALU.is_lt, ALU.mult)
                        dve.drain()
                        tt(place, place, trial, ALU.add)
                    dve.drain()
                    ts(counts[:], column[:], place, BIG, ALU.is_ge, ALU.mult)
                    dve.drain()
                    tt(counts[:], counts[:], sums[:], ALU.add)
                    dve.drain()
                    nc.vector.tensor_reduce(one[:, 0:1], counts[:], AX_X, ALU.min).then_inc(least_ready, 1)
                    dve.wait_ge(least_turned, 1)
                    nc.vector.tensor_reduce(one[:, 1:2], l_ps[:, 0, 0:P], AX_X, ALU.min)
                    dve.drain()

                    def keep(values, least, budget, room, rows):
                        gr, ti = greater[0:rows, :], ties[0:rows, :]
                        ts(gr, values, least, 0.0, ALU.is_gt, ALU.add, accum_out=room)
                        dve.drain()
                        if isinstance(budget, float):
                            ts(room, room, -1.0, budget, ALU.mult, ALU.add)
                        else:
                            tt(room, budget, room, ALU.subtract)
                        ts(ti, values, least, None, ALU.is_equal)
                        dve.drain()
                        nc.vector.tensor_tensor_scan(so_far[0:rows, :], ones[0:rows, 0:1].to_broadcast([rows, N]), ti, 0.0,
                                                     ALU.mult, ALU.add)
                        dve.drain()
                        ts(so_far[0:rows, :], so_far[0:rows, :], room, None, ALU.is_le)
                        dve.drain()
                        tt(ti, ti, so_far[0:rows, :], ALU.mult)
                        dve.drain()
                        tt(gr, gr, ti, ALU.add)
                        dve.drain()

                    keep(all_sums[0:E, :], one[0:E, 1:2], float(BUDGET), one[0:E, 2:3], E)
                    nc.vector.tensor_reduce(per_expert[:], greater[0:E, :].rearrange("p (g e) -> p e g", e=E), AX_X,
                                            ALU.add)
                    dve.drain()
                    tt(per_expert[:], per_expert[:], consts["ident_sb"][0:E, 0:E], ALU.mult)
                    dve.drain()
                    nc.vector.tensor_reduce(one[0:E, 3:4], per_expert[:], AX_X, ALU.add)
                    dve.drain()
                    ts(one[0:E, 4:5], one[0:E, 3:4], float(GS), None, ALU.mult)
                    ts(one[E:P, 4:5], one[0:E, 3:4], float(GS), None, ALU.mult)
                    dve.drain()
                    ts(halves[:, 1 - src, :], rank_row[:], one[:, 4:5], BIG, ALU.is_ge, ALU.mult)
                    dve.drain()
                    tt(halves[:, 1 - src, :], halves[:, 1 - src, :], ranked, ALU.add)
                    dve.drain()
                    nc.vector.tensor_reduce(one[:, 5:6], halves[:, 1 - src, :], AX_X, ALU.min)
                    dve.drain()
                    nc.vector.tensor_copy(one[0:E, 6:7], one[E:P, 5:6])
                    dve.drain()
                    tt(one[0:E, 5:6], one[0:E, 5:6], one[0:E, 6:7], ALU.min)
                    dve.drain()
                    keep(sT[:], one[0:E, 5:6], one[0:E, 4:5], one[0:E, 7:8], E)
                    tt(fsT[:], sT[:], greater[0:E, :], ALU.mult).then_inc(fs_ready, 1)
                    dve.wait_ge(totals_made, 1)
                    totals = t_ps[:].rearrange("p g (c n) -> p (g c) n", n=P)[:, :, 0]
                    ts(recip[:], totals, 1e-6, None, ALU.add)
                    dve.drain()
                    nc.vector.reciprocal(recip[:], recip[:])

        with Scope(nc, name + "f") as m:
            fs_now = m.sb("fs_now", [E, W])
            silu = m.sb("silu", [P, 2, W])
            prod = m.sb("prod", [P, 2, W])
            hidden = m.sb("hidden", [P, HT, W])
            up_ps = m.ps("up_ps", [P, 2, W])
            gate_ps = m.ps("gate_ps", [P, 2, W])
            fs_ps = m.ps("fs_ps", [P, 2, W])
            y_ps = m.ps("y_ps", [P, W])
            up_full = m.sem("up_full")
            gate_full = m.sem("gate_full")
            fs_full = m.sem("fs_full")
            silu_done = m.sem("silu_done")
            prod_done = m.sem("prod_done")
            hidden_ready = m.sem("hidden_ready")
            fs_copied = m.sem("fs_copied")
            y_full = m.sem("y_full")
            y_free = m.sem("y_free")
            with nc.Block() as block:
                @block.tensor
                def _(pe):
                    def spread_fs(n, i):
                        pe.wait_ge(hidden_ready, n + 1)
                        nc.tensor.matmul(fs_ps[:, i % 2, :], spread[:, i, :], fs_now[:],
                                         start=True, stop=True).then_inc(fs_full, 1)

                    def down(g, units):
                        pe.wait_ge(y_free, g + 1)
                        pe.wait_ge(hidden_ready, (g + 1) * HT + 2)
                        for c in range(4):
                            cols = slice(c * P, (c + 1) * P)
                            for i in range(HT):
                                nc.tensor.matmul(y_ps[:, cols], units[:, i, cols], wdown[:, i, :],
                                                 start=(i == 0), stop=False)
                            mm = nc.tensor.matmul(y_ps[:, cols], fs_now[:, cols], bdown[:], start=False, stop=True)
                        mm.then_inc(y_full, 1)

                    for g in range(EARLY):
                        pe.wait_ge(fs_copied, g + 1)
                        for i in range(HT):
                            spread_fs(g * HT + i, i)
                        down(g, early[:, g, :, :])
                    with pe.Fori(EARLY, NG) as g:
                        for i in range(HT):
                            n = (g - EARLY) * HT + i
                            tokens = xT[:, bass.ds(g * W, W)]
                            pe.wait_ge(silu_done, n + 1)
                            nc.tensor.matmul(up_ps[:, i % 2, :], wup[:, i * P:(i + 1) * P], tokens,
                                             start=True, stop=True).then_inc(up_full, 1)
                            pe.wait_ge(prod_done, n + 1)
                            nc.tensor.matmul(gate_ps[:, i % 2, :], wgate[:, i * P:(i + 1) * P], tokens,
                                             start=True, stop=True).then_inc(gate_full, 1)
                            if i == 0:
                                pe.wait_ge(fs_copied, g + 1)
                            spread_fs(g * HT + i, i)
                        down(g, hidden)

                @block.scalar
                def _(act):
                    def copy_fs(g):
                        act.wait_ge(y_full, g + 1)
                        nc.scalar.copy(fs_now[:], fsT[:, bass.ds(g * W, W)]).then_inc(fs_copied, 1)

                    for g in range(EARLY):
                        copy_fs(g)
                    with act.Fori(EARLY, NG) as g:
                        copy_fs(g)
                        for i in range(HT):
                            n = (g - EARLY) * HT + i
                            act.wait_ge(up_full, n + 1)
                            act.wait_ge(prod_done, n + 1)
                            nc.scalar.activation(silu[:, i % 2, :], up_ps[:, i % 2, :], ACT.Silu,
                                                 bias=bias[:, 0, i:i + 1]).then_inc(silu_done, 1)

                @block.vector
                def _(dve):
                    def times_fs(g, i, to, frm):
                        dve.wait_ge(fs_full, g * HT + i + 1)
                        nc.vector.tensor_tensor(to, frm, fs_ps[:, i % 2, :], ALU.mult).then_inc(hidden_ready, 1)

                    def add(g):
                        dve.wait_ge(y_full, g + 2)
                        for c in range(4):
                            t = 4 * g + c
                            row = x[:, bass.ds(t, 1), :].rearrange("p a n -> p (a n)")
                            last = nc.vector.scalar_tensor_tensor(row, y_ps[:, c * P:(c + 1) * P],
                                                                  recip[:, bass.ds(t, 1)], row, ALU.mult, ALU.add)
                        last.then_inc(y_free, 1)
                        dve.drain()

                    for s, k in ((silu_done, 2), (prod_done, 2), (hidden_ready, 2), (y_full, 1), (y_free, 1)):
                        dve.sem_inc(s, k)
                    for g in range(EARLY):
                        for i in range(HT):
                            times_fs(g, i, early[:, g, i, :], early[:, g, i, :])
                        add(g)
                    with dve.Fori(EARLY, NG) as g:
                        for i in range(HT + 1):
                            n = (g - EARLY) * HT + i
                            if i < HT:
                                dve.wait_ge(gate_full, n + 1)
                                dve.wait_ge(silu_done, n + 3)
                                dve.wait_ge(hidden_ready, g * HT + i + 1)
                                nc.vector.scalar_tensor_tensor(prod[:, i % 2, :], gate_ps[:, i % 2, :],
                                                               bias[:, 1, i:i + 1], silu[:, i % 2, :],
                                                               ALU.add, ALU.mult).then_inc(prod_done, 1)
                            if i:
                                dve.wait_ge(prod_done, n + 2)
                                times_fs(g, i - 1, hidden[:, i - 1, :], prod[:, (i - 1) % 2, :])
                        add(g)


def leaf_layers(nc, name, y_tok, yT, outs, w, act_fn, consts):
    DEPTH, NL, LW = 8, 256, 16
    TILES, SUB = NL * LW // P, P // LW
    BLOCKS = NT + TILES
    GROUPS = len(outs) * BLOCKS // 4
    ROW = D + SUB
    T = len(outs)
    I32 = mybir.dt.int32
    slots = nc.dram_tensor(f"{name}_slots", [T * BLOCKS * P, ROW], F32, kind="Internal").ap()
    results = nc.dram_tensor(f"{name}_results", [T * BLOCKS * P, D], F32, kind="Internal").ap()
    with Scope(nc, name) as outer:
        rows = outer.sb("rows", [P, T, NT, ROW])
        slot_of = outer.sb("slot_of", [P, T, NT], I32)
        leaf_of = outer.sb("leaf_of", [P, T, NT], I32)
        tile_of = outer.sb("tile_of", [1, T * BLOCKS], I32)

        with Scope(nc, name + "t") as m:
            nw = m.sb("nw", [P, T, NL])
            nb = m.sb("nb", [P, T, NL])
            zeros = m.sb("zeros", [P, BLOCKS // 4 * ROW])
            iota = m.sb("iota", [P, BLOCKS])
            before = m.sb("before", [P, 2, P], BF16)
            right = m.sb("right", [P, NT, NL], BF16)
            ways = m.sb("ways", [P, 2, NT, TILES], BF16)
            own_turns = m.sb("own_turns", [P, NT, SUB - 1, TILES], BF16)
            turn = m.sb("turn", [P, NT, SUB - 1])
            below = m.sb("below", [P, 2, NT, SUB])
            first = m.sb("first", [P, NT, 1])
            in_tile = m.sb("in_tile", [P, T, NT, TILES], BF16)
            over = m.sb("over", [P, TILES, NT])
            some = m.sb("some", [P, 4, TILES])
            table = m.sb("table", [1, BLOCKS, TILES])
            short = m.sb("short", [1, BLOCKS])
            place = m.sb("place", [P, NT, TILES])
            spot = m.sb("spot", [P, 3, NT])
            by_sub = m.sb("by_sub", [P, NT, SUB])
            l_ps = m.ps("l_ps", [P, 4, W])
            rank_ps = m.ps("rank_ps", [P, 2, W])
            count_ps = m.ps("count_ps", [P, 2, W])
            loaded = m.sem("loaded")
            cleared = m.sem("cleared")
            zeros_ready = m.sem("zeros_ready")
            logits_full = m.sem("logits_full")
            logits_free = m.sem("logits_free")
            tile_ready = m.sem("tile_ready")
            rank_full = m.sem("rank_full")
            rows_copied = m.sem("rows_copied")
            routed = m.sem("routed")
            moved = m.sem("moved")
            with nc.Block() as block:
                @block.sync
                def _(sp):
                    sp.dma_start(nw[:], w["nw"].rearrange("t p n -> p t n")).then_inc(loaded, 16)
                    sp.dma_start(nb[:], w["nb"].partition_broadcast(P)).then_inc(loaded, 16)
                    sp.dma_start(iota[:], consts["iota"].partition_broadcast(P)).then_inc(loaded, 16)
                    sp.dma_start(before[:], consts["before"]).then_inc(loaded, 16)
                    sp.wait_ge(zeros_ready, 1)
                    wide = slots.rearrange("(p q r) c -> p q (r c)", p=P, q=4 * T)
                    for q in range(4 * T):
                        sp.dma_start(wide[:, q, :], zeros[:]).then_inc(cleared, 16)
                    sp.wait_ge(cleared, 16 * 4 * T)

                @block.tensor
                def _(pe):
                    pe.wait_ge(loaded, 64)
                    for n in range(T):
                        for t in range(NT):
                            s = 8 * n + t // 2
                            if s >= 4 and t % 2 == 0:
                                pe.wait_ge(logits_free, s - 3)
                            mm = nc.tensor.matmul(l_ps[:, s % 4, t % 2 * NL:(t % 2 + 1) * NL],
                                                  yT[:, t * P:(t + 1) * P], nw[:, n, :], start=True, stop=True)
                            if t % 2:
                                mm.then_inc(logits_full, 1)
                        pe.wait_ge(tile_ready, n + 1)
                        if n >= 2:
                            pe.wait_ge(routed, n - 1)
                        ones = in_tile[:, n, :, :].rearrange("p t e -> p (t e)")
                        nc.tensor.matmul(rank_ps[:, n % 2, :], before[:, 0, :], ones, start=True, stop=False)
                        for s in range(1, NT):
                            nc.tensor.matmul(rank_ps[:, n % 2, s * TILES:W], before[:, 1, :],
                                             ones[:, 0:W - s * TILES], start=False, stop=(s == NT - 1))
                        for t in range(NT):
                            mm = nc.tensor.matmul(count_ps[:, n % 2, 0:TILES], before[:, 1, :],
                                                  in_tile[:, n, t, :], start=(t == 0), stop=(t == NT - 1))
                        mm.then_inc(rank_full, 1)

                @block.scalar
                def _(act):
                    for n in range(T):
                        nc.scalar.copy(rows[:, n, :, 0:D], y_tok[:]).then_inc(rows_copied, 1)

                @block.vector
                def _(dve):
                    nc.vector.memset(zeros[:], 0.0).then_inc(zeros_ready, 1)
                    nc.vector.memset(some[:, 3, :], 1.0)
                    nc.vector.memset(first[:], 1.0)
                    dve.wait_ge(loaded, 64)
                    nc.vector.tensor_scalar(nb[:], nb[:], -1.0, None, ALU.mult)
                    dve.drain()
                    tile_step = DEPTH - SUB.bit_length() + 1
                    for n in range(T):
                        for s in range(NT // 2):
                            dve.wait_ge(logits_full, 8 * n + s + 1)
                            nc.vector.tensor_tensor(right[:, 2 * s:2 * s + 2, :],
                                                    l_ps[:, s % 4, :].rearrange("p (t n) -> p t n", n=NL),
                                                    nb[:, n:n + 1, :].to_broadcast([P, 2, NL]),
                                                    ALU.is_gt).then_inc(logits_free, 1)
                        nc.vector.memset(ways[:, 0, :, 0:1], 1.0)
                        for level in range(tile_step):
                            k = 2 ** level
                            now = ways[:, level % 2, :, 0:k]
                            nxt = in_tile[:, n, :, :] if level == tile_step - 1 else \
                                ways[:, 1 - level % 2, :, 0:2 * k]
                            nxt = nxt.rearrange("p t (j s) -> p t j s", s=2)
                            dve.drain()
                            nc.vector.tensor_tensor(nxt[:, :, :, 1], now, right[:, :, k - 1:2 * k - 1], ALU.mult)
                            dve.drain()
                            last = nc.vector.tensor_tensor(nxt[:, :, :, 0], now, nxt[:, :, :, 1], ALU.subtract)
                        last.then_inc(tile_ready, 1)
                        dve.drain()
                        for level in range(tile_step, DEPTH):
                            k = 2 ** (level - tile_step)
                            turns = right[:, :, k * TILES - 1:2 * k * TILES - 1]
                            nc.vector.tensor_tensor(own_turns[:, :, k - 1:2 * k - 1, :],
                                                    turns.rearrange("p t (e s) -> p t s e", s=k),
                                                    in_tile[:, n, :, None, :].to_broadcast([P, NT, k, TILES]),
                                                    ALU.mult)
                        dve.drain()
                        nc.vector.tensor_reduce(turn[:], own_turns[:], AX_X, ALU.add)
                        sub = rows[:, n, :, D:ROW]
                        now = first[:]
                        for level in range(tile_step, DEPTH):
                            k = 2 ** (level - tile_step)
                            both = sub if level == DEPTH - 1 else below[:, k - 1, :, 0:2 * k]
                            nxt = both.rearrange("p t (j s) -> p t j s", s=2)
                            dve.drain()
                            nc.vector.tensor_tensor(nxt[:, :, :, 1], now, turn[:, :, k - 1:2 * k - 1], ALU.mult)
                            dve.drain()
                            nc.vector.tensor_tensor(nxt[:, :, :, 0], now, nxt[:, :, :, 1], ALU.subtract)
                            now = both
                        nc.vector.tensor_tensor(place[:], in_tile[:, n, :, :],
                                                iota[:, None, 0:TILES].to_broadcast([P, NT, TILES]), ALU.mult)
                        dve.drain()
                        nc.vector.tensor_tensor(by_sub[:], sub, iota[:, None, 0:SUB].to_broadcast([P, NT, SUB]),
                                                ALU.mult)
                        nc.vector.tensor_reduce(spot[:, 0, :], place[:], AX_X, ALU.add)
                        dve.wait_ge(rank_full, n + 1)
                        nc.vector.tensor_scalar(some[:, 0, :], count_ps[:, n % 2, 0:TILES], 1.0 / P, None, ALU.mult)
                        dve.drain()
                        nc.vector.tensor_tensor(over[:], some[:, 0, :, None].to_broadcast([P, TILES, NT]),
                                                iota[:, None, 0:NT].to_broadcast([P, TILES, NT]), ALU.is_gt)
                        nc.vector.tensor_reduce(spot[:, 1, :], by_sub[:], AX_X, ALU.add)
                        dve.drain()
                        nc.vector.tensor_reduce(some[:, 1, :], over[:], AX_X, ALU.add)
                        nc.vector.tensor_scalar(spot[:, 0, :], spot[:, 0, :], float(SUB), float(n * NL),
                                                ALU.mult, ALU.add)
                        dve.drain()
                        nc.vector.tensor_tensor(leaf_of[:, n, :], spot[:, 0, :], spot[:, 1, :], ALU.add)
                        nc.vector.tensor_tensor_scan(some[:, 2, :], some[:, 3, :], some[:, 1, :], 0.0,
                                                     ALU.mult, ALU.add)
                        dve.drain()
                        nc.vector.tensor_tensor(some[:, 0, :], some[:, 2, :], some[:, 1, :], ALU.subtract)
                        nc.vector.tensor_tensor(table[:], some[0:1, 2:3, :].to_broadcast([1, BLOCKS, TILES]),
                                                iota[0:1, 0:BLOCKS, None].to_broadcast([1, BLOCKS, TILES]), ALU.is_le)
                        dve.drain()
                        nc.vector.tensor_scalar(some[:, 0, :], some[:, 0, :], float(P), float(n * BLOCKS * P),
                                                ALU.mult, ALU.add)
                        nc.vector.tensor_reduce(short[:], table[:], AX_X, ALU.add)
                        dve.drain()
                        nc.vector.tensor_tensor(place[:], rank_ps[:, n % 2, :].rearrange("p (t e) -> p t e", e=TILES),
                                                some[:, 0:1, :].to_broadcast([P, NT, TILES]), ALU.add)
                        nc.vector.tensor_scalar(short[:], short[:], TILES - 1.0, float(n * TILES), ALU.min, ALU.add)
                        dve.drain()
                        nc.vector.tensor_tensor(place[:], place[:], in_tile[:, n, :, :], ALU.mult)
                        nc.vector.tensor_copy(tile_of[:, n * BLOCKS:(n + 1) * BLOCKS], short[:])
                        dve.drain()
                        nc.vector.tensor_reduce(spot[:, 2, :], place[:], AX_X, ALU.add)
                        dve.drain()
                        nc.vector.tensor_copy(slot_of[:, n, :], spot[:, 2, :]).then_inc(routed, 1)

                @block.gpsimd
                def _(pool):
                    pool.wait_ge(rows_copied, T)
                    for n in range(T):
                        pool.wait_ge(routed, n + 1)
                        pool.wait_ge(cleared, 16 * 4 * T)
                        for t in range(NT):
                            nc.gpsimd.indirect_dma_start(slots,
                                                         bass.IndirectOffsetOnAxis(slot_of[:, n, t:t + 1], 0),
                                                         rows[:, n, t, :], None).then_inc(moved, 16)
                    pool.wait_ge(moved, 16 * NT * T)

        with Scope(nc, name + "l") as m:
            R, Q = 2, 4
            block_rows = m.sb("block_rows", [P, Q, 4, ROW])
            w12 = m.sb("w12", [P, Q, 4, 2 * P + 1])
            ident_bf = m.sb("ident_bf", [P, P], BF16)
            widen = m.sb("widen", [4 * SUB, 4, P], BF16)
            turned_rows = m.sb("turned_rows", [P, R, W])
            sub_ones = m.sb("sub_ones", [P, R, 4, SUB], BF16)
            sub_turned = m.sb("sub_turned", [4 * SUB, R, P], BF16)
            active = m.sb("active", [P, R, W])
            own = m.sb("own", [P, R, W])
            result = m.sb("result", [P, R, 4, D])
            y_ps = m.ps("y_ps", [P, W])
            s_ps = m.ps("s_ps", [4 * SUB, 2 * W], BF16)
            m_ps = m.ps("m_ps", [P, R, W])
            h_ps = m.ps("h_ps", [P, R, W])
            o_ps = m.ps("o_ps", [P, R, W])
            const_in = m.sem("const_in")
            rows_in = [m.sem(f"rows_in{q}") for q in range(Q)]
            weights_in = [m.sem(f"weights_in{q}") for q in range(Q)]
            sub_ready = m.sem("sub_ready")
            y_turned = m.sem("y_turned")
            y_copied = m.sem("y_copied")
            sub_out = m.sem("sub_out")
            sub_copied = m.sem("sub_copied")
            hidden_full = m.sem("hidden_full")
            mask_full = m.sem("mask_full")
            active_done = m.sem("active_done")
            own_done = m.sem("own_done")
            out_full = m.sem("out_full")
            out_copied = m.sem("out_copied")
            stored = [m.sem(f"stored{r}") for r in range(R)]
            gathered = [m.sem(f"gathered{n}") for n in range(T)]
            LOOPS = GROUPS // Q

            def load_weights(engine, k, q, which):
                for c in which:
                    tile = engine.value_load(tile_of[0:1, bass.ds(4 * k + c, 1)], min_val=0,
                                             max_val=T * TILES - 1)
                    engine.dma_start(w12[:, q, c, :], w["w12"][bass.ds(tile, 1), :, :].rearrange("a p n -> p (a n)")
                                     ).then_inc(weights_in[q], 16)

            with nc.Block() as block:
                @block.sync
                def _(sp):
                    def load(k, q):
                        sp.wait_ge(out_full, k + 1)
                        sp.dma_start(block_rows[:, q, :, :],
                                     slots[bass.ds(k * 4 * P, 4 * P), :].rearrange("(c p) n -> p c n", p=P)
                                     ).then_inc(rows_in[q], 16)
                        load_weights(sp, k, q, (0, 1))

                    def store(k, r):
                        sp.wait_ge(out_copied, k + 1 + R)
                        sp.dma_start(results[bass.ds(k * 4 * P, 4 * P), :].rearrange("(c p) n -> p c n", p=P),
                                     result[:, r, :, :]).then_inc(stored[r], 16)

                    sp.dma_start(ident_bf[:], consts["ident_bf"]).then_inc(const_in, 16)
                    sp.dma_start(widen[:], consts["widen"]).then_inc(const_in, 16)
                    for q in range(Q):
                        load(q, q)
                    with sp.Fori(1, LOOPS) as i:
                        for q in range(Q):
                            load(Q * i + q, q)
                            store(Q * i + q - Q, q % R)
                    for q in range(Q):
                        store(GROUPS - Q + q, q % R)

                @block.tensor
                def _(pe):
                    def turn(k, i, q):
                        pe.wait_ge(rows_in[q], 16 * (i + 1))
                        pe.wait_ge(y_copied, k + 1)
                        for c in range(4):
                            mm = nc.tensor.transpose(y_ps[:, c * P:(c + 1) * P], block_rows[:, q, c, 0:D],
                                                     consts["ident_sb"][:])
                        mm.then_inc(y_turned, 1)
                        pe.wait_ge(sub_ready, k + 1)
                        nc.tensor.transpose(s_ps[:, 0:P], sub_ones[:, q % R, :, :].rearrange("p c s -> p (c s)"),
                                            ident_bf[:]).then_inc(sub_out, 1)

                    def hidden(k, i, q):
                        r = q % R
                        pe.wait_ge(own_done, k + 1)
                        pe.wait_ge(y_copied, k + 2)
                        pe.wait_ge(weights_in[q], 64 * (i + 1))
                        for c in range(4):
                            mm = nc.tensor.matmul(h_ps[:, r, c * P:(c + 1) * P], w12[:, q, c, 0:P],
                                                  turned_rows[:, r, c * P:(c + 1) * P], start=True, stop=True)
                        mm.then_inc(hidden_full, 1)
                        pe.wait_ge(sub_copied, k + 1)
                        for c in range(4):
                            mm = nc.tensor.matmul(m_ps[:, r, c * P:(c + 1) * P], widen[:, c, :],
                                                  sub_turned[:, r, :], start=True, stop=True)
                        mm.then_inc(mask_full, 1)

                    def down(k, q):
                        r = q % R
                        pe.wait_ge(own_done, k + 1 + R)
                        pe.wait_ge(out_copied, k + 1)
                        for c in range(4):
                            mm = nc.tensor.matmul(o_ps[:, r, c * P:(c + 1) * P], own[:, r, c * P:(c + 1) * P],
                                                  w12[:, q, c, P:2 * P], start=True, stop=True)
                        mm.then_inc(out_full, 1)

                    def body(i, first):
                        for q in range(Q):
                            k = Q * i + q
                            turn(k, i, q)
                            if not (first and q == 0):
                                hidden(k - 1, i if q else i - 1, (q - 1) % Q)
                            if not (first and q < 2):
                                down(k - 2, (q - 2) % Q)

                    pe.wait_ge(const_in, 32)
                    body(0, True)
                    with pe.Fori(1, LOOPS) as i:
                        body(i, False)
                    hidden(GROUPS - 1, LOOPS - 1, Q - 1)
                    down(GROUPS - 2, Q - 2)
                    down(GROUPS - 1, Q - 1)

                @block.scalar
                def _(act):
                    def act_y(k, q):
                        act.wait_ge(y_turned, k + 1)
                        nc.scalar.copy(turned_rows[:, q % R, :], y_ps[:]).then_inc(y_copied, 1)

                    def act_hidden(k, q):
                        r = q % R
                        act.wait_ge(hidden_full, k + 1)
                        act.wait_ge(own_done, k + 1)
                        for c in range(4):
                            last = nc.scalar.activation(active[:, r, c * P:(c + 1) * P], h_ps[:, r, c * P:(c + 1) * P],
                                                        act_fn, bias=w12[:, q, c, 2 * P:2 * P + 1])
                        last.then_inc(active_done, 1)

                    def act_load(k, q):
                        act.wait_ge(out_full, k + 1)
                        load_weights(act, k, q, (2, 3))

                    def body(i, first, last=False):
                        for q in range(Q):
                            act_y(Q * i + q, q)
                            if not (last and q == Q - 1):
                                act_load(Q * i + q + 1, (q + 1) % Q)
                            if not (first and q == 0):
                                act_hidden(Q * i + q - 1, (q - 1) % Q)

                    act_load(0, 0)
                    body(0, True)
                    with act.Fori(1, LOOPS - 1) as i:
                        body(i, False)
                    body(LOOPS - 1, False, last=True)
                    act_hidden(GROUPS - 1, Q - 1)

                @block.vector
                def _(dve):
                    def dve_sub(k, i, q):
                        dve.wait_ge(rows_in[q], 16 * (i + 1))
                        nc.vector.tensor_copy(sub_ones[:, q % R, :, :],
                                              block_rows[:, q, :, D:ROW]).then_inc(sub_ready, 1)

                    def dve_turned(k, q):
                        dve.wait_ge(sub_out, k + 1)
                        nc.vector.tensor_copy(sub_turned[:, q % R, :], s_ps[:, 0:P]).then_inc(sub_copied, 1)

                    def dve_own(k, q):
                        r = q % R
                        dve.wait_ge(active_done, k + 1 + R)
                        dve.wait_ge(mask_full, k + 1)
                        dve.wait_ge(out_full, k + 1 + Q - R)
                        nc.vector.tensor_tensor(own[:, r, :], active[:, r, :], m_ps[:, r, :],
                                                ALU.mult).then_inc(own_done, 1)

                    def dve_out(k, times, q):
                        r = q % R
                        dve.wait_ge(out_full, k + 1 + Q)
                        if not (isinstance(times, int) and times == 0):
                            dve.wait_ge(stored[r], 16 * times)
                        nc.vector.tensor_copy(result[:, r, :, :].rearrange("p c n -> p (c n)"),
                                              o_ps[:, r, :]).then_inc(out_copied, 1)

                    def body(i, first):
                        for q in range(Q):
                            k = Q * i + q
                            dve_sub(k, i, q)
                            dve_turned(k, q)
                            if not (first and q == 0):
                                dve_own(k - 1, (q - 1) % Q)
                            if not (first and q < 2):
                                dve_out(k - 2, 2 * i + q // 2 - 1, (q - 2) % Q)

                    dve.sem_inc(active_done, R)
                    dve.sem_inc(own_done, R)
                    dve.sem_inc(out_full, Q)
                    dve.sem_inc(out_copied, R)
                    dve.sem_inc(y_copied, 1)
                    body(0, True)
                    with dve.Fori(1, LOOPS) as i:
                        body(i, False)
                    dve_own(GROUPS - 1, Q - 1)
                    dve_out(GROUPS - 2, GROUPS // 2 - 1, Q - 2)
                    dve_out(GROUPS - 1, GROUPS // 2 - 1, Q - 1)
                    for n in range(T):
                        dve.wait_ge(gathered[n], 32 * NT)
                        nc.vector.tensor_tensor(outs[n][:], outs[n][:], rows[:, n, :, 0:D], ALU.add)

                @block.gpsimd
                def _(pool):
                    for n in range(T):
                        for t in range(NT):
                            nc.gpsimd.indirect_dma_start(outs[n][:, t, :], None, w["b2"],
                                                         bass.IndirectOffsetOnAxis(leaf_of[:, n, t:t + 1], 0)
                                                         ).then_inc(gathered[n], 16)
                        for r in range(R):
                            pool.wait_ge(stored[r], 16 * (BLOCKS // 4 // R) * (n + 1))
                        for t in range(NT):
                            nc.gpsimd.indirect_dma_start(rows[:, n, t, 0:D], None, results[0:(n + 1) * BLOCKS * P, :],
                                                         bass.IndirectOffsetOnAxis(slot_of[:, n, t:t + 1], 0)
                                                         ).then_inc(gathered[n], 16)


def single_attention(nc, name, xn, yT, q_tok, k_tok, v_tok, consts):
    SCALE = D ** -0.5
    with Scope(nc, name) as m:
        qT = m.sb("qT", [P, B * S])
        kT = m.sb("kT", [P, B * S])
        q_now = m.sb("q_now", [P, B, P])
        probs = m.sb("probs", [P, B, S])
        probsT = m.sb("probsT", [P, B, TB, P])
        top = m.sb("top", [P, B, 4])
        s_ps = m.ps("s_ps", [P, B, S])
        t_ps = m.ps("t_ps", [P, 2, W])
        o_ps = m.ps("o_ps", [P, W])
        qk_turned = m.sem("qk_turned")
        qk_copied = m.sem("qk_copied")
        q_in = m.sem("q_in")
        scores_full = m.sem("scores_full")
        top_ready = m.sem("top_ready")
        probs_ready = m.sem("probs_ready")
        turned = m.sem("turned")
        copied = m.sem("copied")
        out_full = m.sem("out_full")
        out_free = m.sem("out_free")
        ident = consts["ident_sb"]

        def rounds(engine, step):
            for b in range(B):
                step(b, b, 0, b == 0, False)
            with engine.Fori(1, TB - 1) as t:
                for b in range(B):
                    step(2 * t + b, b, t, False, False)
            for b in range(B):
                step(2 * TB - 2 + b, b, TB - 1, False, b == 1)

        with nc.Block() as block:
            @block.gpsimd
            def _(pool):
                pool.wait_ge(qk_copied, B)
                with pool.Fori(0, TB) as t:
                    for b in range(B):
                        pool.wait_ge(probs_ready, 2 * t + 1 + b)
                        nc.gpsimd.tensor_copy(q_now[:, b, :], qT[:, bass.ds(b * S + t * P, P)])
                        pool.drain()
                        pool.sem_inc(q_in, 1)

            @block.tensor
            def _(pe):
                for n, tok in enumerate((q_tok, k_tok)):
                    for b in range(B):
                        if n:
                            pe.wait_ge(qk_copied, b + 1)
                        for t in range(TB):
                            mm = nc.tensor.transpose(s_ps[:, b, t * P:(t + 1) * P], tok[:, b * TB + t, :], ident[:])
                        mm.then_inc(qk_turned, 1)
                pe.wait_ge(qk_copied, 2 * B)

                def scores(n, b):
                    pe.wait_ge(q_in, n + 1)
                    pe.wait_ge(probs_ready, n + 1)
                    for c in range(2):
                        mm = nc.tensor.matmul(s_ps[:, b, c * W:(c + 1) * W], q_now[:, b, :],
                                              kT[:, b * S + c * W:b * S + (c + 1) * W], start=True, stop=True)
                    mm.then_inc(scores_full, 1)

                def sums(n, b):
                    pe.wait_ge(copied, 2 * n + 4)
                    pe.wait_ge(out_free, n + 1)
                    for c in range(TB):
                        mm = nc.tensor.matmul(o_ps[:, 0:D], probsT[:, b, c, :], v_tok[:, b * TB + c, :],
                                              start=(c == 0), stop=(c == TB - 1))
                    mm.then_inc(out_full, 1)

                def step(n, b, t, first, last):
                    if not last:
                        scores(n + 1, 1 - b)
                    pe.wait_ge(probs_ready, n + 3)
                    for h in range(2):
                        pe.wait_ge(copied, 2 * n + h + 1)
                        for c in range(4):
                            at = 4 * h + c
                            mm = nc.tensor.transpose(t_ps[:, h, c * P:(c + 1) * P],
                                                     probs[:, b, at * P:(at + 1) * P], ident[:])
                        mm.then_inc(turned, 1)
                    if not first:
                        sums(n - 1, 1 - b)

                scores(0, 0)
                rounds(pe, step)
                sums(2 * TB - 1, 1)
                pe.wait_ge(out_free, 2 * TB + 1)
                for g in range(NG):
                    for c in range(4):
                        t = 4 * g + c
                        mm = nc.tensor.transpose(s_ps[:, g // 2, g % 2 * W + c * P:g % 2 * W + (c + 1) * P],
                                                 xn[:, t, :], ident[:])
                    mm.then_inc(qk_turned, 1)

            @block.scalar
            def _(act):
                for n, turned_to in enumerate((qT, kT)):
                    for b in range(B):
                        act.wait_ge(qk_turned, B * n + b + 1)
                        nc.scalar.copy(turned_to[:, b * S:(b + 1) * S], s_ps[:, b, :]).then_inc(qk_copied, 1)

                def exp(n, b):
                    act.wait_ge(top_ready, n + 1)
                    nc.scalar.activation(probs[:, b, :], s_ps[:, b, :], ACT.Exp, bias=top[:, b, 1:2],
                                         scale=SCALE, accum_out=top[:, b, 2:3]).then_inc(probs_ready, 1)

                def step(n, b, t, first, last):
                    if not last:
                        exp(n + 1, 1 - b)
                    for h in range(2):
                        act.wait_ge(turned, 2 * n + h + 1)
                        act.wait_ge(out_full, n + 1)
                        nc.scalar.copy(probsT[:, b, 4 * h:4 * h + 4, :].rearrange("p c n -> p (c n)"),
                                       t_ps[:, h, :]).then_inc(copied, 1)

                exp(0, 0)
                rounds(act, step)
                for g in range(NG):
                    act.wait_ge(qk_turned, 2 * B + g + 1)
                    nc.scalar.copy(yT[:, g * W:(g + 1) * W], s_ps[:, g // 2, g % 2 * W:(g % 2 + 1) * W])

            @block.vector
            def _(dve):
                dve.sem_inc(probs_ready, 2)
                dve.sem_inc(copied, 2)
                dve.sem_inc(out_full, 2)
                dve.sem_inc(out_free, 1)

                def maximum(n, b):
                    dve.wait_ge(scores_full, n + 1)
                    nc.vector.tensor_reduce(top[:, b, 0:1], s_ps[:, b, :], AX_X, ALU.max)
                    dve.drain()
                    nc.vector.tensor_scalar(top[:, b, 1:2], top[:, b, 0:1], -SCALE, None,
                                            ALU.mult).then_inc(top_ready, 1)

                def add(n, b, t):
                    dve.wait_ge(out_full, n + 3)
                    tile = xn[:, b * TB + t, :] if isinstance(t, int) else \
                        xn[:, bass.ds(b * TB + t, 1), :].rearrange("p a n -> p (a n)")
                    nc.vector.scalar_tensor_tensor(tile, o_ps[:, 0:D], top[:, b, 3:4], tile,
                                                   ALU.mult, ALU.add).then_inc(out_free, 1)
                    dve.drain()

                def step(n, b, t, first, last):
                    if not last:
                        maximum(n + 1, 1 - b)
                    dve.wait_ge(probs_ready, n + 3)
                    nc.vector.reciprocal(top[:, b, 3:4], top[:, b, 2:3])
                    dve.drain()
                    if not first:
                        add(n - 1, 1 - b, t if b else t - 1)

                maximum(0, 0)
                rounds(dve, step)
                add(2 * TB - 1, 1, TB - 1)


def constants():
    bf = mybir.dt.np(BF16)
    ident = np.eye(P, dtype=np.float32)
    k, q = np.indices((P, P))
    spread_expert = np.zeros((64, 16, P), np.float32)
    for e in range(64):
        spread_expert[e, e // 4, 32 * (e % 4):32 * (e % 4) + 32] = 1.0
    widen = np.zeros((32, 4, P), np.float32)
    for leaf in range(32):
        widen[leaf, leaf // 8, 16 * (leaf % 8):16 * (leaf % 8) + 16] = 1.0
    ranks = np.arange(B * S // 2, dtype=np.float32)
    return {
        "ident": ident,
        "ident_bf": ident.astype(bf),
        "mask_q": np.where(q > k, NEG, 0.0).astype(bf),
        "mask_k": np.where(k > q, NEG, 0.0).astype(bf),
        "widen": widen.astype(bf),
        "iota": np.arange(48, dtype=np.float32),
        "before": np.stack([k < q, k < P], axis=1).astype(bf),
        "spread_expert": spread_expert,
        "rank_row": np.concatenate([np.tile(ranks, (64, 1)), np.tile(ranks + B * S // 2, (64, 1))]),
        "lower": np.tril(np.ones((8, 8), np.float32), -1),
    }


def twice(w):
    return np.ascontiguousarray(np.concatenate([w, w], axis=2))


def stacked(wo):
    return np.ascontiguousarray(np.concatenate([wo, wo], axis=1).transpose(1, 0, 2))


def hidden_tiles(w):
    return np.ascontiguousarray(np.pad(w, ((0, 0), (0, 0), (0, 1))))


def program(nc, a, out, stages=range(8)):
    Scope.SPENT = []
    with Scope(nc, "all") as m:
        x = m.sb("x", [P, NT, D])
        ident = m.sb("ident", [P, P])
        x_in = m.sem("x_in")
        x_out = m.sem("x_out")
        consts = dict(a, ident_sb=ident)
        with nc.Block() as block:
            @block.sync
            def _(sp):
                sp.dma_start(x[:], a["x"].rearrange("b (t p) d -> p (b t) d", p=P)).then_inc(x_in, 16)
                sp.dma_start(ident[:], a["ident"]).then_inc(x_in, 16)
                sp.wait_ge(x_in, 32)
        xT_h = m.sb("xT", [P, B * S])
        xn = m.sb("xn", [P, NT, D])

        def normed(name):
            return lambda loads: layer_norm(nc, name, x, xn, ident, xT_h, loads=loads)

        if 0 in stages:
            narrow_attention(nc, "a0", x, xT_h, None,
                             [a[k] for k in ("a0_wq", "a0_wk", "a0_wv", "a0_bq", "a0_bk", "a0_bv", "a0_wo", "a0_bo")],
                             consts, causal=True, norm=normed("n0"))
        if 1 in stages:
            recycle(nc)
            routed_experts(nc, "f1", x, xT_h, {k: a["f1_" + k] for k in
                           ("wr", "br", "wup", "wgate", "wdown", "bdown", "bias")}, consts, normed("n1"), xn)
        if 2 in stages:
            recycle(nc)
            with Scope(nc, "s2") as t:
                ln = t.sb("ln", [P, 2])
                zz = t.sb("zz", [P, NT, D])
                layer_norm(nc, "n2", x, xn, ident, loads=[(ln[:, n:n + 1], a[k].rearrange("(p a) -> p a", a=1))
                                                          for n, k in enumerate(("a2_ln_w", "a2_ln_b"))])
                narrow_attention(nc, "a2", x, xT_h, xn,
                                 [a[k] for k in ("a2_wq", "a2_wk", "a2_wv", "a2_bq", "a2_bk", "a2_bv", "a2_wo", "a2_bo")],
                                 consts, causal=False,
                                 norm=lambda loads: layer_norm(nc, "n2b", xn, zz, ident, xT_h, affine=ln, loads=loads))
        if 3 in stages:
            recycle(nc)
            layer_norm(nc, "n3", x, xn, ident)
            layer_norm(nc, "n3b", xn, xn, ident, xT_h, root_of_deviation=True)
            with Scope(nc, "s3") as t:
                q, k, v = (t.sb(f"{k}_tok", [P, NT, D]) for k in "qkv")
                trees = [{n: a[f"f3_{k}_{n}"] for n in ("nw", "nb", "w12", "b2")} for k in ("qkv", "f")]
                leaf_layers(nc, "f3q", xn, xT_h, (q, k, v), trees[0], ACT.Relu, consts)
                single_attention(nc, "a3", xn, xT_h, q, k, v, consts)
                leaf_layers(nc, "f3f", xn, xT_h, (q,), trees[1], ACT.Gelu, consts)
                with nc.Block() as block:
                    @block.vector
                    def _(dve):
                        nc.vector.tensor_tensor(x[:], x[:], xn[:], ALU.add)
                        dve.drain()
                        nc.vector.tensor_tensor(x[:], x[:], q[:], ALU.add)
        if 4 in stages:
            recycle(nc)
            wide_attention(nc, "a4", x, xT_h, [a[k] for k in ("a4_wq", "a4_wk", "a4_wv", "a4_wo", "a4_bo")],
                           consts, shared_keys=False, norm=normed("n4"))
        if 5 in stages:
            recycle(nc)
            top2_experts(nc, "f5", x, xT_h, a["f5_wg"], a["f5_w1"], a["f5_w2"], a["f5_w3"], a["lower"],
                         normed("n5"))
        if 6 in stages:
            recycle(nc)
            wide_attention(nc, "a6", x, xT_h, [a[k] for k in ("a6_wq", "a6_wk", "a6_wv", "a6_wo", "a6_bo")],
                           consts, shared_keys=True, norm=normed("n6"))
        if 7 in stages:
            recycle(nc)
            binary_linear(nc, "f7", x, xT_h, a["f7_w"], a["f7_scale"], a["f7_bias"], normed("n7"))
        with nc.Block() as block:
            @block.sync
            def _(sp):
                sp.dma_start(out.rearrange("b (t p) d -> p (b t) d", p=P), x[:]).then_inc(x_out, 16)
                sp.wait_ge(x_out, 16)


def layout(i):
    c = np.ascontiguousarray
    i = {k: np.asarray(v) for k, v in i.items()}
    a = {"x": i["L0_attn_x"]}
    kv = i["L0_attn_Wkv"]
    a.update(a0_wq=i["L0_attn_Wq"], a0_wk=c(kv[:, :D]), a0_wv=c(kv[:, D:]), a0_bq=i["L0_attn_bq"],
             a0_bk=c(i["L0_attn_bkv"][:D]), a0_bv=c(i["L0_attn_bkv"][D:]), a0_wo=i["L0_attn_Wo"],
             a0_bo=i["L0_attn_bo"])
    w, wb = i["L1_attn_W_qkv"], i["L1_attn_b_qkv"]
    a.update(a2_ln_w=i["L1_attn_ln_w"], a2_ln_b=i["L1_attn_ln_b"],
             a2_wq=c(w[:, :D]), a2_wk=c(w[:, D:2 * D]), a2_wv=c(w[:, 2 * D:]),
             a2_bq=c(wb[:D]), a2_bk=c(wb[D:2 * D]), a2_bv=c(wb[2 * D:]),
             a2_wo=i["L1_attn_W_proj"], a2_bo=i["L1_attn_b_proj"])
    wkv = i["L2_attn_Wkv"]
    a.update(a4_wq=i["L2_attn_Wq"].reshape(D, HEADS, 64), a4_wk=c(wkv[:, :1024]).reshape(D, HEADS, 64),
             a4_wv=c(wkv[:, 1024:].reshape(D, HEADS // 2, P)),
             a4_wo=stacked(i["L2_attn_Wo"].reshape(HEADS, 64, D)), a4_bo=i["L2_attn_bo"])
    a.update(a6_wq=c(i["L3_attn_query_proj"].transpose(2, 0, 1)),
             a6_wk=i["L3_attn_key_proj"].reshape(D, 1, 64), a6_wv=twice(i["L3_attn_value_proj"].reshape(D, 1, 64)),
             a6_wo=stacked(i["L3_attn_output_proj"].transpose(1, 2, 0)), a6_bo=np.zeros(D, np.float32))
    up, gate = i["L0_ffn_Wup"], i["L0_ffn_Wgate"]
    a.update(f1_wr=i["L0_ffn_Wr"], f1_br=i["L0_ffn_br"], f1_wup=c(up.transpose(1, 0, 2).reshape(D, 2048)),
             f1_wgate=c(gate.transpose(1, 0, 2).reshape(D, 2048)),
             f1_wdown=c(i["L0_ffn_Wdown"].reshape(16, P, D).transpose(1, 0, 2)), f1_bdown=i["L0_ffn_bdown"],
             f1_bias=c(np.stack([i["L0_ffn_bup"].reshape(16, P).T, i["L0_ffn_bgate"].reshape(16, P).T], axis=1)))
    a.update(f5_wg=c(i["L2_ffn_Wg"].T), f5_w1=hidden_tiles(i["L2_ffn_W1"].transpose(0, 2, 1)),
             f5_w2=hidden_tiles(i["L2_ffn_W2"].transpose(0, 2, 1)),
             f5_w3=c(hidden_tiles(i["L2_ffn_W3"]).transpose(0, 2, 1).reshape(8, 3, 114, D).transpose(0, 2, 1, 3)))
    a.update(f7_w=c(i["L3_ffn_weights"].T), f7_scale=i["L3_ffn_scale"], f7_bias=i["L3_ffn_bias"])
    for trees in ("qkv", "f"):
        def stack(part):
            return np.stack([i[f"L1_ffn_{k}_{part}"] for k in trees])
        n = len(trees)
        w1 = stack("w1").reshape(n * 32, 8, D, 16).transpose(0, 2, 1, 3).reshape(n * 32, D, P)
        a.update({
            f"f3_{trees}_nw": c(np.pad(stack("nw").transpose(0, 2, 1), ((0, 0), (0, 0), (0, 1)))),
            f"f3_{trees}_nb": c(np.pad(stack("nb"), ((0, 0), (0, 1)))),
            f"f3_{trees}_w12": np.concatenate([w1, stack("w2").reshape(n * 32, P, D),
                                               stack("b1").reshape(n * 32, P, 1)], axis=2),
            f"f3_{trees}_b2": c(stack("b2").reshape(n * 256, D)),
        })
    a.update(constants())
    return a


def kernel(**inputs):
    import concourse.bacc as bacc
    from concourse.bass_utils import run_bass_kernel_spmd

    nc = bacc.Bacc("TRN2", target_bir_lowering=False, num_devices=1)
    arrays = {f"in_{k}": np.ascontiguousarray(v) for k, v in layout(inputs).items()}
    args = {k[3:]: nc.dram_tensor(k, v.shape, mybir.dt.from_np(v.dtype), kind="ExternalInput").ap()
            for k, v in arrays.items()}
    out = nc.dram_tensor("out_x", (B, S, D), F32, kind="ExternalOutput").ap()
    program(nc, args, out)
    r = run_bass_kernel_spmd(nc, [arrays], core_ids=[0])
    return r.results[0]["out_x"]
```
